# Optimizing a Trainium2 kernel written in Bass

```python
import numpy as np
import jax
import jax.numpy as jnp

def _softmax(x, axis=-1):
    return jax.nn.softmax(x, axis=axis)

def _gelu(x):
    return jax.nn.gelu(x, approximate=True)

def _silu(x):
    return jax.nn.silu(x)

def _sigmoid(x):
    return jax.nn.sigmoid(x)

def _layernorm(x, axis=-1, eps=1e-05):
    m = jnp.mean(x, axis=axis, keepdims=True)
    v = jnp.var(x, axis=axis, keepdims=True)
    return (x - m) / jnp.sqrt(v + eps)

def _scatter_add(tgt, idx, src, axis=0):
    return tgt.at[idx].add(src)

def _segment_sum(src, seg, n):
    return jax.ops.segment_sum(src, seg, n)
kernel_name = 'mk_pixart_seq_d2_seqx_r4_0e4c78'

def setup_inputs(seed: int=0):
    np.random.seed(seed)
    _w = jnp.asarray

    def _rec_inputs():
        import jax
        import jax.numpy as jnp
        _rk = jax.random.key(seed)
        x = -0.0002928 + 1 * jax.random.normal(jax.random.fold_in(_rk, 1), (4, 512, 256), jnp.float32)
        _lenS = 512 - jax.random.randint(jax.random.fold_in(_rk, 7), (4,), 0, max(1, 512 // 4) + 1, jnp.int32)
        _lenS2 = 64 - jax.random.randint(jax.random.fold_in(_rk, 8), (4,), 0, max(1, 64 // 4) + 1, jnp.int32)
        cond_1024 = 0.0061147 + 1.02565 * jax.random.normal(jax.random.fold_in(_rk, 11), (4, 256), jnp.float32)
        _ctx_1024P = jax.random.normal(jax.random.fold_in(_rk, 12), (4, 16, 256), jnp.float32)
        _ctx_1024c = jax.random.dirichlet(jax.random.fold_in(_rk, 512), 0.3 * jnp.ones((16,), jnp.float32), (4, 64))
        _ctx_1024t = jnp.einsum('bsk,bkd->bsd', _ctx_1024c, _ctx_1024P)
        _ctx_1024t = _ctx_1024t * jax.lax.rsqrt(jnp.mean(jnp.square(_ctx_1024t)) + 1e-12) * 0.953939
        ctx_1024 = -0.00265004 + 0.998804 * (_ctx_1024t + 0.3 * jax.random.normal(jax.random.fold_in(_rk, 612), (4, 64, 256), jnp.float32))
        _validS = jnp.arange(512)[None, :] < _lenS[:, None]
        _validS2 = jnp.arange(64)[None, :] < _lenS2[:, None]
        _causal = jnp.tril(jnp.ones((512, 512), dtype=bool))
        mask_BxS2_bf0 = jnp.logical_not(jnp.ones((4, 64), dtype=bool))
        return (x, cond_1024, ctx_1024, mask_BxS2_bf0)
    x, cond_1024, ctx_1024, mask_BxS2_bf0 = _rec_inputs()

    def _L0_xcond_setup():
        import jax, jax.numpy as jnp
        import numpy as np
        D, H, B, N, S = (256, 16, 4, 256, 77)
        HD = D // H
        DF = 4 * D
        EPS = 1e-06
        SCALE = HD ** (-0.5)

        def _ln(x):
            m = jnp.mean(x, axis=-1, keepdims=True)
            v = jnp.mean((x - m) ** 2, axis=-1, keepdims=True)
            return (x - m) / jnp.sqrt(v + EPS)
        key = jax.random.key(seed)
        ks = jax.random.split(key, 24)
        s = 0.02
        inp = {'x': jax.random.normal(ks[0], (B, N, D), jnp.float32), 't_emb': jax.random.normal(ks[1], (B, D), jnp.float32), 'context': jax.random.normal(ks[2], (B, S, D), jnp.float32), 'context_mask': jnp.zeros((B, S), jnp.bool_), 'ada_w': jax.random.normal(ks[3], (D, 6 * D), jnp.float32) * s, 'ada_b': jnp.zeros((6 * D,), jnp.float32), 'qkv_w': jax.random.normal(ks[4], (D, 3 * D), jnp.float32) * s, 'qkv_b': jnp.zeros((3 * D,), jnp.float32), 'sa_proj_w': jax.random.normal(ks[5], (D, D), jnp.float32) * s, 'sa_proj_b': jnp.zeros((D,), jnp.float32), 'q_w': jax.random.normal(ks[6], (D, D), jnp.float32) * s, 'q_b': jnp.zeros((D,), jnp.float32), 'kv_w': jax.random.normal(ks[7], (D, 2 * D), jnp.float32) * s, 'kv_b': jnp.zeros((2 * D,), jnp.float32), 'ca_proj_w': jax.random.normal(ks[8], (D, D), jnp.float32) * s, 'ca_proj_b': jnp.zeros((D,), jnp.float32), 'fc1_w': jax.random.normal(ks[9], (D, DF), jnp.float32) * s, 'fc1_b': jnp.zeros((DF,), jnp.float32), 'fc2_w': jax.random.normal(ks[10], (DF, D), jnp.float32) * s, 'fc2_b': jnp.zeros((D,), jnp.float32)}
        return inp
    _L0_xcond_all = _L0_xcond_setup()
    _L0_xcond_in = {k: v for k, v in _L0_xcond_all.items() if k in ('ada_w', 'ada_b', 'qkv_w', 'qkv_b', 'sa_proj_w', 'sa_proj_b', 'q_w', 'q_b', 'kv_w', 'kv_b', 'ca_proj_w', 'ca_proj_b', 'fc1_w', 'fc1_b', 'fc2_w', 'fc2_b')}
    del _L0_xcond_all

    def _L1_xcond_setup():
        import jax, jax.numpy as jnp
        import numpy as np
        LN_EPS = 1e-06

        def _ln(x):
            mu = jnp.mean(x, axis=-1, keepdims=True)
            var = jnp.var(x, axis=-1, keepdims=True)
            return (x - mu) * jax.lax.rsqrt(var + LN_EPS)
        key = jax.random.key(seed)
        H, NH = (256, 16)
        B, N, S = (4, 256, 77)
        MLP = int(H * 4.0)
        ks = jax.random.split(key, 20)
        s = 1.0 / np.sqrt(H)
        return {'x': jax.random.normal(ks[0], (B, N, H), jnp.float32), 'c': jax.random.normal(ks[1], (B, H), jnp.float32), 'context': jax.random.normal(ks[2], (B, S, H), jnp.float32), 'W_mod': jax.random.normal(ks[3], (H, 6 * H), jnp.float32) * s, 'b_mod': jnp.zeros((6 * H,), jnp.float32), 'W_qkv': jax.random.normal(ks[4], (H, 3 * H), jnp.float32) * s, 'b_qkv': jnp.zeros((3 * H,), jnp.float32), 'W_proj': jax.random.normal(ks[5], (H, H), jnp.float32) * s, 'b_proj': jnp.zeros((H,), jnp.float32), 'W_qc': jax.random.normal(ks[6], (H, H), jnp.float32) * s, 'b_qc': jnp.zeros((H,), jnp.float32), 'W_kvc': jax.random.normal(ks[7], (H, 2 * H), jnp.float32) * s, 'b_kvc': jnp.zeros((2 * H,), jnp.float32), 'W_cproj': jax.random.normal(ks[8], (H, H), jnp.float32) * s, 'b_cproj': jnp.zeros((H,), jnp.float32), 'W_mlp1': jax.random.normal(ks[9], (H, MLP), jnp.float32) * s, 'b_mlp1': jnp.zeros((MLP,), jnp.float32), 'W_mlp2': jax.random.normal(ks[10], (MLP, H), jnp.float32) * (1.0 / np.sqrt(MLP)), 'b_mlp2': jnp.zeros((H,), jnp.float32)}
    _L1_xcond_all = _L1_xcond_setup()
    _L1_xcond_in = {k: v for k, v in _L1_xcond_all.items() if k in ('W_mod', 'b_mod', 'W_qkv', 'b_qkv', 'W_proj', 'b_proj', 'W_qc', 'b_qc', 'W_kvc', 'b_kvc', 'W_cproj', 'b_cproj', 'W_mlp1', 'b_mlp1', 'W_mlp2', 'b_mlp2')}
    del _L1_xcond_all
    return {'x': x, 'cond_1024': cond_1024, 'ctx_1024': ctx_1024, 'mask_BxS2_bf0': mask_BxS2_bf0, 'L0_xcond_ada_w': _L0_xcond_in['ada_w'], 'L0_xcond_ada_b': _L0_xcond_in['ada_b'], 'L0_xcond_qkv_w': _L0_xcond_in['qkv_w'], 'L0_xcond_qkv_b': _L0_xcond_in['qkv_b'], 'L0_xcond_sa_proj_w': _L0_xcond_in['sa_proj_w'], 'L0_xcond_sa_proj_b': _L0_xcond_in['sa_proj_b'], 'L0_xcond_q_w': _L0_xcond_in['q_w'], 'L0_xcond_q_b': _L0_xcond_in['q_b'], 'L0_xcond_kv_w': _L0_xcond_in['kv_w'], 'L0_xcond_kv_b': _L0_xcond_in['kv_b'], 'L0_xcond_ca_proj_w': _L0_xcond_in['ca_proj_w'], 'L0_xcond_ca_proj_b': _L0_xcond_in['ca_proj_b'], 'L0_xcond_fc1_w': _L0_xcond_in['fc1_w'], 'L0_xcond_fc1_b': _L0_xcond_in['fc1_b'], 'L0_xcond_fc2_w': _L0_xcond_in['fc2_w'], 'L0_xcond_fc2_b': _L0_xcond_in['fc2_b'], 'L1_xcond_W_mod': _L1_xcond_in['W_mod'], 'L1_xcond_b_mod': _L1_xcond_in['b_mod'], 'L1_xcond_W_qkv': _L1_xcond_in['W_qkv'], 'L1_xcond_b_qkv': _L1_xcond_in['b_qkv'], 'L1_xcond_W_proj': _L1_xcond_in['W_proj'], 'L1_xcond_b_proj': _L1_xcond_in['b_proj'], 'L1_xcond_W_qc': _L1_xcond_in['W_qc'], 'L1_xcond_b_qc': _L1_xcond_in['b_qc'], 'L1_xcond_W_kvc': _L1_xcond_in['W_kvc'], 'L1_xcond_b_kvc': _L1_xcond_in['b_kvc'], 'L1_xcond_W_cproj': _L1_xcond_in['W_cproj'], 'L1_xcond_b_cproj': _L1_xcond_in['b_cproj'], 'L1_xcond_W_mlp1': _L1_xcond_in['W_mlp1'], 'L1_xcond_b_mlp1': _L1_xcond_in['b_mlp1'], 'L1_xcond_W_mlp2': _L1_xcond_in['W_mlp2'], 'L1_xcond_b_mlp2': _L1_xcond_in['b_mlp2']}

def reference(x, cond_1024, ctx_1024, mask_BxS2_bf0, L0_xcond_ada_w, L0_xcond_ada_b, L0_xcond_qkv_w, L0_xcond_qkv_b, L0_xcond_sa_proj_w, L0_xcond_sa_proj_b, L0_xcond_q_w, L0_xcond_q_b, L0_xcond_kv_w, L0_xcond_kv_b, L0_xcond_ca_proj_w, L0_xcond_ca_proj_b, L0_xcond_fc1_w, L0_xcond_fc1_b, L0_xcond_fc2_w, L0_xcond_fc2_b, L1_xcond_W_mod, L1_xcond_b_mod, L1_xcond_W_qkv, L1_xcond_b_qkv, L1_xcond_W_proj, L1_xcond_b_proj, L1_xcond_W_qc, L1_xcond_b_qc, L1_xcond_W_kvc, L1_xcond_b_kvc, L1_xcond_W_cproj, L1_xcond_b_cproj, L1_xcond_W_mlp1, L1_xcond_b_mlp1, L1_xcond_W_mlp2, L1_xcond_b_mlp2):
    import jax
    import jax.numpy as jnp

    def _L0_xcond_ref(x, t_emb, context, context_mask, ada_w, ada_b, qkv_w, qkv_b, sa_proj_w, sa_proj_b, q_w, q_b, kv_w, kv_b, ca_proj_w, ca_proj_b, fc1_w, fc1_b, fc2_w, fc2_b):
        import jax, jax.numpy as jnp
        import numpy as np
        D, H, B, N, S = (256, 16, 4, 256, 77)
        HD = D // H
        DF = 4 * D
        EPS = 1e-06
        SCALE = HD ** (-0.5)

        def _ln(x):
            m = jnp.mean(x, axis=-1, keepdims=True)
            v = jnp.mean((x - m) ** 2, axis=-1, keepdims=True)
            return (x - m) / jnp.sqrt(v + EPS)
        Bx, Nx, C = x.shape
        Sx = context.shape[1]
        mod = jax.nn.silu(t_emb) @ ada_w + ada_b
        shift_sa, scale_sa, gate_sa, shift_ff, scale_ff, gate_ff = [m[:, None, :] for m in jnp.split(mod, 6, axis=-1)]
        xm1 = _ln(x) * (1 + scale_sa) + shift_sa
        qkv = (xm1 @ qkv_w + qkv_b).reshape(Bx, Nx, 3, H, HD)
        q, k, v = (qkv[:, :, 0], qkv[:, :, 1], qkv[:, :, 2])
        attn = jnp.einsum('bnhd,bmhd->bhnm', q, k) * SCALE
        attn = jax.nn.softmax(attn, axis=-1)
        sa = jnp.einsum('bhnm,bmhd->bnhd', attn, v).reshape(Bx, Nx, C)
        sa = sa @ sa_proj_w + sa_proj_b
        x = x + gate_sa * sa
        xn2 = _ln(x)
        qc = (xn2 @ q_w + q_b).reshape(Bx, Nx, H, HD)
        kvc = (context @ kv_w + kv_b).reshape(Bx, Sx, 2, H, HD)
        kc, vc = (kvc[:, :, 0], kvc[:, :, 1])
        attn_c = jnp.einsum('bnhd,bshd->bhns', qc, kc) * SCALE
        attn_c = jnp.where(context_mask[:, None, None, :], -jnp.inf, attn_c)
        attn_c = jax.nn.softmax(attn_c, axis=-1)
        ca = jnp.einsum('bhns,bshd->bnhd', attn_c, vc).reshape(Bx, Nx, C)
        ca = ca @ ca_proj_w + ca_proj_b
        x = x + ca
        xm3 = _ln(x) * (1 + scale_ff) + shift_ff
        h = jax.nn.gelu(xm3 @ fc1_w + fc1_b, approximate=False)
        ff = h @ fc2_w + fc2_b
        x = x + gate_ff * ff
        return x

    def _L1_xcond_ref(x, c, context, W_mod, b_mod, W_qkv, b_qkv, W_proj, b_proj, W_qc, b_qc, W_kvc, b_kvc, W_cproj, b_cproj, W_mlp1, b_mlp1, W_mlp2, b_mlp2):
        import jax, jax.numpy as jnp
        import numpy as np
        LN_EPS = 1e-06

        def _ln(x):
            mu = jnp.mean(x, axis=-1, keepdims=True)
            var = jnp.var(x, axis=-1, keepdims=True)
            return (x - mu) * jax.lax.rsqrt(var + LN_EPS)
        B, N, H = x.shape
        NH = 16
        hd = H // NH
        scale = hd ** (-0.5)
        c_proj = jax.nn.silu(c) @ W_mod + b_mod
        shift_a, scale_a, gate_a, shift_m, scale_m, gate_m = jnp.split(c_proj, 6, axis=-1)

        def modulate(t, shift, sc):
            return t * (1 + sc[:, None]) + shift[:, None]
        x_norm = modulate(_ln(x), shift_a, scale_a)
        qkv = x_norm @ W_qkv + b_qkv
        q, k, v = jnp.split(qkv, 3, axis=-1)
        q = q.reshape(B, N, NH, hd).transpose(0, 2, 1, 3)
        k = k.reshape(B, N, NH, hd).transpose(0, 2, 1, 3)
        v = v.reshape(B, N, NH, hd).transpose(0, 2, 1, 3)
        attn_w = jax.nn.softmax(jnp.einsum('bhqd,bhkd->bhqk', q, k) * scale, axis=-1)
        attn_out = jnp.einsum('bhqk,bhkd->bhqd', attn_w, v)
        attn_out = attn_out.transpose(0, 2, 1, 3).reshape(B, N, H)
        attn_out = attn_out @ W_proj + b_proj
        x = x + gate_a[:, None] * attn_out
        S = context.shape[1]
        q_c = _ln(x) @ W_qc + b_qc
        kv_c = _ln(context) @ W_kvc + b_kvc
        k_c, v_c = jnp.split(kv_c, 2, axis=-1)
        q_c = q_c.reshape(B, N, NH, hd).transpose(0, 2, 1, 3)
        k_c = k_c.reshape(B, S, NH, hd).transpose(0, 2, 1, 3)
        v_c = v_c.reshape(B, S, NH, hd).transpose(0, 2, 1, 3)
        c_attn_w = jax.nn.softmax(jnp.einsum('bhqd,bhsd->bhqs', q_c, k_c) * scale, axis=-1)
        c_attn_out = jnp.einsum('bhqs,bhsd->bhqd', c_attn_w, v_c)
        c_attn_out = c_attn_out.transpose(0, 2, 1, 3).reshape(B, N, H)
        c_attn_out = c_attn_out @ W_cproj + b_cproj
        x = x + c_attn_out
        x_norm2 = modulate(_ln(x), shift_m, scale_m)
        h = jax.nn.gelu(x_norm2 @ W_mlp1 + b_mlp1)
        h = h @ W_mlp2 + b_mlp2
        x = x + gate_m[:, None] * h
        return x
    x = _L0_xcond_ref(x, cond_1024, ctx_1024, mask_BxS2_bf0, L0_xcond_ada_w, L0_xcond_ada_b, L0_xcond_qkv_w, L0_xcond_qkv_b, L0_xcond_sa_proj_w, L0_xcond_sa_proj_b, L0_xcond_q_w, L0_xcond_q_b, L0_xcond_kv_w, L0_xcond_kv_b, L0_xcond_ca_proj_w, L0_xcond_ca_proj_b, L0_xcond_fc1_w, L0_xcond_fc1_b, L0_xcond_fc2_w, L0_xcond_fc2_b)
    x = _L1_xcond_ref(x, cond_1024, ctx_1024, L1_xcond_W_mod, L1_xcond_b_mod, L1_xcond_W_qkv, L1_xcond_b_qkv, L1_xcond_W_proj, L1_xcond_b_proj, L1_xcond_W_qc, L1_xcond_b_qc, L1_xcond_W_kvc, L1_xcond_b_kvc, L1_xcond_W_cproj, L1_xcond_b_cproj, L1_xcond_W_mlp1, L1_xcond_b_mlp1, L1_xcond_W_mlp2, L1_xcond_b_mlp2)
    return x

_drawn_inputs = setup_inputs


def setup_inputs(seed=0):
    import zlib

    import numpy as np

    out = dict(_drawn_inputs(seed))
    spreads = {'L0_xcond_ada_b': (0.0, 0.399),
     'L0_xcond_qkv_b': (0.0, 0.8),
     'L0_xcond_sa_proj_b': (0.0, 0.32),
     'L0_xcond_q_b': (0.0, 2.0),
     'L0_xcond_kv_b': (0.0, 0.678),
     'L0_xcond_ca_proj_b': (0.0, 0.1),
     'L0_xcond_fc1_b': (0.0, 0.8),
     'L0_xcond_fc2_b': (0.0, 0.375),
     'L1_xcond_b_mod': (0.0, 0.1),
     'L1_xcond_b_qkv': (0.0, 0.399),
     'L1_xcond_b_proj': (0.0, 0.358),
     'L1_xcond_b_qc': (0.0, 0.444),
     'L1_xcond_b_kvc': (0.0, 0.1),
     'L1_xcond_b_cproj': (0.0, 0.1),
     'L1_xcond_b_mlp1': (0.0, 0.55),
     'L1_xcond_b_mlp2': (0.0, 0.401)}
    factors = {'L0_xcond_qkv_w': 8.0,
     'L0_xcond_sa_proj_w': 6.516,
     'L0_xcond_q_w': 64.0,
     'L0_xcond_fc1_w': 2.728,
     'L0_xcond_kv_w': 2.789}
    for name, (base, spread) in spreads.items():
        noise = np.random.default_rng([zlib.crc32(name.encode()), seed]).standard_normal(out[name].shape)
        drawn = base * np.exp(spread * noise) if base else spread * noise
        out[name] = jnp.asarray(drawn.astype(out[name].dtype))
    for name, factor in factors.items():
        out[name] = (out[name] * factor).astype(out[name].dtype)
    return out
```

```python
from contextlib import ExitStack

import concourse.bass as bass
from concourse import mybir

ALU = mybir.AluOpType
ACT = mybir.ActivationFunctionType
AX = mybir.AxisListType
F32 = mybir.dt.float32
BF16 = mybir.dt.bfloat16
U8 = mybir.dt.uint8

P = 128
B, N, D = 4, 512, 256
H, HD = 16, 16
S = 64
DF = 4 * D
TN = N // P
KC = D // P
MC = DF // P
G = 4
NG = H // G
HC = H // KC
EPS = 1e-6
SCALE = float(HD) ** -0.5
Q_TERMS = (0, 0, 1, 1, 0, 2)
K_TERMS = (0, 1, 0, 1, 2, 0)
ROWS = HD * len(Q_TERMS)
QK_ORDER = (0, 2, 1, 3)
AT_PROJ, AT_NORM2, AT_CROSS, AT_CROSS2, AT_CMROW, AT_ATTEND = 4, 8, 24, 26, 28, 32
AT_NORM3, AT_MLP2 = 44, 52
TILES = H * TN
QK_AT = (4, 6, 8, 10)
MROW_LAG = 4

LAYER = [
    dict(mod_w="L0_xcond_ada_w", mod_b="L0_xcond_ada_b", qkv_w="L0_xcond_qkv_w", qkv_b="L0_xcond_qkv_b",
         p_w="L0_xcond_sa_proj_w", p_b="L0_xcond_sa_proj_b", q_w="L0_xcond_q_w", q_b="L0_xcond_q_b",
         kv_w="L0_xcond_kv_w", kv_b="L0_xcond_kv_b", c_w="L0_xcond_ca_proj_w", c_b="L0_xcond_ca_proj_b",
         w1="L0_xcond_fc1_w", b1="L0_xcond_fc1_b", w2="L0_xcond_fc2_w", b2="L0_xcond_fc2_b"),
    dict(mod_w="L1_xcond_W_mod", mod_b="L1_xcond_b_mod", qkv_w="L1_xcond_W_qkv", qkv_b="L1_xcond_b_qkv",
         p_w="L1_xcond_W_proj", p_b="L1_xcond_b_proj", q_w="L1_xcond_W_qc", q_b="L1_xcond_b_qc",
         kv_w="L1_xcond_W_kvc", kv_b="L1_xcond_b_kvc", c_w="L1_xcond_W_cproj", c_b="L1_xcond_b_cproj",
         w1="L1_xcond_W_mlp1", b1="L1_xcond_b_mlp1", w2="L1_xcond_W_mlp2", b2="L1_xcond_b_mlp2"),
]
GELU = [ACT.Gelu, ACT.Gelu_apprx_tanh]
SHIFT_A, SCALE_A, GATE_A, SHIFT_M, SCALE_M, GATE_M = range(6)


def build(nc, a, out):
    ctx = ExitStack()
    with ctx:
        def sb(name, shape, dt=F32):
            t = ctx.enter_context(nc.sbuf_tensor(name, shape, dt))
            return t[tuple(slice(None) for _ in shape)]

        def sem(name):
            return ctx.enter_context(nc.semaphore(name))

        w_qk = sb("w_qk", [P, KC, 2 * D])
        w_v = sb("w_v", [P, KC, D])
        w_p = sb("w_p", [P, KC, D])
        w_q = sb("w_q", [P, KC, D])
        w_c = sb("w_c", [P, KC, D])
        w_1 = sb("w_1", [P, KC, DF])
        w_2 = sb("w_2", [P, MC, D])
        rows = sb("rows", [P, 5, D])
        b_v, b_p, b_c, b_2, b_cv = (rows[:, i, :] for i in range(5))
        colr = sb("colr", [12 + MC, P])
        colp = sb("colp", [8, P])
        columns = sb("columns", [P, 12 + MC + 8])
        modb = columns[:, 0:12]
        col1 = columns[:, 12:12 + MC]
        cols = columns[:, 12 + MC:]
        colq = sb("colq", [P, 4])
        modc = sb("modc", [P, 12, B])
        gate = sb("gate", [P, B, 2, D])
        gb_m = sb("gb_m", [P, 2, D])
        gbt = sb("gbt", [P, D])
        x = sb("x", [P, B, TN, D])
        xn_a = sb("xn_a", [P, TN, D])
        xt_a = sb("xt_a", [P, KC, N])
        xn_b = sb("xn_b", [P, TN, D])
        xt_b = sb("xt_b", [P, KC, N])
        qst = sb("qst", [ROWS + 3, H, N], BF16)
        kst = sb("kst", [ROWS + 3, H, N], BF16)
        cqst = sb("cqst", [ROWS + 4, H, N], BF16)
        ckst = sb("ckst", [ROWS + 4, H, B * S], BF16)
        vaug = sb("vaug", [P, TN, H, 2 * HD])
        cv = sb("cv", [P, B, H // 2, 4 * HD])
        big = sb("big", [P, 4, 2, N])
        hid = big[:, :, :, :].rearrange("p a b n -> p (a b) n")
        qf = sb("qf", [P, 2, N])
        part = sb("part", [P, 3, 4, N], BF16)
        cpart = sb("cpart", [P, 3, 2, N], BF16)
        u = sb("u", [P, 2, N])
        tmp = sb("tmp", [P, 2, D])
        nmax = sb("nmax", [P, NG, TN, G])
        nres = sb("nres", [P, TN, G])
        mp = sb("mp", [P, NG, TN, 3, G], BF16)
        mrow = sb("mrow", [3 * G, 2, N], BF16)
        cnmax = sb("cnmax", [P, TN, H])
        cnres = sb("cnres", [P, TN, H])
        cmp_ = sb("cmp", [P, TN, 3, H], BF16)
        cmrow = sb("cmrow", [3 * H, N], BF16)
        stat = sb("stat", [P, TN, 6])
        mv = sb("mv", [P, TN, 2])
        rstd = sb("rstd", [P, TN])
        half = sb("half", [P, TN])
        rsum = sb("rsum", [P, TN, G])
        ident = sb("ident", [P, P])
        identb = sb("identb", [P, P], BF16)
        cond = sb("cond", [B, D])
        cs = sb("cs", [B, D])
        csT = sb("csT", [P, KC, B])
        csb = sb("csb", [P, KC, B, P])
        mask8 = sb("mask8", [ROWS + 1, B * S], U8)
        w_mod = big[:, :, :, :].rearrange("p a b n -> p (a b n)")[:, 0:KC * 6 * D].rearrange("p (k n) -> p k n", k=KC)
        w_kv = xt_a
        raw_qk = qf
        raw_q = u[:, 0, :].rearrange("p (k n) -> p k n", k=KC)
        w_ck = u[:, 1, :].rearrange("p (k n) -> p k n", k=KC)
        colpp = sb("colpp", [8, P])
        cx = xn_a[:, 0:2, :]
        cxn = xn_a[:, 2:4, :]
        cxT = xt_b[:, 0, :].rearrange("p (k n) -> p k n", k=KC)
        ckf = xt_b[:, 1, :].rearrange("p (k n) -> p k n", k=KC)

        A = ctx.enter_context(nc.psum_tensor("A", [P, 4, 512], F32))
        R = ctx.enter_context(nc.psum_tensor("R", [P, 2, 512], F32))
        OA = ctx.enter_context(nc.psum_tensor("OA", [P, 512], F32))
        MI = ctx.enter_context(nc.psum_tensor("MI", [P, 512], F32))

        consts = sem("consts")
        c_pool = sem("c_pool")
        c_dve = sem("c_dve")
        ld_x = sem("ld_x")
        ld_w = sem("ld_w")
        ld_c = sem("ld_c")
        lp_cols = sem("lp_cols")
        lp_pe = sem("lp_pe")
        lp_act = sem("lp_act")
        lp_dve = sem("lp_dve")
        lp_pool = sem("lp_pool")
        lp_dma = sem("lp_dma")
        lnv_a = sem("lnv_a")
        lnr_a = sem("lnr_a")
        ln_a = sem("ln_a")
        lnv_b = sem("lnv_b")
        lnr_b = sem("lnr_b")
        ln_b = sem("ln_b")
        xta_full = sem("xta_full")
        xta_ready = sem("xta_ready")
        qk_full = sem("qk_full")
        qk_evac = sem("qk_evac")
        parts = sem("parts")
        stack0 = sem("stack0")
        stack1 = sem("stack1")
        v_full = sem("v_full")
        v_ready = sem("v_ready")
        s_full = sem("s_full")
        s_max = sem("s_max")
        nmparts = sem("nmparts")
        mrow_full = sem("mrow_full")
        mrow_ready = sem("mrow_ready")
        mrd0 = sem("mrd0")
        mrd1 = sem("mrd1")
        mrd2 = sem("mrd2")
        mrd3 = sem("mrd3")
        st_full = sem("st_full")
        exp_done = sem("exp_done")
        av_done = sem("av_done")
        u_ready = sem("u_ready")
        ut_full = sem("ut_full")
        on_ready = sem("on_ready")
        ot_full = sem("ot_full")
        ot_ready = sem("ot_ready")
        pj_full = sem("pj_full")
        x1 = sem("x1")
        xg1 = sem("xg1")
        xtb_full = sem("xtb_full")
        xtb_ready = sem("xtb_ready")
        cq_full = sem("cq_full")
        cq_evac = sem("cq_evac")
        cparts = sem("cparts")
        cstack = sem("cstack")
        cs_full = sem("cs_full")
        cs_max = sem("cs_max")
        cnmparts = sem("cnmparts")
        cmrow_full = sem("cmrow_full")
        cmrow_ready = sem("cmrow_ready")
        cmrd = sem("cmrd")
        cst_full = sem("cst_full")
        cexp_done = sem("cexp_done")
        cav_done = sem("cav_done")
        cu_ready = sem("cu_ready")
        cut_full = sem("cut_full")
        con_ready = sem("con_ready")
        cot_full = sem("cot_full")
        cot_ready = sem("cot_ready")
        cpj_full = sem("cpj_full")
        x2 = sem("x2")
        xg2 = sem("xg2")
        xtc_full = sem("xtc_full")
        xtc_ready = sem("xtc_ready")
        h_full = sem("h_full")
        h_ready = sem("h_ready")
        mo_full = sem("mo_full")
        x3 = sem("x3")
        xg3 = sem("xg3")
        st_out = sem("st_out")
        mrd = [mrd0, mrd1, mrd2, mrd3]
        stack = [stack0, stack1]


        block = ctx.enter_context(nc.Block())
        LPE, LACT, LDVE, LPOOL = 8, 3, 9, 7


        @block.sync
        def _(e):
            def load_weights(L):
                n = LAYER[L]
                if L:
                    e.wait_ge(x3, 2 * B * L)
                    e.wait_ge(mo_full, 2 * B * L)
                cnt = 0

                def ld(dst, src):
                    e.dma_start(dst, src).then_inc(ld_w, 16)
                ld(w_mod, a[n["mod_w"]].rearrange("(k p) n -> p k n", p=P))
                ld(w_kv, a[n["kv_w"]].rearrange("(k p) n -> p k n", p=P))
                for i, t in enumerate(("p_b", "c_b", "b2")):
                    ld(rows[:, i + 1, :], a[n[t]].partition_broadcast(P))
                ld(b_v, a[n["qkv_b"]][2 * D:3 * D].partition_broadcast(P))
                ld(b_cv, a[n["kv_b"]][D:2 * D].partition_broadcast(P))
                ld(gb_m[:, 0, :], a[n["mod_b"]][GATE_A * D:(GATE_A + 1) * D].partition_broadcast(P))
                ld(gb_m[:, 1, :], a[n["mod_b"]][GATE_M * D:(GATE_M + 1) * D].partition_broadcast(P))
                ld(colr[0:12, :], a[n["mod_b"]].rearrange("(j p) -> j p", p=P))
                ld(colr[12:, :], a[n["b1"]].rearrange("(j p) -> j p", p=P))
                ld(colp[0:4, :], a[n["qkv_b"]][0:2 * D].rearrange("(j p) -> j p", p=P))
                ld(colp[4:6, :], a[n["q_b"]].rearrange("(j p) -> j p", p=P))
                ld(colp[6:8, :], a[n["kv_b"]][0:D].rearrange("(j p) -> j p", p=P))
                ld(raw_qk, a[n["qkv_w"]][:, 0:2 * D].rearrange("(k p) n -> p k n", p=P))
                ld(w_v, a[n["qkv_w"]][:, 2 * D:3 * D].rearrange("(k p) n -> p k n", p=P))
                ld(w_p, a[n["p_w"]].rearrange("(k p) n -> p k n", p=P))
                ld(raw_q, a[n["q_w"]].rearrange("(k p) n -> p k n", p=P))
                ld(w_c, a[n["c_w"]].rearrange("(k p) n -> p k n", p=P))
                ld(w_1, a[n["w1"]].rearrange("(k p) n -> p k n", p=P))
                ld(w_2, a[n["w2"]].rearrange("(k p) n -> p k n", p=P))
                ld(cx, a["ctx_1024"].rearrange("(i b) s d -> (b s) i d", i=2))

            def stack_cross_keys(L):
                e.wait_ge(lp_pool, LPOOL * L + 7)
                for c in range(KC):
                    for t, k in enumerate(K_TERMS):
                        e.dma_start(ckst[HD * t:HD * (t + 1), HC * c:HC * (c + 1), :],
                                    cpart[:, k, c, 0:B * S]).then_inc(lp_dma, 16)

            def stack_self(s):
                for i, j in enumerate(QK_ORDER):
                    c, dst, terms = j % 2, (qst, kst)[j // 2], (Q_TERMS, K_TERMS)[j // 2]
                    if s:
                        e.wait_ge(st_full, 32 * (s - 1) + 16 * (c + 1))
                    e.wait_ge(parts, 4 * s + i + 1)
                    for t, k in enumerate(terms):
                        e.dma_start(dst[HD * t:HD * (t + 1), HC * c:HC * (c + 1), :],
                                    part[:, k, j, :]).then_inc(stack[c], 16)

            def max_rows(s, g):
                e.wait_ge(mrow_ready, NG * s + g + 1)
                e.dma_start(qst[ROWS:ROWS + 3, G * g:G * (g + 1), :], mrow[:, g % 2, :]).then_inc(mrd[g], 16)

            def stack_cross(s):
                e.wait_ge(cst_full, NG * s)
                for c in range(KC):
                    e.wait_ge(cparts, KC * s + c + 1)
                    for t, k in enumerate(Q_TERMS):
                        e.dma_start(cqst[HD * t:HD * (t + 1), HC * c:HC * (c + 1), :],
                                    cpart[:, k, c, :]).then_inc(cstack, 16)

            def cross_max_rows(s):
                e.wait_ge(cmrow_ready, s + 1)
                e.dma_start(cqst[ROWS + 1:ROWS + 4, :, :], cmrow[:, :]).then_inc(cmrd, 16)

            def store(s):
                e.wait_ge(x3, 2 * (s + 1))
                e.dma_start(out[s - B].rearrange("(t p) d -> p t d", p=P), x[:, s - B, :, :]).then_inc(st_out, 16)

            e.dma_start(cond[:, :], a["cond_1024"]).then_inc(ld_c, 16)
            e.dma_start(mask8[ROWS:ROWS + 1, :],
                        a["mask_BxS2_bf0"].rearrange("(o b) s -> o (b s)", o=1)).then_inc(ld_c, 16)
            e.dma_start(x[:, :, :, :], a["x"].rearrange("b (t p) d -> p b t d", p=P)).then_inc(ld_x, 16)
            for L in range(2):
                load_weights(L)
                stack_cross_keys(L)
                stack_self(B * L)
                for g in range(NG):
                    max_rows(B * L, g)
                for s in range(B * L, B * L + B):
                    more = s % B < B - 1
                    if more:
                        stack_self(s + 1)
                    stack_cross(s)
                    if more:
                        max_rows(s + 1, 0)
                    cross_max_rows(s)
                    if more:
                        for g in range(1, NG):
                            max_rows(s + 1, g)
                    if L:
                        store(s)
            e.wait_ge(st_out, 16 * B)

        NLD = 22 * 16
        @block.gpsimd
        def _(e):
            n = [0]

            def link(ins):
                n[0] += 1
                ins.then_inc(c_pool, 1)
                e.wait_ge(c_pool, n[0])

            def constants():
                e.memset(ident[:, :], 0.0).then_inc(c_pool, 1)
                link(e.memset(identb[:, :], 0.0))
                n[0] += 1
                e.wait_ge(c_pool, 2)
                for m in (ident, identb):
                    link(e.affine_select(out=m[:, :], in_=m[:, :], compare_op=ALU.not_equal, fill=1.0, base=0,
                                         pattern=[[-1, P]], channel_multiplier=1))
                link(e.memset(half[:, :], -0.5))
                link(e.memset(vaug[:, :, :, HD:2 * HD], 1.0))
                link(e.memset(cv[:, :, :, :], 0.0))
                link(e.memset(cv[0:S, :, :, HD:2 * HD], 1.0))
                link(e.memset(cv[S:P, :, :, 3 * HD:4 * HD], 1.0))
                link(e.memset(kst[ROWS:ROWS + 3, :, :], 1.0))
                link(e.memset(cqst[ROWS:ROWS + 4, :, :], 1.0))
                e.memset(ckst[ROWS:ROWS + 4, :, :], 1.0).then_inc(consts, 1)
                e.wait_ge(consts, 1)

            def power(v, r, vs, rs, target):
                e.wait_ge(vs, target)
                link(e.tensor_scalar(r, v, EPS, 1.0, ALU.add, ALU.mult))
                e.tensor_tensor(r, r, half[:, 0:r.shape[1]], ALU.pow).then_inc(rs, 1)

            def split(f, p0, p1, p2, done):
                link(e.tensor_scalar(p0, f, 1.0, 0.0, ALU.mult, ALU.add))
                link(e.tensor_tensor(f, f, p0, ALU.subtract))
                link(e.tensor_scalar(p1, f, 1.0, 0.0, ALU.mult, ALU.add))
                e.tensor_tensor(p2, f, p1, ALU.subtract).then_inc(done, 1)

            def prepare(L):
                if L:
                    e.wait_ge(cst_full, NG * B * L)
                    pass
                base = LPOOL * L
                if L:
                    e.wait_ge(lp_dve, LDVE * L + 4)
                    link(e.tensor_scalar(rstd[:, 0:2], mv[:, 0:2, 1], EPS, 1.0, ALU.add, ALU.mult))
                    e.tensor_tensor(rstd[:, 0:2], rstd[:, 0:2], half[:, 0:2], ALU.pow).then_inc(lp_pool, 5)
                else:
                    e.memset(rstd[:, 0:2], 1.0).then_inc(lp_pool, 5)
                for c in range(KC):
                    e.wait_ge(lp_act, LACT * L + 2 + c)
                    if L == 0 and c == 0:
                        pass
                    split(ckf[:, c, :], cpart[:, 0, c, 0:B * S], cpart[:, 1, c, 0:B * S], cpart[:, 2, c, 0:B * S], lp_pool)

            def self_parts(s):
                for i, j in enumerate(QK_ORDER):
                    e.wait_ge(qk_evac, 4 * s + i + 1)
                    if i == 0 and s:
                        e.wait_ge(stack0, 192 * s)
                        e.wait_ge(stack1, 192 * s)
                    split(qf[:, i % 2, :], part[:, 0, j, :], part[:, 1, j, :], part[:, 2, j, :], parts)

            def max_parts(s, g):
                e.wait_ge(s_max, 64 * s + 16 * (g + 1))
                if g == 0:
                    e.wait_ge(mrow_full, NG * s)
                f = nmax[:, g, :, :]
                link(e.tensor_scalar(mp[:, g, :, 0, :], f, 1.0, 0.0, ALU.mult, ALU.add))
                link(e.tensor_tensor(nres[:, :, :], f, mp[:, g, :, 0, :], ALU.subtract))
                link(e.tensor_scalar(mp[:, g, :, 1, :], nres[:, :, :], 1.0, 0.0, ALU.mult, ALU.add))
                link(e.tensor_tensor(mp[:, g, :, 2, :], nres[:, :, :], mp[:, g, :, 1, :], ALU.subtract))
                e.tensor_scalar(nres[:, :, :], f, 1.0, 0.0, ALU.mult, ALU.add).then_inc(nmparts, 1)

            def add_bias(s, b_row, gate_row, ready, target, done):
                e.wait_ge(ready, target)
                b = s % B
                if gate_row is not None:
                    link(e.tensor_tensor(gbt[:, :], gate_row, b_row, ALU.mult))
                    b_row = gbt[:, :]
                e.tensor_tensor(x[:, b, :, :], x[:, b, :, :], b_row.unsqueeze(1).broadcast_to([P, TN, D]),
                                ALU.add).then_inc(done, 1)

            constants()
            for L in range(2):
                prepare(L)

                def pre(s):
                    power(mv[:, :, 1], rstd[:, :], lnv_a, lnr_a, s + 1)
                    add_bias(s, b_p, gate[:, s % B, 0, :], ln_a, s + 1, xg1)
                    self_parts(s)

                pre(B * L)
                for g in range(NG):
                    max_parts(B * L, g)
                for s in range(B * L, B * L + B):
                    more = s % B < B - 1
                    if more:
                        pre(s + 1)
                    power(mv[:, :, 1], rstd[:, :], lnv_b, lnr_b, 2 * s + 1)
                    add_bias(s, b_c, None, ln_b, 2 * s + 1, xg2)
                    if more:
                        max_parts(s + 1, 0)
                        max_parts(s + 1, 1)
                    power(mv[:, :, 1], rstd[:, :], lnv_b, lnr_b, 2 * s + 2)
                    add_bias(s, b_2, gate[:, s % B, 1, :], ln_b, 2 * s + 2, xg3)
                    if more:
                        max_parts(s + 1, 2)
                        max_parts(s + 1, 3)

        @block.vector
        def _(e):
            n = [0]

            def link(ins):
                n[0] += 1
                ins.then_inc(c_dve, 1)
                e.wait_ge(c_dve, n[0])

            def statistics(src, vs):
                for t in range(TN):
                    ins = e.bn_stats(stat[:, t, :], src[:, t, :])
                link(ins)
                for t in range(TN):
                    ins = e.bn_aggr(mv[:, t, :], stat[:, t, :])
                ins.then_inc(vs, 1)

            def normalise(src, dst, vs, rs, done, k):
                e.wait_ge(vs, k)
                e.wait_ge(rs, k)
                for t in range(TN):
                    ins = e.tensor_scalar(dst[:, t, :], src[:, t, :], mv[:, t, 0:1], rstd[:, t:t + 1],
                                          ALU.subtract, ALU.mult)
                ins.then_inc(done, 1)

            def prepare(L):
                base = LDVE * L
                n_ = LAYER[L]
                e.wait_ge(ld_w, NLD * (L + 1))
                if L == 0:
                    e.wait_ge(ld_c, 32)
                    e.wait_ge(consts, 1)
                    link(e.tensor_scalar(ckst[ROWS:ROWS + 1, :, :],
                                         mask8[ROWS:ROWS + 1, :].unsqueeze(1).broadcast_to([1, H, B * S]),
                                         -3e38, 3e38, ALU.mult, ALU.mult))
                else:
                    e.wait_ge(h_ready, MC * B * L)
                    link(e.memset(ckst[ROWS:ROWS + 1, :, :], 0.0))
                def permute(dst, src):
                    return e.tensor_copy(dst.rearrange("p (j d h) -> p j d h", d=HD, h=HC),
                                         src.rearrange("p (j h d) -> p j d h", d=HD, h=HC))
                for k in range(KC):
                    permute(w_qk[:, k, :], raw_qk[:, k, :])
                    permute(w_q[:, k, :], raw_q[:, k, :])
                    permute(w_ck[:, k, :], w_kv[:, k, 0:D])
                link(permute(colpp[:, :], colp[:, :]))
                e.tensor_copy(gbt[:, 0:1], gb_m[:, 0, 0:1]).then_inc(lp_cols, 1)
                e.wait_ge(lp_pe, LPE * L + 1)
                if L == 0:
                    link(e.tensor_copy(csT[:, :, :], MI[:, 0:KC * B].rearrange("p (k b) -> p k b", k=KC)))
                    link(e.tensor_copy(csb[:, :, :, :], csT[:, :, :].unsqueeze(3).broadcast_to([P, KC, B, P])))
                e.tensor_copy(columns[:, :], MI[:, 256:256 + 20 + MC]).then_inc(lp_dve, 1)
                e.wait_ge(lp_dve, base + 1)
                link(e.tensor_scalar(colq[:, 0:2], cols[:, 0:2], SCALE, None, ALU.mult))
                e.tensor_scalar(colq[:, 2:4], cols[:, 4:6], SCALE, None, ALU.mult).then_inc(lp_dve, 1)
                e.wait_ge(lp_pe, LPE * L + 2)
                e.tensor_tensor(modc[:, :, :], MI[:, 0:12 * B].rearrange("p (j b) -> p j b", j=12),
                                modb[:, :].unsqueeze(2).broadcast_to([P, 12, B]), ALU.add).then_inc(lp_dve, 1)
                e.wait_ge(lp_dve, base + 3)
                for m in (SCALE_A, SCALE_M):
                    link(e.tensor_scalar(modc[:, 2 * m:2 * m + 2, :], modc[:, 2 * m:2 * m + 2, :], 1.0, None, ALU.add))
                for b in range(B):
                    e.wait_ge(lp_pe, LPE * L + 3)
                    ins = e.tensor_tensor(gate[:, b, :, :], A[:, b, :].rearrange("p (g n) -> p g n", g=2),
                                          gb_m[:, :, :], ALU.add)
                link(ins)
                if L:
                    for t in range(2):
                        ins = e.bn_stats(stat[:, t, :], cx[:, t, :])
                    link(ins)
                    for t in range(2):
                        ins = e.bn_aggr(mv[:, t, :], stat[:, t, :])
                    ins.then_inc(lp_dve, 1)
                    e.wait_ge(lp_dve, base + 4)
                    e.wait_ge(lp_pool, LPOOL * L + 5)
                    for t in range(2):
                        ins = e.tensor_scalar(cxn[:, t, :], cx[:, t, :], mv[:, t, 0:1], rstd[:, t:t + 1],
                                              ALU.subtract, ALU.mult)
                    ins.then_inc(lp_dve, 1)
                else:
                    e.tensor_copy(cxn, cx).then_inc(lp_dve, 2)
                e.wait_ge(lp_pe, LPE * L + 4)
                for k in range(KC):
                    ins = e.tensor_copy(cxT[:, k, :], R[:, k, 0:B * S])
                ins.then_inc(lp_dve, 1)
                for b in range(B):
                    e.wait_ge(lp_pe, LPE * L + 5 + (b // 2))
                    if b == 0 and L:
                        e.wait_ge(cav_done, NG * B * L)
                    src = A[:, b, 0:D].rearrange("p (i o d) -> p i o d", o=2, d=HD)
                    br = b_cv.rearrange("p (i o d) -> p i o d", o=2, d=HD)
                    e.tensor_tensor(cv[0:S, b, :, 0:HD], src[0:S, :, 0, :], br[0:S, :, 0, :], ALU.add)
                    ins = e.tensor_tensor(cv[S:P, b, :, 2 * HD:3 * HD], src[S:P, :, 1, :], br[S:P, :, 1, :], ALU.add)
                ins.then_inc(lp_dve, 3)

            def modulate(full, k, ready, dst, scale, shift, b, src):
                for c in range(KC):
                    e.wait_ge(full, k + c + 1)
                    e.tensor_scalar(dst[:, c, :], src[:, c, :], modc[:, 2 * scale + c, b:b + 1],
                                    modc[:, 2 * shift + c, b:b + 1], ALU.mult, ALU.add).then_inc(ready, 1)

            def pre(s):
                b = s % B
                if s == 0:
                    e.wait_ge(ld_x, 16)
                elif s >= B:
                    e.wait_ge(x3, 2 * (s - B + 1))
                e.wait_ge(xta_full, KC * s)
                statistics(x[:, b, :, :], lnv_a)
                normalise(x[:, b, :, :], xn_a, lnv_a, lnr_a, ln_a, s + 1)
                e.wait_ge(v_full, 2 * s)
                modulate(xta_full, KC * s, xta_ready, xt_a, SCALE_A, SHIFT_A, b, R)

            def values(s):
                e.wait_ge(av_done, 16 * s)
                for i in range(2):
                    e.wait_ge(v_full, 2 * s + i + 1)
                    e.tensor_tensor(vaug[:, 2 * i:2 * i + 2, :, 0:HD],
                                    R[:, i, :].rearrange("p (t h d) -> p t h d", t=2, h=H),
                                    b_v.rearrange("p (h d) -> p h d", h=H).unsqueeze(1).broadcast_to([P, 2, H, HD]),
                                    ALU.add).then_inc(v_ready, 1)

            def maxes(s, m0, m1):
                if s is None:
                    return
                if m0 == 0:
                    e.wait_ge(nmparts, NG * s)
                for m in range(m0, m1):
                    h, t = m // TN, m % TN
                    e.wait_ge(s_full, TILES * s + m + 1)
                    e.tensor_reduce(nmax[:, h // G, t, h % G:h % G + 1], R[:, m % 2, :], AX.X, ALU.max,
                                    negate=True).then_inc(s_max, 1)

            def out_norm(k, g, av, av_k, ur, ut, on):
                e.wait_ge(av, av_k)
                if k >= 2:
                    e.wait_ge(ut, k - 1)
                e.tensor_copy(u[:, g % 2, :], OA[:, :]).then_inc(ur, 1)
                e.wait_ge(ut, k + 1)
                m = MI[:, :].rearrange("p (t j d) -> p t j d", t=TN, j=G)
                link(e.reciprocal(rsum[:, :, :], m[:, :, :, HD]))
                dst = xn_b[:, :, HD * G * g:HD * G * (g + 1)].rearrange("p t (j d) -> p t j d", j=G)
                e.tensor_tensor(dst, m[:, :, :, 0:HD], rsum[:, :, :].unsqueeze(3).broadcast_to([P, TN, G, HD]),
                                ALU.mult).then_inc(on, 1)

            def residual(s, full, xg, xs, gate_row, banks):
                b = s % B
                e.wait_ge(xg, s + 1)
                for i in range(2):
                    e.wait_ge(full, 2 * s + i + 1)
                    y = banks[:, i, :].rearrange("p (t n) -> p t n", t=2)
                    if gate_row is not None:
                        e.wait_ge(xs, 2 * s + i)
                        link(e.tensor_tensor(tmp[:, :, :], y, gate_row.unsqueeze(1).broadcast_to([P, 2, D]), ALU.mult))
                        y = tmp[:, :, :]
                    e.tensor_tensor(x[:, b, 2 * i:2 * i + 2, :], y, x[:, b, 2 * i:2 * i + 2, :], ALU.add).then_inc(xs, 1)

            def split(f, p0, p1, p2, done):
                link(e.tensor_copy(p0, f))
                link(e.tensor_tensor(f, f, p0, ALU.subtract))
                link(e.tensor_copy(p1, f))
                e.tensor_tensor(p2, f, p1, ALU.subtract).then_inc(done, 1)

            def cross_parts(s):
                e.wait_ge(cstack, 192 * s)
                e.wait_ge(lp_dma, 192 * (s // B + 1))
                for c in range(KC):
                    e.wait_ge(cq_evac, KC * s + c + 1)
                    split(qf[:, c, :], cpart[:, 0, c, :], cpart[:, 1, c, :], cpart[:, 2, c, :], cparts)

            def cross_max(s, t0):
                e.wait_ge(cmrow_full, s)
                for t in (t0, t0 + 1):
                    e.wait_ge(cs_full, TN * s + t + 1)
                    i = 2 * (t % 2)
                    e.tensor_reduce(cnmax[:, t, :], A[:, i:i + 2, :].rearrange("p i (h n) -> p (i h) n", n=S),
                                    AX.X, ALU.max, negate=True).then_inc(cs_max, 1)

            def cross_max_parts(s):
                e.wait_ge(cs_max, TN * (s + 1))
                f = cnmax[:, :, :]
                link(e.tensor_copy(cmp_[:, :, 0, :], f))
                link(e.tensor_tensor(cnres[:, :, :], f, cmp_[:, :, 0, :], ALU.subtract))
                link(e.tensor_copy(cmp_[:, :, 1, :], cnres[:, :, :]))
                e.tensor_tensor(cmp_[:, :, 2, :], cnres[:, :, :], cmp_[:, :, 1, :], ALU.subtract).then_inc(cnmparts, 1)

            for L in range(2):
                prepare(L)
                pre(B * L)
                values(B * L)
                maxes(B * L, 0, TILES)
                for s in range(B * L, B * L + B):
                    b = s % B
                    nxt = s + 1 if b < B - 1 else None
                    if nxt is not None:
                        pre(nxt)
                    e.wait_ge(xtc_full, KC * s)
                    for g in range(NG):
                        out_norm(NG * s + g, g, av_done, 16 * s + 4 * (g + 1), u_ready, ut_full, on_ready)
                    if nxt is not None:
                        values(nxt)
                    maxes(nxt, 0, AT_PROJ)
                    residual(s, pj_full, xg1, x1, gate[:, b, 0, :], A[:, 2:4, :])
                    e.wait_ge(x1, 2 * (s + 1))
                    e.wait_ge(ot_full, KC * (s + 1))
                    statistics(x[:, b, :, :], lnv_b)
                    maxes(nxt, AT_PROJ, AT_NORM2)
                    normalise(x[:, b, :, :], xn_b, lnv_b, lnr_b, ln_b, 2 * s + 1)
                    cross_parts(s)
                    maxes(nxt, AT_NORM2, AT_CROSS)
                    cross_max(s, 0)
                    maxes(nxt, AT_CROSS, AT_CROSS2)
                    cross_max(s, 2)
                    cross_max_parts(s)
                    maxes(nxt, AT_CROSS2, AT_ATTEND)
                    e.wait_ge(xtb_full, KC * (s + 1))
                    for g in range(NG):
                        out_norm(NG * s + g, g, cav_done, NG * s + g + 1, cu_ready, cut_full, con_ready)
                        maxes(nxt, AT_ATTEND + 2 * g, AT_ATTEND + 2 * g + 2)
                    residual(s, cpj_full, xg2, x2, None, A[:, 2:4, :])
                    e.wait_ge(x2, 2 * (s + 1))
                    e.wait_ge(cot_full, KC * (s + 1))
                    statistics(x[:, b, :, :], lnv_b)
                    maxes(nxt, AT_ATTEND + 2 * NG, AT_NORM3)
                    normalise(x[:, b, :, :], xn_b, lnv_b, lnr_b, ln_b, 2 * s + 2)
                    e.wait_ge(cpj_full, 2 * (s + 1))
                    modulate(xtc_full, KC * s, xtc_ready, xt_b, SCALE_M, SHIFT_M, b, A)
                    maxes(nxt, AT_NORM3, TILES)
                    residual(s, mo_full, xg3, x3, gate[:, b, 1, :], A[:, 0:2, :])

        @block.scalar
        def _(e):
            def prepare(L):
                if L == 0:
                    e.wait_ge(ld_c, 32)
                    e.activation(cs[:, :], cond[:, :], ACT.Silu).then_inc(lp_act, 1)
                else:
                    e.activation(colq[0:1, 3:4], colq[0:1, 3:4], ACT.Copy) if False else None
                for c in range(KC):
                    e.wait_ge(lp_pe, LPE * L + 7 + c)
                    if c == 0 and L == 0:
                        e.wait_ge(ld_w, NLD)
                    e.activation(ckf[:, c, :], R[:, c, 0:B * S], ACT.Identity, bias=cols[:, 6 + c:7 + c]).then_inc(lp_act, 1 if L == 0 or c == 0 else 2)

            def qk(s, i):
                j = QK_ORDER[i]
                if i == 0:
                    e.wait_ge(lp_dve, LDVE * (s // B) + 2)
                    e.wait_ge(cparts, KC * (s if s % B == 0 else s - 1))
                e.wait_ge(qk_full, 4 * s + i + 1)
                if i >= 2:
                    e.wait_ge(parts, 4 * s + i - 1)
                if j < 2:
                    ins = e.activation(qf[:, i % 2, :], R[:, i % 2, :], ACT.Identity, bias=colq[:, j:j + 1], scale=SCALE)
                else:
                    ins = e.activation(qf[:, i % 2, :], R[:, i % 2, :], ACT.Identity, bias=cols[:, j:j + 1])
                ins.then_inc(qk_evac, 1)

            def row(s, g):
                if s is None:
                    return
                k = NG * s + g
                e.wait_ge(mrow_full, k + 1)
                if k >= 2:
                    e.wait_ge(mrd[(k - 2) % NG], 16 * ((k - 2) // NG + 1))
                e.copy(mrow[:, g % 2, :], R[0:3 * G, 0, :]).then_inc(mrow_ready, 1)

            def exps(s, n):
                if n == 0:
                    e.wait_ge(mo_full, 2 * s)
                    if s % B == 0:
                        e.wait_ge(lp_pe, LPE * (s // B + 1))
                for m in (2 * n, 2 * n + 1):
                    e.wait_ge(st_full, 32 * s + m + 1)
                    if m >= 4:
                        e.wait_ge(av_done, 16 * s + (m - 4) // 2 + 1)
                    e.activation(big[:, m % 4, :, :], A[:, 2 * (m % 2):2 * (m % 2) + 2, :], ACT.Exp).then_inc(exp_done, 1)

            def copies(full, k, dst, ready, src, free, fk):
                e.wait_ge(free, fk)
                for c in range(KC):
                    e.wait_ge(full, k + c + 1)
                    e.copy(dst[:, c, :], src[:, c, :]).then_inc(ready, 1)

            def cross_q(s, nxt):
                e.wait_ge(parts, 4 * (s + 1 if nxt is None else nxt + 1))
                for c in range(KC):
                    e.wait_ge(cq_full, KC * s + c + 1)
                    e.activation(qf[:, c, :], A[:, 2 + c, :], ACT.Identity, bias=colq[:, 2 + c:3 + c],
                                 scale=SCALE).then_inc(cq_evac, 1)

            def cross(s, nxt):
                e.wait_ge(cmrow_full, s + 1)
                e.wait_ge(cmrd, 16 * s)
                e.copy(cmrow[:, :], MI[0:3 * H, :]).then_inc(cmrow_ready, 1)
                e.wait_ge(av_done, 16 * (s + 1))
                for g in range(NG):
                    e.wait_ge(cst_full, NG * s + g + 1)
                    i = 2 * (g % 2)
                    e.activation(big[:, g, :, :], A[:, i:i + 2, :], ACT.Exp).then_inc(cexp_done, 1)
                row(nxt, 1)

            def gelu(s):
                e.wait_ge(cav_done, NG * (s + 1))
                for m in range(MC):
                    e.wait_ge(h_full, MC * s + m + 1)
                    e.activation(hid[:, m, :], A[:, m % 4, :], GELU[s // B], bias=col1[:, m:m + 1]).then_inc(h_ready, 1)

            for L in range(2):
                prepare(L)
                for i in range(4):
                    qk(B * L, i)
                for g in range(NG):
                    row(B * L, g)
                for s in range(B * L, B * L + B):
                    nxt = s + 1 if s % B < B - 1 else None
                    for n in range(16):
                        exps(s, n)
                        if nxt is not None and n in QK_AT:
                            qk(nxt, QK_AT.index(n))
                    copies(ot_full, KC * s, xt_b, ot_ready, A, h_full, MC * s)
                    copies(xtb_full, KC * s, xt_b, xtb_ready, A, pj_full, 2 * (s + 1))
                    cross_q(s, nxt)
                    row(nxt, 0)
                    cross(s, nxt)
                    copies(cot_full, KC * s, xt_b, cot_ready, A, cq_full, KC * (s + 1))
                    gelu(s)
                    row(nxt, 2)
                    row(nxt, 3)

        @block.tensor
        def _(e):
            def mm(o, l, r, start=True, stop=True):
                return e.matmul(o, l, r, start=start, stop=stop, skip_group_check=True)

            def prepare(L):
                if L == 0:
                    e.wait_ge(lp_act, 1)
                    e.wait_ge(consts, 1)
                    for k in range(KC):
                        ins = e.transpose(MI[:, k * B:(k + 1) * B], cs[:, k * P:(k + 1) * P], ident[0:B, 0:B])
                else:
                    e.wait_ge(con_ready, NG * B * L)
                    e.wait_ge(c_dve, 0)
                e.wait_ge(ld_w, NLD * (L + 1))
                e.transpose(MI[:, 256:256 + 12 + MC], colr[:, :], ident[0:12 + MC, 0:12 + MC])
                e.wait_ge(lp_cols, L + 1)
                e.transpose(MI[:, 268 + MC:276 + MC], colpp[:, :], ident[0:8, 0:8]).then_inc(lp_pe, 1)
                e.wait_ge(lp_dve, LDVE * L + 1)
                for j in range(12):
                    for k in range(KC):
                        ins = mm(MI[:, j * B:(j + 1) * B], w_mod[:, k, j * P:(j + 1) * P], csT[:, k, :],
                                 k == 0, k == KC - 1)
                ins.then_inc(lp_pe, 1)
                for b in range(B):
                    for i, m in enumerate((GATE_A, GATE_M)):
                        for k in range(KC):
                            ins = mm(A[:, b, i * D:(i + 1) * D], csb[:, k, b, :], w_mod[:, k, m * D:(m + 1) * D],
                                     k == 0, k == KC - 1)
                ins.then_inc(lp_pe, 1)
                e.wait_ge(lp_dve, LDVE * L + 5)
                for k in range(KC):
                    for i in range(2):
                        ins = e.transpose(R[:, k, i * P:(i + 1) * P], cxn[:, i, k * P:(k + 1) * P], ident[:, :])
                ins.then_inc(lp_pe, 1)
                e.wait_ge(lp_dve, LDVE * L + 6)
                for b in range(B):
                    for o in (0, S):
                        for k in range(KC):
                            ins = mm(A[o:o + S, b, 0:D], cxT[:, k, b * S:(b + 1) * S], w_kv[:, k, D:2 * D],
                                     k == 0, k == KC - 1)
                    if b % 2:
                        ins.then_inc(lp_pe, 1)
                for c in range(KC):
                    for k in range(KC):
                        ins = mm(R[:, c, 0:B * S], w_ck[:, k, c * P:(c + 1) * P], cxT[:, k, :],
                                 k == 0, k == KC - 1)
                    ins.then_inc(lp_pe, 1)

            def transposes(src, dst, full):
                for c in range(KC):
                    for t in range(TN):
                        ins = e.transpose(dst[:, c, t * P:(t + 1) * P], src[:, t, c * P:(c + 1) * P], ident[:, :])
                    ins.then_inc(full, 1)

            def rows_out(src, w, dst, full, kc):
                for i in range(2):
                    for t in (2 * i, 2 * i + 1):
                        for k in range(kc):
                            ins = mm(dst[:, i, (t % 2) * D:(t % 2 + 1) * D], src[:, k, t * P:(t + 1) * P], w[:, k, :],
                                     k == 0, k == kc - 1)
                    ins.then_inc(full, 1)

            def norm_rows(s):
                e.wait_ge(ln_a, s + 1)
                e.wait_ge(s_max, TILES * s)
                e.wait_ge(mrow_ready, NG * s)
                if s % B == 0:
                    e.wait_ge(lp_act, LACT * (s // B + 1))
                transposes(xn_a, R, xta_full)

            def qk(s, i):
                e.wait_ge(xta_ready, KC * (s + 1))
                if i >= 2:
                    e.wait_ge(qk_evac, 4 * s + i - 1)
                for k in range(KC):
                    ins = mm(R[:, i % 2, :], w_qk[:, k, QK_ORDER[i] * P:(QK_ORDER[i] + 1) * P], xt_a[:, k, :],
                             k == 0, k == KC - 1)
                ins.then_inc(qk_full, 1)

            def values(s):
                e.wait_ge(qk_evac, 4 * (s + 1))
                rows_out(xt_a, w_v, R, v_full, KC)

            def scores_rows(s, m0, m1):
                if s is None:
                    return
                if m0 == 0:
                    e.wait_ge(v_ready, 2 * (s + 1))
                for m in range(m0, m1):
                    h, t = m // TN, m % TN
                    if m % (TILES // KC) == 0:
                        e.wait_ge(stack[h // HC], 192 * (s + 1))
                    if m >= 2:
                        e.wait_ge(s_max, TILES * s + m - 1)
                    if m % 16 == MROW_LAG and m > 16:
                        max_row(s, m // 16 - 1)
                        e.wait_ge(mrow_ready, NG * s + m // 16)
                    mm(R[:, m % 2, :], qst[0:ROWS, h, t * P:(t + 1) * P], kst[0:ROWS, h, :]).then_inc(s_full, 1)
                if m1 == TILES:
                    e.wait_ge(s_max, TILES * s + m1 - 1)
                    max_row(s, NG - 1)

            def max_row(s, g):
                e.wait_ge(nmparts, NG * s + g + 1)
                for t in range(TN):
                    ins = mm(R[0:3 * G, 0, t * P:(t + 1) * P], mp[:, g, t, :, :].rearrange("p a b -> p (a b)"), identb[:, :])
                ins.then_inc(mrow_full, 1)

            def un_transpose(k, g, ur, ut, free):
                e.wait_ge(ur, k + 1)
                for f, v in free:
                    e.wait_ge(f, v)
                for t in range(TN):
                    ins = e.transpose(MI[:, t * P:(t + 1) * P], u[:, g % 2, t * P:(t + 1) * P], ident[:, :])
                ins.then_inc(ut, 1)

            def attend(s, nxt):
                def st(g, kc):
                    for i in range(2):
                        m = 32 * s + 2 * (4 * g + kc) + i
                        if m % 32 >= 2:
                            e.wait_ge(exp_done, m - 1)
                        else:
                            e.wait_ge(x3, 2 * s)
                        for j in (2 * i, 2 * i + 1):
                            h = G * g + j
                            ins = mm(A[:, j, :], kst[0:ROWS + 3, h, kc * P:(kc + 1) * P], qst[0:ROWS + 3, h, :])
                        ins.then_inc(st_full, 1)

                def av(g, kc):
                    e.wait_ge(exp_done, 32 * s + 2 * (4 * g + kc) + 2)
                    if kc == 0:
                        if g:
                            e.wait_ge(u_ready, NG * s + g)
                        else:
                            e.wait_ge(cu_ready, NG * s)
                    for j in range(G):
                        ins = mm(OA[32 * j:32 * j + 32, :], vaug[:, kc, G * g + j, :], big[:, 2 * (kc % 2) + j // 2, j % 2, :],
                                 kc == 0, kc == TN - 1)
                    ins.then_inc(av_done, 1)

                last = None
                for g in range(NG):
                    for kc in range(TN):
                        if kc == 0:
                            e.wait_ge(mrd[g], 16 * (s + 1))
                        st(g, kc)
                        n = TN * g + kc
                        if nxt is not None and n == QK_AT[0] - 2:
                            norm_rows(nxt)
                        if nxt is not None and n in QK_AT:
                            qk(nxt, QK_AT.index(n))
                        if last:
                            av(*last)
                        if kc == 2 and g:
                            un_transpose(NG * s + g - 1, g - 1, u_ready, ut_full,
                                         [(on_ready, NG * s + g - 1)] if g > 1 else [(con_ready, NG * s), (lp_dve, LDVE * (s // B + 1))])
                        last = (g, kc)
                av(*last)
                un_transpose(NG * s + NG - 1, NG - 1, u_ready, ut_full, [(on_ready, NG * s + NG - 1)])

            def post_self(s, nxt):
                e.wait_ge(on_ready, NG * (s + 1))
                e.wait_ge(exp_done, 32 * (s + 1))
                transposes(xn_b, A, ot_full)
                scores_rows(nxt, 0, AT_PROJ)
                e.wait_ge(ot_ready, KC * (s + 1))
                rows_out(xt_b, w_p, A[:, 2:4, :], pj_full, KC)

            def cross(s, nxt):
                b = s % B
                scores_rows(nxt, AT_PROJ, AT_NORM2)
                e.wait_ge(ln_b, 2 * s + 1)
                transposes(xn_b, A, xtb_full)
                e.wait_ge(xtb_ready, KC * (s + 1))
                e.wait_ge(x1, 2 * (s + 1))
                for c in range(KC):
                    for k in range(KC):
                        ins = mm(A[:, 2 + c, :], w_q[:, k, c * P:(c + 1) * P], xt_b[:, k, :], k == 0, k == KC - 1)
                    ins.then_inc(cq_full, 1)
                scores_rows(nxt, AT_NORM2, AT_CROSS)
                e.wait_ge(cstack, 192 * (s + 1))
                e.wait_ge(cq_evac, KC * (s + 1))
                e.wait_ge(lp_dma, 192 * (s // B + 1))
                for t in range(TN):
                    if t == 2:
                        scores_rows(nxt, AT_CROSS, AT_CROSS2)
                    if t >= 2:
                        e.wait_ge(cs_max, TN * s + t - 1)
                    for h in range(H):
                        ins = mm(A[:, 2 * (t % 2) + h // HC, (h % HC) * S:(h % HC + 1) * S],
                                 cqst[0:ROWS + 1, h, t * P:(t + 1) * P], ckst[0:ROWS + 1, h, b * S:(b + 1) * S])
                    ins.then_inc(cs_full, 1)
                scores_rows(nxt, AT_CROSS2, AT_CMROW)
                e.wait_ge(cnmparts, s + 1)
                e.wait_ge(on_ready, NG * (s + 1))
                for t in range(TN):
                    ins = mm(MI[0:3 * H, t * P:(t + 1) * P], cmp_[:, t, :, :].rearrange("p a b -> p (a b)"), identb[:, :])
                ins.then_inc(cmrow_full, 1)
                scores_rows(nxt, AT_CMROW, AT_ATTEND)
                e.wait_ge(cmrd, 16 * (s + 1))
                e.wait_ge(cs_max, TN * (s + 1))

                def st(g):
                    if g >= 2:
                        e.wait_ge(cexp_done, NG * s + g - 1)
                    for j in range(G):
                        o = S * (j % 2)
                        ins = mm(A[o:o + S, 2 * (g % 2) + j // 2, :], ckst[:, G * g + j, b * S:(b + 1) * S], cqst[:, G * g + j, :])
                    ins.then_inc(cst_full, 1)

                def av(g):
                    e.wait_ge(cexp_done, NG * s + g + 1)
                    if g:
                        e.wait_ge(cu_ready, NG * s + g)
                    else:
                        e.wait_ge(u_ready, NG * (s + 1))
                    for i in range(2):
                        ins = mm(OA[S * i:S * (i + 1), :], cv[:, b, 2 * g + i, :], big[:, g, i, :])
                    ins.then_inc(cav_done, 1)

                st(0)
                for g in range(NG):
                    if g + 1 < NG:
                        st(g + 1)
                    av(g)
                    un_transpose(NG * s + g, g, cu_ready, cut_full,
                                 [(con_ready, NG * s + g)] if g else [(cmrow_ready, s + 1)])
                    scores_rows(nxt, AT_ATTEND + 2 * g, AT_ATTEND + 2 * g + 2)
                e.wait_ge(con_ready, NG * (s + 1))
                e.wait_ge(cexp_done, NG * (s + 1))
                transposes(xn_b, A, cot_full)
                e.wait_ge(cot_ready, KC * (s + 1))
                rows_out(xt_b, w_c, A[:, 2:4, :], cpj_full, KC)
                scores_rows(nxt, AT_ATTEND + 2 * NG, AT_NORM3)

            def mlp(s, nxt):
                e.wait_ge(ln_b, 2 * s + 2)
                transposes(xn_b, A, xtc_full)
                e.wait_ge(xtc_ready, KC * (s + 1))
                e.wait_ge(x2, 2 * (s + 1))
                for m in range(MC):
                    if m >= 4:
                        e.wait_ge(h_ready, MC * s + m - 3)
                    for k in range(KC):
                        ins = mm(A[:, m % 4, :], w_1[:, k, m * P:(m + 1) * P], xt_b[:, k, :], k == 0, k == KC - 1)
                    ins.then_inc(h_full, 1)
                    scores_rows(nxt, AT_NORM3 + m, AT_NORM3 + m + 1)
                e.wait_ge(h_ready, MC * (s + 1))
                for t in range(TN):
                    for k in range(MC):
                        ins = mm(A[:, t // 2, (t % 2) * D:(t % 2 + 1) * D], hid[:, k, t * P:(t + 1) * P], w_2[:, k, :],
                                 k == 0, k == MC - 1)
                    if t % 2:
                        ins.then_inc(mo_full, 1)
                    m = AT_MLP2 + (TILES - AT_MLP2) // TN * t
                    scores_rows(nxt, m, m + (TILES - AT_MLP2) // TN)

            for L in range(2):
                prepare(L)
                norm_rows(B * L)
                for i in range(4):
                    qk(B * L, i)
                values(B * L)
                scores_rows(B * L, 0, TILES)
                for s in range(B * L, B * L + B):
                    nxt = s + 1 if s % B < B - 1 else None
                    attend(s, nxt)
                    if nxt is not None:
                        values(nxt)
                    post_self(s, nxt)
                    cross(s, nxt)
                    mlp(s, nxt)


_INS = ["x", "cond_1024", "ctx_1024", "mask_BxS2_bf0"] + [n for layer in LAYER for n in layer.values()]


def kernel(**inputs):
    import numpy as _np
    import concourse.bacc as _bacc
    from concourse import mybir as _mybir
    from concourse.bass_utils import run_bass_kernel_spmd as _run

    nc = _bacc.Bacc("TRN2", target_bir_lowering=False, num_devices=1)
    arrays, args = {}, {}
    for name in _INS:
        v = _np.ascontiguousarray(inputs[name])
        arrays[f"in_{name}_dram"] = v
        args[name] = nc.dram_tensor(f"in_{name}_dram", v.shape, _mybir.dt.from_np(v.dtype), kind="ExternalInput").ap()
    o = nc.dram_tensor("out_0_dram", (B, N, D), _mybir.dt.float32, kind="ExternalOutput").ap()
    build(nc, args, o)
    r = _run(nc, [arrays], core_ids=[0])
    return r.results[0]["out_0_dram"]
```

```python
from contextlib import ExitStack

import concourse.bass as bass
from concourse import mybir

ALU = mybir.AluOpType
ACT = mybir.ActivationFunctionType
AX = mybir.AxisListType
F32 = mybir.dt.float32
BF16 = mybir.dt.bfloat16
U8 = mybir.dt.uint8

P = 128
B, N, D = 4, 512, 256
H, HD = 16, 16
S = 64
DF = 4 * D
TN = N // P
KC = D // P
MC = DF // P
G = 4
NG = H // G
HC = H // KC
EPS = 1e-6
SCALE = float(HD) ** -0.5
Q_TERMS = (0, 0, 1, 1, 0, 2)
K_TERMS = (0, 1, 0, 1, 2, 0)
ROWS = HD * len(Q_TERMS)
QK_ORDER = (0, 2, 1, 3)
TILES = H * TN
TILES_OF = dict(unit13=0, unit14=2, unit15=2, proj=4, norm2=4, halfq=2, stack=10, cross2=2, cmrow=2, crows=4,
                g0=2, g1=2, g2=2, g3=2, norm3=2, halfm=2, h4=2, h5=2, h6=2, h7=2, o0=3, o1=3, o2=3, o3=3)
AT, _m = {}, 0
for _step, _n in TILES_OF.items():
    AT[_step], _m = (_m, _m + _n), _m + _n
assert _m == TILES
QK_AT = (4, 6, 8, 10)
MROW_LAG = 4

LAYER = [
    dict(mod_w="L0_xcond_ada_w", mod_b="L0_xcond_ada_b", qkv_w="L0_xcond_qkv_w", qkv_b="L0_xcond_qkv_b",
         p_w="L0_xcond_sa_proj_w", p_b="L0_xcond_sa_proj_b", q_w="L0_xcond_q_w", q_b="L0_xcond_q_b",
         kv_w="L0_xcond_kv_w", kv_b="L0_xcond_kv_b", c_w="L0_xcond_ca_proj_w", c_b="L0_xcond_ca_proj_b",
         w1="L0_xcond_fc1_w", b1="L0_xcond_fc1_b", w2="L0_xcond_fc2_w", b2="L0_xcond_fc2_b"),
    dict(mod_w="L1_xcond_W_mod", mod_b="L1_xcond_b_mod", qkv_w="L1_xcond_W_qkv", qkv_b="L1_xcond_b_qkv",
         p_w="L1_xcond_W_proj", p_b="L1_xcond_b_proj", q_w="L1_xcond_W_qc", q_b="L1_xcond_b_qc",
         kv_w="L1_xcond_W_kvc", kv_b="L1_xcond_b_kvc", c_w="L1_xcond_W_cproj", c_b="L1_xcond_b_cproj",
         w1="L1_xcond_W_mlp1", b1="L1_xcond_b_mlp1", w2="L1_xcond_W_mlp2", b2="L1_xcond_b_mlp2"),
]
GELU = [ACT.Gelu, ACT.Gelu_apprx_tanh]
GATE_A, GATE_M = 2, 5
SHIFT_A, SCALE_A, SHIFT_M, SCALE_M = range(4)


def build(nc, a, out):
    ctx = ExitStack()
    with ctx:
        def sb(name, shape, dt=F32):
            t = ctx.enter_context(nc.sbuf_tensor(name, shape, dt))
            return t[tuple(slice(None) for _ in shape)]

        def sem(name):
            return ctx.enter_context(nc.semaphore(name))

        w_qk = sb("w_qk", [P, KC, 2 * D])
        w_v = sb("w_v", [P, KC, D])
        w_p = sb("w_p", [P, KC, D])
        w_q = sb("w_q", [P, KC, D])
        w_c = sb("w_c", [P, KC, D])
        w_1 = sb("w_1", [P, KC, DF])
        w_2 = sb("w_2", [P, MC, D])
        rows = sb("rows", [P, 5, D])
        b_v, b_p, b_c, b_2, b_cv = (rows[:, i, :] for i in range(5))
        colr = sb("colr", [12 + MC, P])
        colp = sb("colp", [8, P])
        colpp = sb("colpp", [8, P])
        NCOL = 12 + MC + 8
        columns = sb("columns", [P, 2, NCOL])
        modb = columns[:, :, 0:12]
        col1 = columns[:, :, 12:12 + MC]
        cols = columns[:, :, 12 + MC:]
        colq = sb("colq", [P, 2, 4])
        modc = sb("modc", [P, 2, 8, B])
        gate = sb("gate", [P, 2, D])
        grow = sb("grow", [B, 2, 2, D])
        gb_m = sb("gb_m", [B, 2, D])
        gbt = sb("gbt", [P, D])
        x = sb("x", [P, B, TN, D])
        xn_a = sb("xn_a", [P, TN, D])
        xt_a = sb("xt_a", [P, KC, N])
        xn_b = sb("xn_b", [P, TN, D])
        xt_b = sb("xt_b", [P, KC, N])
        qst = sb("qst", [ROWS + 3, H, N], BF16)
        kst = sb("kst", [ROWS + 3, H, N], BF16)
        cqst = sb("cqst", [ROWS + 4, H, N], BF16)
        ckst = sb("ckst", [ROWS + 4, H, B * S], BF16)
        vaug = sb("vaug", [P, TN, H, 2 * HD])
        cv = sb("cv", [P, B, H // 2, 4 * HD])
        big = sb("big", [P, 4, 2, N])
        hid = big[:, :, :, :].rearrange("p a b n -> p (a b) n")
        qf = sb("qf", [P, 2, N])
        part = sb("part", [P, 3, 4, N], BF16)
        cpart = sb("cpart", [P, 3, 2, N], BF16)
        u = sb("u", [P, 2, N])
        tmp = sb("tmp", [P, 2, D])
        nmax = sb("nmax", [P, NG, TN, G])
        nres = sb("nres", [P, TN, G])
        mp = sb("mp", [P, NG, TN, 3, G], BF16)
        mrow = sb("mrow", [3 * G, 2, N], BF16)
        cnmax = sb("cnmax", [P, TN, H])
        cnres = sb("cnres", [P, TN, H])
        cmp_ = sb("cmp", [P, TN, 3, H], BF16)
        cmrow = sb("cmrow", [3 * H, N], BF16)
        stat = sb("stat", [P, TN, 6])
        mv = sb("mv", [P, TN, 2])
        rstd = sb("rstd", [P, TN])
        half = sb("half", [P, TN])
        rsum = sb("rsum", [P, TN, G])
        ident = sb("ident", [P, P])
        identb = sb("identb", [P, P], BF16)
        cond = sb("cond", [B, D])
        cs = gbt[0:B, :]
        csT = sb("csT", [P, KC, B])
        stage = sb("stage", [P, KC, 2 * D])
        cxT = sb("cxT", [P, 2, KC, B * S])
        cmv = sb("cmv", [P, 2, 2])
        crstd = sb("crstd", [P, 2])
        mask8 = sb("mask8", [ROWS + 1, B * S], U8)
        w_mod = big[:, 0:3, :, :].rearrange("p a b n -> p (a b n)").rearrange("p (k n) -> p k n", k=KC)
        modr = xn_b.rearrange("p t d -> p (t d)")[0:B, :]
        w_kv = xt_b
        w_ck = tmp
        raw_q = (big[:, 3, 0, :].rearrange("p (k n) -> p k n", k=KC), stage[:, 0, :].rearrange("p (k n) -> p k n", k=KC))
        ckf = (big[:, 3, 1, :].rearrange("p (k n) -> p k n", k=KC), stage[:, 1, :].rearrange("p (k n) -> p k n", k=KC))
        cx = u[:, 0, :].rearrange("p (k n) -> p k n", k=2)
        cxn = u[:, 1, :].rearrange("p (k n) -> p k n", k=2)

        A = ctx.enter_context(nc.psum_tensor("A", [P, 4, 512], F32))
        R = ctx.enter_context(nc.psum_tensor("R", [P, 2, 512], F32))
        OA = ctx.enter_context(nc.psum_tensor("OA", [P, 512], F32))
        MI = ctx.enter_context(nc.psum_tensor("MI", [P, 512], F32))

        idents = sem("idents")
        fill_v = sem("fill_v")
        fill_k = sem("fill_k")
        c_pool = sem("c_pool")
        c_dve = sem("c_dve")
        ld_x0 = sem("ld_x0")
        ld_x = sem("ld_x")
        ld_cond = sem("ld_cond")
        ld_ctx = sem("ld_ctx")
        ld_cols = sem("ld_cols")
        ld_mod = sem("ld_mod")
        ld_qk = sem("ld_qk")
        ld_v = sem("ld_v")
        ld_bp = sem("ld_bp")
        ld_kv = sem("ld_kv")
        ld_w = sem("ld_w")
        silu = sem("silu")
        csT_full = sem("csT_full")
        csT_ready = sem("csT_ready")
        colp_ready = sem("colp_ready")
        cols_full = sem("cols_full")
        cols_ready = sem("cols_ready")
        mr_full = sem("mr_full")
        mr_ready = sem("mr_ready")
        mc_full = sem("mc_full")
        mc_ready = sem("mc_ready")
        cxv = sem("cxv")
        cxr = sem("cxr")
        cxn_ready = sem("cxn_ready")
        cxt_full = sem("cxt_full")
        cxt_ready = sem("cxt_ready")
        wqk_ready = sem("wqk_ready")
        wq_ready = sem("wq_ready")
        kv_full = sem("kv_full")
        kv_ready = sem("kv_ready")
        ck_full = sem("ck_full")
        ck_ready = sem("ck_ready")
        ckparts = sem("ckparts")
        ckstack = sem("ckstack")
        gate_full = sem("gate_full")
        gate_ready = sem("gate_ready")
        lnv_a = sem("lnv_a")
        lnr_a = sem("lnr_a")
        ln_a = sem("ln_a")
        lnv_b = sem("lnv_b")
        lnr_b = sem("lnr_b")
        ln_b = sem("ln_b")
        xta_full = sem("xta_full")
        xta_ready = sem("xta_ready")
        qk_full = sem("qk_full")
        qk_evac = sem("qk_evac")
        parts = sem("parts")
        stack0 = sem("stack0")
        stack1 = sem("stack1")
        v_full = sem("v_full")
        v_ready = sem("v_ready")
        s_full = sem("s_full")
        s_max = sem("s_max")
        nmparts = sem("nmparts")
        mrow_full = sem("mrow_full")
        mrow_ready = sem("mrow_ready")
        mrd0 = sem("mrd0")
        mrd1 = sem("mrd1")
        mrd2 = sem("mrd2")
        mrd3 = sem("mrd3")
        st_full = sem("st_full")
        exp_done = sem("exp_done")
        av_done = sem("av_done")
        u_ready = sem("u_ready")
        ut_full = sem("ut_full")
        on_ready = sem("on_ready")
        ot_full = sem("ot_full")
        ot_ready = sem("ot_ready")
        pj_full = sem("pj_full")
        x1 = sem("x1")
        xg1 = sem("xg1")
        xtb_full = sem("xtb_full")
        xtb_ready = sem("xtb_ready")
        cq_full = sem("cq_full")
        cq_evac = sem("cq_evac")
        cparts = sem("cparts")
        cstack = sem("cstack")
        cs_full = sem("cs_full")
        cs_max = sem("cs_max")
        cnmparts = sem("cnmparts")
        cmrow_full = sem("cmrow_full")
        cmrow_ready = sem("cmrow_ready")
        cmrd = sem("cmrd")
        cst_full = sem("cst_full")
        cexp_done = sem("cexp_done")
        cav_done = sem("cav_done")
        cu_ready = sem("cu_ready")
        cut_full = sem("cut_full")
        con_ready = sem("con_ready")
        cot_full = sem("cot_full")
        cot_ready = sem("cot_ready")
        cpj_full = sem("cpj_full")
        x2 = sem("x2")
        xg2 = sem("xg2")
        xtc_full = sem("xtc_full")
        xtc_ready = sem("xtc_ready")
        h_full = sem("h_full")
        h_ready = sem("h_ready")
        mo_full = sem("mo_full")
        x3 = sem("x3")
        xg3 = sem("xg3")
        st_out = sem("st_out")
        mrd = [mrd0, mrd1, mrd2, mrd3]
        stack = [stack0, stack1]


        block = ctx.enter_context(nc.Block())
        NLD_COLS, NLD_MOD, NLD_V, NLD_KV, NLD_W = 16 * 5, 16 * 3, 16 * 2, 16 * 3, 16 * 6


        @block.sync
        def _(e):
            def ld(dst, src, done):
                e.dma_start(dst, src).then_inc(done, 16)

            def weight(name):
                return a[name].rearrange("(k p) n -> p k n", p=P)

            def load_modulation(L):
                n = LAYER[L]
                if L:
                    e.wait_ge(cols_full, L)
                ld(colr[0:12, :], a[n["mod_b"]].rearrange("(j p) -> j p", p=P), ld_cols)
                ld(colr[12:, :], a[n["b1"]].rearrange("(j p) -> j p", p=P), ld_cols)
                ld(colp[0:4, :], a[n["qkv_b"]][0:2 * D].rearrange("(j p) -> j p", p=P), ld_cols)
                ld(colp[4:6, :], a[n["q_b"]].rearrange("(j p) -> j p", p=P), ld_cols)
                ld(colp[6:8, :], a[n["kv_b"]][0:D].rearrange("(j p) -> j p", p=P), ld_cols)
                if L:
                    e.wait_ge(mr_full, L)
                    e.wait_ge(mr_ready, L)
                ld(w_mod, weight(n["mod_w"]), ld_mod)
                for i, m in enumerate((GATE_A, GATE_M)):
                    ld(gb_m[:, i, :], a[n["mod_b"]][m * D:(m + 1) * D].partition_broadcast(B), ld_mod)

            def load_qk(L):
                if L:
                    e.wait_ge(wqk_ready, L)
                ld(stage, weight(LAYER[L]["qkv_w"])[:, :, 0:2 * D], ld_qk)

            def load_v(L):
                n = LAYER[L]
                if L:
                    e.wait_ge(v_ready, 2 * B * L)
                ld(w_v, weight(n["qkv_w"])[:, :, 2 * D:3 * D], ld_v)
                ld(b_v, a[n["qkv_b"]][2 * D:3 * D].partition_broadcast(P), ld_v)

            def load_bp(L):
                if L:
                    e.wait_ge(xg1, B * L)
                ld(b_p, a[LAYER[L]["p_b"]].partition_broadcast(P), ld_bp)

            def load_rest(L):
                n = LAYER[L]
                if L:
                    e.wait_ge(x3, 2 * B * L)
                    e.wait_ge(wqk_ready, L + 1)
                ld(w_kv, weight(n["kv_w"]), ld_kv)
                ld(raw_q[L], weight(n["q_w"]), ld_kv)
                ld(b_cv, a[n["kv_b"]][D:2 * D].partition_broadcast(P), ld_kv)
                ld(w_p, weight(n["p_w"]), ld_w)
                ld(w_c, weight(n["c_w"]), ld_w)
                ld(w_1, weight(n["w1"]), ld_w)
                ld(w_2, weight(n["w2"]), ld_w)
                for row, t in ((b_c, "c_b"), (b_2, "b2")):
                    ld(row, a[n[t]].partition_broadcast(P), ld_w)

            def stack_cross_keys(L):
                if L:
                    e.wait_ge(cst_full, NG * B * L)
                for c in range(KC):
                    e.wait_ge(ckparts, KC * L + c + 1)
                    for t, k in enumerate(K_TERMS):
                        ld(ckst[HD * t:HD * (t + 1), HC * c:HC * (c + 1), :], cpart[:, k, c, 0:B * S], ckstack)

            def stack_self(s):
                for i, j in enumerate(QK_ORDER):
                    c, dst, terms = j % 2, (qst, kst)[j // 2], (Q_TERMS, K_TERMS)[j // 2]
                    if s:
                        e.wait_ge(st_full, 32 * (s - 1) + 16 * (c + 1))
                    e.wait_ge(parts, 4 * s + i + 1)
                    for t, k in enumerate(terms):
                        e.dma_start(dst[HD * t:HD * (t + 1), HC * c:HC * (c + 1), :],
                                    part[:, k, j, :]).then_inc(stack[c], 16)

            def max_rows(s, g):
                e.wait_ge(mrow_ready, NG * s + g + 1)
                e.dma_start(qst[ROWS:ROWS + 3, G * g:G * (g + 1), :], mrow[:, g % 2, :]).then_inc(mrd[g], 16)

            def stack_cross(s):
                e.wait_ge(cst_full, NG * s)
                for c in range(KC):
                    e.wait_ge(cparts, KC * s + c + 1)
                    for t, k in enumerate(Q_TERMS):
                        e.dma_start(cqst[HD * t:HD * (t + 1), HC * c:HC * (c + 1), :],
                                    cpart[:, k, c, :]).then_inc(cstack, 16)

            def cross_max_rows(s):
                e.wait_ge(cmrow_ready, s + 1)
                e.dma_start(cqst[ROWS + 1:ROWS + 4, :, :], cmrow[:, :]).then_inc(cmrd, 16)

            def store(s):
                e.wait_ge(x3, 2 * (s + 1))
                e.dma_start(out[s - B].rearrange("(t p) d -> p t d", p=P), x[:, s - B, :, :]).then_inc(st_out, 16)

            ld(cond[:, :], a["cond_1024"], ld_cond)
            ld(x[:, 0, :, :], a["x"][0].rearrange("(t p) d -> p t d", p=P), ld_x0)
            load_modulation(0)
            load_qk(0)
            ld(cx, a["ctx_1024"].rearrange("(i b) s d -> (b s) i d", i=2), ld_ctx)
            ld(mask8[ROWS:ROWS + 1, :], a["mask_BxS2_bf0"].rearrange("(o b) s -> o (b s)", o=1), ld_ctx)
            load_v(0)
            load_bp(0)
            load_rest(0)
            ld(x[:, 1:B, :, :], a["x"][1:B].rearrange("b (t p) d -> p b t d", p=P), ld_x)
            load_modulation(1)
            load_qk(1)
            stack_self(0)
            stack_cross_keys(0)
            for g in range(NG):
                max_rows(0, g)
            for s in range(2 * B):
                more = s < 2 * B - 1
                if s == B:
                    load_rest(1)
                if more:
                    stack_self(s + 1)
                if s == B - 1:
                    load_v(1)
                    load_bp(1)
                if s == B:
                    stack_cross_keys(1)
                stack_cross(s)
                for g in range(NG):
                    if g == 1:
                        cross_max_rows(s)
                    if more:
                        max_rows(s + 1, g)
                if s >= B:
                    store(s)
            e.wait_ge(st_out, 16 * B)

        @block.gpsimd
        def _(e):
            n = [0]

            def link(ins):
                n[0] += 1
                ins.then_inc(c_pool, 1)
                e.wait_ge(c_pool, n[0])

            def constants():
                e.memset(ident[:, :], 0.0).then_inc(c_pool, 1)
                link(e.memset(identb[:, :], 0.0))
                n[0] += 1
                e.wait_ge(c_pool, 2)
                for m in (ident, identb):
                    ins = e.affine_select(out=m[:, :], in_=m[:, :], compare_op=ALU.not_equal, fill=1.0, base=0,
                                          pattern=[[-1, P]], channel_multiplier=1)
                ins.then_inc(idents, 1)
                link(e.memset(half[:, :], -0.5))

            def fill():
                link(e.memset(vaug[:, :, :, HD:2 * HD], 1.0))
                link(e.memset(cv[:, :, :, :], 0.0))
                link(e.memset(cv[0:S, :, :, HD:2 * HD], 1.0))
                e.memset(cv[S:P, :, :, 3 * HD:4 * HD], 1.0).then_inc(fill_v, 1)
                e.wait_ge(fill_v, 1)

            def power_halves(k):
                for i in range(2):
                    ts = slice(2 * i, 2 * i + 2)
                    power(mv[:, ts, 1], rstd[:, ts], lnv_b, lnr_b, k + i + 1)

            def power(v, r, vs, rs, target):
                e.wait_ge(vs, target)
                link(e.tensor_scalar(r, v, EPS, 1.0, ALU.add, ALU.mult))
                e.tensor_tensor(r, r, half[:, 0:r.shape[1]], ALU.pow).then_inc(rs, 1)

            def split(f, p0, p1, p2, done):
                link(e.tensor_scalar(p0, f, 1.0, 0.0, ALU.mult, ALU.add))
                link(e.tensor_tensor(f, f, p0, ALU.subtract))
                link(e.tensor_scalar(p1, f, 1.0, 0.0, ALU.mult, ALU.add))
                e.tensor_tensor(p2, f, p1, ALU.subtract).then_inc(done, 1)

            def key_parts(L):
                if L:
                    e.wait_ge(cstack, 192 * B * L)
                for c in range(KC):
                    e.wait_ge(ck_ready, KC * L + c + 1)
                    split(ckf[L][:, c, :], cpart[:, 0, c, 0:B * S], cpart[:, 1, c, 0:B * S], cpart[:, 2, c, 0:B * S], ckparts)

            def self_parts(s):
                for i, j in enumerate(QK_ORDER):
                    e.wait_ge(qk_evac, 4 * s + i + 1)
                    if i == 0 and s:
                        e.wait_ge(stack0, 192 * s)
                        e.wait_ge(stack1, 192 * s)
                    split(qf[:, i % 2, :], part[:, 0, j, :], part[:, 1, j, :], part[:, 2, j, :], parts)

            def max_parts(s, g):
                e.wait_ge(s_max, 64 * s + 16 * (g + 1))
                if g == 0:
                    e.wait_ge(mrow_full, NG * s)
                f = nmax[:, g, :, :]
                link(e.tensor_scalar(mp[:, g, :, 0, :], f, 1.0, 0.0, ALU.mult, ALU.add))
                link(e.tensor_tensor(nres[:, :, :], f, mp[:, g, :, 0, :], ALU.subtract))
                link(e.tensor_scalar(mp[:, g, :, 1, :], nres[:, :, :], 1.0, 0.0, ALU.mult, ALU.add))
                link(e.tensor_tensor(mp[:, g, :, 2, :], nres[:, :, :], mp[:, g, :, 1, :], ALU.subtract))
                e.tensor_scalar(nres[:, :, :], f, 1.0, 0.0, ALU.mult, ALU.add).then_inc(nmparts, 1)

            def add_bias(s, b_row, gate_row, ready, target, done):
                e.wait_ge(ready, target)
                b = s % B
                if gate_row is not None:
                    link(e.tensor_tensor(gbt[:, :], gate_row, b_row, ALU.mult))
                    b_row = gbt[:, :]
                e.tensor_tensor(x[:, b, :, :], x[:, b, :, :], b_row.unsqueeze(1).broadcast_to([P, TN, D]),
                                ALU.add).then_inc(done, 1)

            def parts_until(s, m0, m1, more):
                for g in range(NG):
                    if more and m0 < TILES // NG * (g + 1) <= m1:
                        max_parts(s, g)

            constants()
            power(mv[:, :, 1], rstd[:, :], lnv_a, lnr_a, 1)
            power(cmv[:, :, 1], crstd[:, :], cxv, cxr, 1)
            fill()
            self_parts(0)
            key_parts(0)
            for g in range(NG):
                max_parts(0, g)
            for s in range(2 * B):
                more = s < 2 * B - 1
                L = s // B
                if more:
                    power(mv[:, :, 1], rstd[:, :], lnv_a, lnr_a, s + 2)
                e.wait_ge(ld_bp, 16 * (L + 1))
                e.wait_ge(gate_ready, s + 1)
                add_bias(s, b_p, gate[:, 0, :], ln_a, s + 1, xg1)
                if more:
                    self_parts(s + 1)
                if s == B:
                    key_parts(1)
                parts_until(s + 1, 0, AT["proj"][1], more)
                power_halves(4 * s)
                e.wait_ge(ld_w, NLD_W * (L + 1))
                add_bias(s, b_c, None, ln_b, 4 * s + 2, xg2)
                parts_until(s + 1, AT["proj"][1], AT["norm3"][0], more)
                power_halves(4 * s + 2)
                add_bias(s, b_2, gate[:, 1, :], ln_b, 4 * s + 4, xg3)
                parts_until(s + 1, AT["norm3"][0], TILES, more)

        @block.vector
        def _(e):
            n = [0]

            def link(ins):
                n[0] += 1
                ins.then_inc(c_dve, 1)
                e.wait_ge(c_dve, n[0])

            def statistics(src, vs, ts=range(TN)):
                for t in ts:
                    ins = e.bn_stats(stat[:, t, :], src[:, t, :])
                link(ins)
                for t in ts:
                    ins = e.bn_aggr(mv[:, t, :], stat[:, t, :])
                ins.then_inc(vs, 1)

            def normalise(src, dst, vs, rs, done, k, ts=range(TN)):
                e.wait_ge(vs, k)
                e.wait_ge(rs, k)
                for t in ts:
                    ins = e.tensor_scalar(dst[:, t, :], src[:, t, :], mv[:, t, 0:1], rstd[:, t:t + 1],
                                          ALU.subtract, ALU.mult)
                ins.then_inc(done, 1)

            def permute(dst, src):
                return e.tensor_copy(dst.rearrange("p (j d h) -> p j d h", d=HD, h=HC),
                                     src.rearrange("p (j h d) -> p j d h", d=HD, h=HC))

            def fill():
                e.memset(kst[ROWS:ROWS + 3, :, :], 1.0)
                e.memset(cqst[ROWS:ROWS + 4, :, :], 1.0)
                link(e.memset(ckst[ROWS:ROWS + 4, :, :], 1.0))
                e.wait_ge(ld_ctx, 32)
                e.tensor_scalar(ckst[ROWS:ROWS + 1, :, :],
                                mask8[ROWS:ROWS + 1, :].unsqueeze(1).broadcast_to([1, H, B * S]),
                                -3e38, 3e38, ALU.mult, ALU.mult).then_inc(fill_k, 1)

            def column_rows(L):
                e.wait_ge(ld_cols, NLD_COLS * (L + 1))
                permute(colpp[:, :], colp[:, :]).then_inc(colp_ready, 1)

            def modulation(L):
                e.wait_ge(cols_full, L + 1)
                e.tensor_copy(columns[:, L, :], MI[:, 256:256 + NCOL]).then_inc(c_dve, 1)
                n[0] += 1
                e.wait_ge(c_dve, n[0])
                e.tensor_scalar(colq[:, L, 0:2], cols[:, L, 0:2], SCALE, None, ALU.mult)
                e.tensor_scalar(colq[:, L, 2:4], cols[:, L, 4:6], SCALE, None, ALU.mult).then_inc(cols_ready, 1)
                e.wait_ge(ld_mod, NLD_MOD * (L + 1))
                e.wait_ge(mr_full, L + 1)
                e.tensor_copy(modr[:, 0:2 * D], A[0:B, 0, :])
                e.tensor_copy(modr[:, 2 * D:3 * D], A[0:B, 1, D:2 * D])
                e.tensor_copy(modr[:, 3 * D:4 * D], A[0:B, 2, 0:D])
                e.tensor_tensor(grow[:, L, 0, :], A[0:B, 1, 0:D], gb_m[:, 0, :], ALU.add)
                e.tensor_tensor(grow[:, L, 1, :], A[0:B, 2, D:2 * D], gb_m[:, 1, :], ALU.add).then_inc(mr_ready, 1)
                e.wait_ge(mc_full, L + 1)
                for i, m in enumerate((0, 6)):
                    ins = e.tensor_tensor(modc[:, L, 4 * i:4 * i + 4, :],
                                          MI[:, 16 * i:16 * i + 16].rearrange("p (j b) -> p j b", j=4),
                                          modb[:, L, m:m + 4].unsqueeze(2).broadcast_to([P, 4, B]), ALU.add)
                link(ins)
                for m in (SCALE_A, SCALE_M):
                    ins = e.tensor_scalar(modc[:, L, 2 * m:2 * m + 2, :], modc[:, L, 2 * m:2 * m + 2, :], 1.0, None, ALU.add)
                ins.then_inc(mc_ready, 1)

            def qk_weights(L):
                e.wait_ge(ld_qk, 16 * (L + 1))
                e.wait_ge(qk_full, 4 * B * L)
                for k in range(KC):
                    ins = permute(w_qk[:, k, :], stage[:, k, :])
                ins.then_inc(wqk_ready, 1)

            def cross_weights(L):
                e.wait_ge(ld_kv, NLD_KV * (L + 1))
                for k in range(KC):
                    permute(w_q[:, k, :], raw_q[L][:, k, :])
                    ins = permute(w_ck[:, k, :], w_kv[:, k, 0:D])
                ins.then_inc(wq_ready, 1)
                if L:
                    e.wait_ge(cst_full, NG * B * L)
                    e.memset(ckst[ROWS:ROWS + 1, :, :], 0.0).then_inc(fill_k, 1)

            def context_norm():
                e.wait_ge(ld_ctx, 32)
                for t in range(2):
                    ins = e.bn_stats(stat[:, t, :], cx[:, t, :])
                link(ins)
                for t in range(2):
                    ins = e.bn_aggr(cmv[:, t, :], stat[:, t, :])
                ins.then_inc(cxv, 1)
                e.wait_ge(cxv, 1)
                e.wait_ge(cxr, 1)
                for t in range(2):
                    ins = e.tensor_scalar(cxn[:, t, :], cx[:, t, :], cmv[:, t, 0:1], crstd[:, t:t + 1],
                                          ALU.subtract, ALU.mult)
                ins.then_inc(cxn_ready, 1)

            def context_columns():
                for L in range(2):
                    e.wait_ge(cxt_full, L + 1)
                    e.tensor_copy(cxT[:, L, :, :], OA[:, :].rearrange("p (k n) -> p k n", k=KC)).then_inc(cxt_ready, 1)

            def cross_values(L, banks):
                if L:
                    e.wait_ge(cav_done, NG * B * L)
                else:
                    e.wait_ge(fill_v, 1)
                for b in range(B):
                    e.wait_ge(kv_full, 2 * L + b // 2 + 1)
                    src = banks[:, b // 2, (b % 2) * D:(b % 2 + 1) * D].rearrange("p (i o d) -> p i o d", o=2, d=HD)
                    br = b_cv.rearrange("p (i o d) -> p i o d", o=2, d=HD)
                    e.tensor_tensor(cv[0:S, b, :, 0:HD], src[0:S, :, 0, :], br[0:S, :, 0, :], ALU.add)
                    ins = e.tensor_tensor(cv[S:P, b, :, 2 * HD:3 * HD], src[S:P, :, 1, :], br[S:P, :, 1, :], ALU.add)
                ins.then_inc(kv_ready, 1)

            def gates(s):
                e.wait_ge(gate_full, s + 1)
                e.tensor_copy(gate[:, :, :], R[:, 1, :].rearrange("p (g n) -> p g n", g=2)).then_inc(gate_ready, 1)

            def norm1(s):
                b = s % B
                if s == 0:
                    e.wait_ge(ld_x0, 16)
                elif s < B:
                    e.wait_ge(ld_x, 16)
                else:
                    e.wait_ge(x3, 2 * (s - B + 1))
                e.wait_ge(xta_full, KC * s)
                statistics(x[:, b, :, :], lnv_a)
                normalise(x[:, b, :, :], xn_a, lnv_a, lnr_a, ln_a, s + 1)

            def modulate1(s):
                b, L = s % B, s // B
                e.wait_ge(v_full, 2 * s)
                e.wait_ge(mc_ready, L + 1)
                for c in range(KC):
                    e.wait_ge(xta_full, KC * s + c + 1)
                    e.tensor_scalar(xt_a[:, c, :], R[:, c, :], modc[:, L, 2 * SCALE_A + c, b:b + 1],
                                    modc[:, L, 2 * SHIFT_A + c, b:b + 1], ALU.mult, ALU.add).then_inc(xta_ready, 1)

            def values(s):
                e.wait_ge(av_done, 16 * s)
                e.wait_ge(ld_v, NLD_V * (s // B + 1))
                for i in range(2):
                    e.wait_ge(v_full, 2 * s + i + 1)
                    e.tensor_tensor(vaug[:, 2 * i:2 * i + 2, :, 0:HD],
                                    R[:, i, :].rearrange("p (t h d) -> p t h d", t=2, h=H),
                                    b_v.rearrange("p (h d) -> p h d", h=H).unsqueeze(1).broadcast_to([P, 2, H, HD]),
                                    ALU.add).then_inc(v_ready, 1)

            def maxes(s, m0, m1):
                if s is None:
                    return
                if m0 == 0:
                    e.wait_ge(nmparts, NG * s)
                for m in range(m0, m1):
                    h, t = m // TN, m % TN
                    e.wait_ge(s_full, TILES * s + m + 1)
                    e.tensor_reduce(nmax[:, h // G, t, h % G:h % G + 1], R[:, m % 2, :], AX.X, ALU.max,
                                    negate=True).then_inc(s_max, 1)

            def unnormalised(s, g):
                e.wait_ge(av_done, 16 * s + 4 * (g + 1))
                if g >= 2:
                    e.wait_ge(ut_full, NG * s + g - 1)
                elif s:
                    e.wait_ge(cut_full, NG * s)
                e.tensor_copy(u[:, g % 2, :], OA[:, :]).then_inc(u_ready, 1)

            def out_norm(k, g, ut, on):
                e.wait_ge(ut, k + 1)
                m = MI[:, :].rearrange("p (t j d) -> p t j d", t=TN, j=G)
                link(e.reciprocal(rsum[:, :, :], m[:, :, :, HD]))
                dst = xn_b[:, :, HD * G * g:HD * G * (g + 1)].rearrange("p t (j d) -> p t j d", j=G)
                e.tensor_tensor(dst, m[:, :, :, 0:HD], rsum[:, :, :].unsqueeze(3).broadcast_to([P, TN, G, HD]),
                                ALU.mult).then_inc(on, 1)

            def residual(s, full, xg, xs, gate_row, banks, halves=(0, 1)):
                b = s % B
                e.wait_ge(xg, s + 1)
                for i in halves:
                    e.wait_ge(full, 2 * s + i + 1)
                    y = banks[:, i, :].rearrange("p (t n) -> p t n", t=2)
                    if gate_row is not None:
                        e.wait_ge(xs, 2 * s + i)
                        link(e.tensor_tensor(tmp[:, :, :], y, gate_row.unsqueeze(1).broadcast_to([P, 2, D]), ALU.mult))
                        y = tmp[:, :, :]
                    e.tensor_tensor(x[:, b, 2 * i:2 * i + 2, :], y, x[:, b, 2 * i:2 * i + 2, :], ALU.add).then_inc(xs, 1)

            def split(f, p0, p1, p2, done):
                link(e.tensor_copy(p0, f))
                link(e.tensor_tensor(f, f, p0, ALU.subtract))
                link(e.tensor_copy(p1, f))
                e.tensor_tensor(p2, f, p1, ALU.subtract).then_inc(done, 1)

            def cross_parts(s):
                e.wait_ge(cstack, 192 * s)
                e.wait_ge(ckstack, 192 * (s // B + 1))
                for c in range(KC):
                    e.wait_ge(cq_evac, KC * s + c + 1)
                    split(qf[:, c, :], cpart[:, 0, c, :], cpart[:, 1, c, :], cpart[:, 2, c, :], cparts)

            def cross_max(s, t0):
                e.wait_ge(cmrow_full, s)
                for t in (t0, t0 + 1):
                    e.wait_ge(cs_full, TN * s + t + 1)
                    i = 2 * (t % 2)
                    e.tensor_reduce(cnmax[:, t, :], A[:, i:i + 2, :].rearrange("p i (h n) -> p (i h) n", n=S),
                                    AX.X, ALU.max, negate=True).then_inc(cs_max, 1)

            def cross_max_parts(s):
                e.wait_ge(cs_max, TN * (s + 1))
                f = cnmax[:, :, :]
                link(e.tensor_copy(cmp_[:, :, 0, :], f))
                link(e.tensor_tensor(cnres[:, :, :], f, cmp_[:, :, 0, :], ALU.subtract))
                link(e.tensor_copy(cmp_[:, :, 1, :], cnres[:, :, :]))
                e.tensor_tensor(cmp_[:, :, 2, :], cnres[:, :, :], cmp_[:, :, 1, :], ALU.subtract).then_inc(cnmparts, 1)

            norm1(0)
            column_rows(0)
            e.wait_ge(csT_full, 1)
            e.tensor_copy(csT[:, :, :], MI[:, 0:KC * B].rearrange("p (k b) -> p k b", k=KC)).then_inc(csT_ready, 1)
            context_norm()
            qk_weights(0)
            modulation(0)
            modulate1(0)
            fill()
            context_columns()
            cross_weights(0)
            values(0)
            cross_values(0, A[:, 0:2, :])
            column_rows(1)
            modulation(1)
            maxes(0, 0, TILES)
            for s in range(2 * B):
                b = s % B
                nxt = s + 1 if s < 2 * B - 1 else None
                gates(s)
                if s == B - 1:
                    qk_weights(1)
                if nxt is not None:
                    norm1(nxt)
                    modulate1(nxt)
                e.wait_ge(xtc_full, KC * s)
                for g in range(NG):
                    unnormalised(s, g)
                    if s == B and g == 1:
                        cross_weights(1)
                    if s == B and g == 2:
                        cross_values(1, R)
                    if g == NG - 2:
                        maxes(nxt, *AT["unit13"])
                    out_norm(NG * s + g, g, ut_full, on_ready)
                    if g == NG - 2:
                        maxes(nxt, AT["unit14"][0], AT["unit15"][1])
                maxes(nxt, *AT["proj"])
                residual(s, pj_full, xg1, x1, gate[:, 0, :], A[:, 2:4, :], (0,))
                e.wait_ge(x1, 2 * s + 1)
                statistics(x[:, b, :, :], lnv_b, (0, 1))
                residual(s, pj_full, xg1, x1, gate[:, 0, :], A[:, 2:4, :], (1,))
                e.wait_ge(ot_full, 2 * (s + 1))
                normalise(x[:, b, :, :], xn_b, lnv_b, lnr_b, ln_b, 4 * s + 1, (0, 1))
                e.wait_ge(x1, 2 * (s + 1))
                statistics(x[:, b, :, :], lnv_b, (2, 3))
                maxes(nxt, *AT["norm2"])
                normalise(x[:, b, :, :], xn_b, lnv_b, lnr_b, ln_b, 4 * s + 2, (2, 3))
                maxes(nxt, *AT["halfq"])
                cross_parts(s)
                if nxt is not None:
                    values(nxt)
                maxes(nxt, *AT["stack"])
                cross_max(s, 0)
                maxes(nxt, *AT["cross2"])
                cross_max(s, 2)
                cross_max_parts(s)
                maxes(nxt, AT["cmrow"][0], AT["crows"][1])
                e.wait_ge(xtb_full, 2 * (s + 1))
                for g in range(NG):
                    maxes(nxt, *AT[f"g{g}"])
                    out_norm(NG * s + g, g, cut_full, con_ready)
                residual(s, cpj_full, xg2, x2, None, A[:, 2:4, :], (0,))
                e.wait_ge(x2, 2 * s + 1)
                statistics(x[:, b, :, :], lnv_b, (0, 1))
                residual(s, cpj_full, xg2, x2, None, A[:, 2:4, :], (1,))
                e.wait_ge(cot_full, 2 * (s + 1))
                normalise(x[:, b, :, :], xn_b, lnv_b, lnr_b, ln_b, 4 * s + 3, (0, 1))
                e.wait_ge(x2, 2 * (s + 1))
                statistics(x[:, b, :, :], lnv_b, (2, 3))
                maxes(nxt, *AT["norm3"])
                normalise(x[:, b, :, :], xn_b, lnv_b, lnr_b, ln_b, 4 * s + 4, (2, 3))
                maxes(nxt, AT["halfm"][0], AT["o1"][1])
                residual(s, mo_full, xg3, x3, gate[:, 1, :], A[:, 0:2, :], (0,))
                maxes(nxt, AT["o2"][0], TILES)
                residual(s, mo_full, xg3, x3, gate[:, 1, :], A[:, 0:2, :], (1,))

        @block.scalar
        def _(e):
            def cross_keys(L, banks):
                e.wait_ge(cols_ready, L + 1)
                for c in range(KC):
                    e.wait_ge(ck_full, KC * L + c + 1)
                    e.activation(ckf[L][:, c, :], banks[:, c, 0:B * S], ACT.Identity,
                                 bias=cols[:, L, 6 + c:7 + c]).then_inc(ck_ready, 1)

            def qk(s, i):
                j, L = QK_ORDER[i], s // B
                if i == 0:
                    e.wait_ge(cols_ready, L + 1)
                    if s > 1:
                        e.wait_ge(cparts, KC * (s - 1))
                e.wait_ge(qk_full, 4 * s + i + 1)
                if i >= 2:
                    e.wait_ge(parts, 4 * s + i - 1)
                if j < 2:
                    ins = e.activation(qf[:, i % 2, :], R[:, i % 2, :], ACT.Identity, bias=colq[:, L, j:j + 1], scale=SCALE)
                else:
                    ins = e.activation(qf[:, i % 2, :], R[:, i % 2, :], ACT.Identity, bias=cols[:, L, j:j + 1])
                ins.then_inc(qk_evac, 1)

            def row_in(s, step):
                for g in range(NG - 1):
                    m0, m1 = AT[step]
                    if s is not None and m0 <= TILES // NG * (g + 1) + MROW_LAG < m1:
                        row(s, g)

            def row(s, g):
                k = NG * s + g
                e.wait_ge(mrow_full, k + 1)
                if k >= 2:
                    e.wait_ge(mrd[(k - 2) % NG], 16 * ((k - 2) // NG + 1))
                e.copy(mrow[:, g % 2, :], R[0:3 * G, 0, :]).then_inc(mrow_ready, 1)

            def exps(s, n):
                if n == 0:
                    e.wait_ge(mo_full, 2 * s)
                    if s == 0:
                        e.wait_ge(mr_full, 2)
                        e.wait_ge(ckparts, KC)
                        e.wait_ge(wq_ready, 1)
                for m in (2 * n, 2 * n + 1):
                    e.wait_ge(st_full, 32 * s + m + 1)
                    if m >= 4:
                        e.wait_ge(av_done, 16 * s + (m - 4) // 2 + 1)
                    e.activation(big[:, m % 4, :, :], A[:, 2 - 2 * (m % 2):4 - 2 * (m % 2), :], ACT.Exp).then_inc(exp_done, 1)

            def copies(full, k, ready, free, fk):
                e.wait_ge(free, fk)
                for i in range(2):
                    h = slice(i * N // 2, (i + 1) * N // 2)
                    e.wait_ge(full, k + i + 1)
                    e.copy(xt_b[:, :, h], A[:, i, :].rearrange("p (c n) -> p c n", c=KC)).then_inc(ready, 1)

            def modulated(s, nxt):
                e.wait_ge(cpj_full, 2 * (s + 1))
                for i in range(2):
                    h = slice(i * N // 2, (i + 1) * N // 2)
                    e.wait_ge(xtc_full, 2 * s + i + 1)
                    for c in range(KC):
                        ins = e.activation(xt_b[:, c, h], A[:, i, c * N // 2:(c + 1) * N // 2], ACT.Identity,
                                           bias=modc[:, s // B, 2 * SHIFT_M + c, s % B:s % B + 1],
                                           scale=modc[:, s // B, 2 * SCALE_M + c, s % B:s % B + 1])
                    ins.then_inc(xtc_ready, 1)
                    if i == 0:
                        row_in(nxt, "halfm")

            def cross_q(s, nxt):
                e.wait_ge(parts, 4 * (s + 1 if nxt is None else nxt + 1))
                for c in range(KC):
                    e.wait_ge(cq_full, KC * s + c + 1)
                    e.activation(qf[:, c, :], A[:, 2 + c, :], ACT.Identity, bias=colq[:, s // B, 2 + c:3 + c],
                                 scale=SCALE).then_inc(cq_evac, 1)

            def cross(s, nxt):
                e.wait_ge(cmrow_full, s + 1)
                e.wait_ge(cmrd, 16 * s)
                e.copy(cmrow[:, :], MI[0:3 * H, :]).then_inc(cmrow_ready, 1)
                row_in(nxt, "crows")
                e.wait_ge(av_done, 16 * (s + 1))
                e.wait_ge(ut_full, NG * (s + 1))
                for g in range(NG + 1):
                    if g < NG:
                        e.wait_ge(cst_full, NG * s + g + 1)
                        i = 2 * (g % 2)
                        e.activation(big[:, g, :, :], A[:, i:i + 2, :], ACT.Exp).then_inc(cexp_done, 1)
                    if g:
                        e.wait_ge(cav_done, NG * s + g)
                        if g > 2:
                            e.wait_ge(cut_full, NG * s + g - 2)
                        e.copy(u[:, (g - 1) % 2, :], OA[:, :]).then_inc(cu_ready, 1)
                        row_in(nxt, f"g{g - 1}")

            def gelu(s, nxt):
                e.wait_ge(cav_done, NG * (s + 1))
                for m in range(MC):
                    e.wait_ge(h_full, MC * s + m + 1)
                    e.activation(hid[:, m, :], A[:, (m + 2) % 4, :], GELU[s // B], bias=col1[:, s // B, m:m + 1]).then_inc(h_ready, 1)
                    if m >= 4:
                        row_in(nxt, f"h{m}")

            e.wait_ge(ld_cond, 16)
            e.activation(cs[:, :], cond[:, :], ACT.Silu).then_inc(silu, 1)
            for i in range(4):
                qk(0, i)
            cross_keys(0, A[:, 2:4, :])
            for g in range(NG - 1):
                row(0, g)
            for s in range(2 * B):
                nxt = s + 1 if s < 2 * B - 1 else None
                for n in range(16):
                    exps(s, n)
                    if s == B and n == 13:
                        cross_keys(1, R)
                    if n == 1:
                        row(s, NG - 1)
                    if nxt is not None and n in QK_AT:
                        qk(nxt, QK_AT.index(n))
                copies(ot_full, 2 * s, ot_ready, h_full, MC * s)
                copies(xtb_full, 2 * s, xtb_ready, pj_full, 2 * (s + 1))
                cross_q(s, nxt)
                row_in(nxt, "stack")
                row_in(nxt, "cross2")
                row_in(nxt, "cmrow")
                cross(s, nxt)
                copies(cot_full, 2 * s, cot_ready, cq_full, KC * (s + 1))
                row_in(nxt, "norm3")
                modulated(s, nxt)
                gelu(s, nxt)
                for t in range(TN):
                    row_in(nxt, f"o{t}")

        @block.tensor
        def _(e):
            def mm(o, l, r, start=True, stop=True):
                return e.matmul(o, l, r, start=start, stop=stop, skip_group_check=True)

            def condition():
                e.wait_ge(silu, 1)
                e.wait_ge(idents, 1)
                for k in range(KC):
                    ins = e.transpose(MI[:, k * B:(k + 1) * B], cs[:, k * P:(k + 1) * P], ident[0:B, 0:B])
                ins.then_inc(csT_full, 1)

            def modulation(L):
                if L:
                    e.wait_ge(mc_ready, L)
                    e.wait_ge(kv_ready, 1)
                    e.wait_ge(ck_ready, KC)
                else:
                    e.wait_ge(csT_ready, 1)
                e.wait_ge(ld_cols, NLD_COLS * (L + 1))
                e.wait_ge(colp_ready, L + 1)
                e.transpose(MI[:, 256:256 + 12 + MC], colr[:, :], ident[0:12 + MC, 0:12 + MC])
                e.transpose(MI[:, 268 + MC:276 + MC], colpp[:, :], ident[0:8, 0:8]).then_inc(cols_full, 1)
                e.wait_ge(ld_mod, NLD_MOD * (L + 1))
                for j in range(3):
                    for k in range(KC):
                        ins = mm(A[0:B, j, :], csT[:, k, :], w_mod[:, k, 2 * j * D:2 * (j + 1) * D], k == 0, k == KC - 1)
                ins.then_inc(mr_full, 1)
                e.wait_ge(mr_ready, L + 1)
                e.wait_ge(cols_ready, L + 1)
                for j in range(8):
                    ins = e.transpose(MI[:, j * B:(j + 1) * B], modr[:, j * P:(j + 1) * P], ident[0:B, 0:B])
                ins.then_inc(mc_full, 1)

            def context():
                for L, src in enumerate((cx, cxn)):
                    if L:
                        e.wait_ge(cxn_ready, 1)
                        e.wait_ge(cxt_ready, 1)
                    else:
                        e.wait_ge(ld_ctx, 32)
                    for k in range(KC):
                        for i in range(2):
                            o = k * B * S + i * P
                            ins = e.transpose(OA[:, o:o + P], src[:, i, k * P:(k + 1) * P], ident[:, :])
                    ins.then_inc(cxt_full, 1)

            def cross_values(L, banks):
                e.wait_ge(cxt_ready, 2)
                e.wait_ge(ld_kv, NLD_KV * (L + 1))
                for b in range(B):
                    for o in (0, S):
                        for k in range(KC):
                            ins = mm(banks[o:o + S, b // 2, (b % 2) * D:(b % 2 + 1) * D],
                                     cxT[:, L, k, b * S:(b + 1) * S], w_kv[:, k, D:2 * D], k == 0, k == KC - 1)
                    if b % 2:
                        ins.then_inc(kv_full, 1)

            def cross_keys(L, banks):
                e.wait_ge(wq_ready, L + 1)
                if L:
                    e.wait_ge(kv_ready, L + 1)
                for c in range(KC):
                    for k in range(KC):
                        ins = mm(banks[:, c, 0:B * S], w_ck[:, k, c * P:(c + 1) * P], cxT[:, L, k, :],
                                 k == 0, k == KC - 1)
                    ins.then_inc(ck_full, 1)

            def gates(s):
                e.wait_ge(mr_ready, s // B + 1)
                e.wait_ge(s_max, TILES * (s + 1))
                e.wait_ge(x3, 2 * s)
                b, L = s % B, s // B
                mm(R[:, 1, :], ident[0:B, b:b + 1].broadcast_to([B, P]),
                   grow[:, L, :, :].rearrange("p g n -> p (g n)")).then_inc(gate_full, 1)

            def transposes(src, dst, full):
                for c in range(KC):
                    for t in range(TN):
                        ins = e.transpose(dst[:, c, t * P:(t + 1) * P], src[:, t, c * P:(c + 1) * P], ident[:, :])
                    ins.then_inc(full, 1)

            def transpose_half(src, i, full):
                for c in range(KC):
                    for t in (2 * i, 2 * i + 1):
                        o = c * N // 2 + (t % 2) * P
                        ins = e.transpose(A[:, i, o:o + P], src[:, t, c * P:(c + 1) * P], ident[:, :])
                ins.then_inc(full, 1)

            def rows_out(src, w, dst, full, kc, ready=None, target=0):
                for i in range(2):
                    if ready is not None:
                        e.wait_ge(ready, target + i + 1)
                    for t in (2 * i, 2 * i + 1):
                        for k in range(kc):
                            ins = mm(dst[:, i, (t % 2) * D:(t % 2 + 1) * D], src[:, k, t * P:(t + 1) * P], w[:, k, :],
                                     k == 0, k == kc - 1)
                    ins.then_inc(full, 1)

            def norm_rows(s):
                e.wait_ge(ln_a, s + 1)
                e.wait_ge(s_max, TILES * s)
                e.wait_ge(mrow_ready, NG * s)
                e.wait_ge(gate_ready, s)
                transposes(xn_a, R, xta_full)

            def qk(s, i):
                e.wait_ge(xta_ready, KC * (s + 1))
                e.wait_ge(wqk_ready, s // B + 1)
                if i >= 2:
                    e.wait_ge(qk_evac, 4 * s + i - 1)
                for k in range(KC):
                    ins = mm(R[:, i % 2, :], w_qk[:, k, QK_ORDER[i] * P:(QK_ORDER[i] + 1) * P], xt_a[:, k, :],
                             k == 0, k == KC - 1)
                ins.then_inc(qk_full, 1)

            def values(s):
                e.wait_ge(qk_evac, 4 * (s + 1))
                e.wait_ge(ld_v, NLD_V * (s // B + 1))
                if s:
                    e.wait_ge(s_max, TILES * s + AT["stack"][0])
                rows_out(xt_a, w_v, R, v_full, KC)

            def scores_rows(s, m0, m1):
                if s is None:
                    return
                if m0 == 0:
                    e.wait_ge(qk_evac, 4 * (s + 1))
                    if s == B + 1:
                        e.wait_ge(ck_ready, 2 * KC)
                if m0 == (AT["stack"][0] if s else 0):
                    e.wait_ge(v_ready, 2 * (s + 1))
                for m in range(m0, m1):
                    h, t = m // TN, m % TN
                    if m % (TILES // KC) == 0:
                        e.wait_ge(stack[h // HC], 192 * (s + 1))
                    if m >= 2:
                        e.wait_ge(s_max, TILES * s + m - 1)
                    if m % 16 == MROW_LAG and m > 16:
                        max_row(s, m // 16 - 1)
                        e.wait_ge(mrow_ready, NG * s + m // 16)
                    mm(R[:, m % 2, :], qst[0:ROWS, h, t * P:(t + 1) * P], kst[0:ROWS, h, :]).then_inc(s_full, 1)

            def max_row(s, g):
                if g == NG - 1:
                    e.wait_ge(s_max, TILES * (s + 1))
                e.wait_ge(nmparts, NG * s + g + 1)
                for t in range(TN):
                    ins = mm(R[0:3 * G, 0, t * P:(t + 1) * P], mp[:, g, t, :, :].rearrange("p a b -> p (a b)"), identb[:, :])
                ins.then_inc(mrow_full, 1)

            def un_transpose(k, g, ur, ut, free):
                e.wait_ge(ur, k + 1)
                for f, v in free:
                    e.wait_ge(f, v)
                for t in range(TN):
                    ins = e.transpose(MI[:, t * P:(t + 1) * P], u[:, g % 2, t * P:(t + 1) * P], ident[:, :])
                ins.then_inc(ut, 1)

            def attend(s, nxt):
                def st(g, kc):
                    for i in range(2):
                        m = 32 * s + 2 * (4 * g + kc) + i
                        if m % 32 >= 2:
                            e.wait_ge(exp_done, m - 1)
                        elif m % 32 == 1:
                            e.wait_ge(x3, 2 * s)
                        for j in (2 * i, 2 * i + 1):
                            h = G * g + j
                            ins = mm(A[:, (j + 2) % 4, :], kst[0:ROWS + 3, h, kc * P:(kc + 1) * P], qst[0:ROWS + 3, h, :])
                        ins.then_inc(st_full, 1)

                def av(g, kc):
                    e.wait_ge(exp_done, 32 * s + 2 * (4 * g + kc) + 2)
                    if kc == 0:
                        if g:
                            e.wait_ge(u_ready, NG * s + g)
                        else:
                            e.wait_ge(cu_ready, NG * s)
                    for j in range(G):
                        ins = mm(OA[32 * j:32 * j + 32, :], vaug[:, kc, G * g + j, :], big[:, 2 * (kc % 2) + j // 2, j % 2, :],
                                 kc == 0, kc == TN - 1)
                    ins.then_inc(av_done, 1)

                last = None
                for g in range(NG):
                    for kc in range(TN):
                        if kc == 0:
                            e.wait_ge(mrd[g], 16 * (s + 1))
                        st(g, kc)
                        n = TN * g + kc
                        if n == 0:
                            gates(s)
                        if n == 1:
                            max_row(s, NG - 1)
                        if s == B and n == 12:
                            cross_values(1, R)
                        if s == B and n == 13:
                            cross_keys(1, R)
                        if nxt is not None and n == QK_AT[0] - 2:
                            norm_rows(nxt)
                        if nxt is not None and n in QK_AT:
                            qk(nxt, QK_AT.index(n))
                        if last:
                            av(*last)
                        if kc == 2 and g:
                            un_transpose(NG * s + g - 1, g - 1, u_ready, ut_full,
                                         [(on_ready, NG * s + g - 1)] if g > 1 else [(con_ready, NG * s), (mc_ready, 2)])
                        if n >= 13:
                            scores_rows(nxt, *AT[f"unit{n}"])
                        last = (g, kc)
                av(*last)
                un_transpose(NG * s + NG - 1, NG - 1, u_ready, ut_full, [(on_ready, NG * s + NG - 1)])

            def post_self(s, nxt):
                e.wait_ge(on_ready, NG * (s + 1))
                e.wait_ge(exp_done, 32 * (s + 1))
                for i in range(2):
                    transpose_half(xn_b, i, ot_full)
                scores_rows(nxt, *AT["proj"])
                e.wait_ge(ld_w, NLD_W * (s // B + 1))
                rows_out(xt_b, w_p, A[:, 2:4, :], pj_full, KC, ot_ready, 2 * s)

            def cross(s, nxt):
                b = s % B
                scores_rows(nxt, *AT["norm2"])
                for i in range(2):
                    e.wait_ge(ln_b, 4 * s + i + 1)
                    transpose_half(xn_b, i, xtb_full)
                    if i == 0:
                        scores_rows(nxt, *AT["halfq"])
                    e.wait_ge(xtb_ready, 2 * s + i + 1)
                    e.wait_ge(x1, 2 * (s + 1))
                    h = slice(i * N // 2, (i + 1) * N // 2)
                    for c in range(KC):
                        for k in range(KC):
                            ins = mm(A[:, 2 + c, h], w_q[:, k, c * P:(c + 1) * P], xt_b[:, k, h], k == 0, k == KC - 1)
                        if i:
                            ins.then_inc(cq_full, 1)
                if nxt is not None:
                    values(nxt)
                scores_rows(nxt, *AT["stack"])
                e.wait_ge(cstack, 192 * (s + 1))
                e.wait_ge(cq_evac, KC * (s + 1))
                e.wait_ge(ckstack, 192 * (s // B + 1))
                e.wait_ge(fill_k, 1 + s // B)
                for t in range(TN):
                    if t == 2:
                        scores_rows(nxt, *AT["cross2"])
                    if t >= 2:
                        e.wait_ge(cs_max, TN * s + t - 1)
                    for h in range(H):
                        ins = mm(A[:, 2 * (t % 2) + h // HC, (h % HC) * S:(h % HC + 1) * S],
                                 cqst[0:ROWS + 1, h, t * P:(t + 1) * P], ckst[0:ROWS + 1, h, b * S:(b + 1) * S])
                    ins.then_inc(cs_full, 1)
                scores_rows(nxt, *AT["cmrow"])
                e.wait_ge(cnmparts, s + 1)
                e.wait_ge(on_ready, NG * (s + 1))
                for t in range(TN):
                    ins = mm(MI[0:3 * H, t * P:(t + 1) * P], cmp_[:, t, :, :].rearrange("p a b -> p (a b)"), identb[:, :])
                ins.then_inc(cmrow_full, 1)
                scores_rows(nxt, *AT["crows"])
                e.wait_ge(cmrd, 16 * (s + 1))
                e.wait_ge(cs_max, TN * (s + 1))

                def st(g):
                    if g >= 2:
                        e.wait_ge(cexp_done, NG * s + g - 1)
                    for j in range(G):
                        o = S * (j % 2)
                        ins = mm(A[o:o + S, 2 * (g % 2) + j // 2, :], ckst[:, G * g + j, b * S:(b + 1) * S], cqst[:, G * g + j, :])
                    ins.then_inc(cst_full, 1)

                def av(g):
                    e.wait_ge(cexp_done, NG * s + g + 1)
                    if g:
                        e.wait_ge(cu_ready, NG * s + g)
                    else:
                        e.wait_ge(u_ready, NG * (s + 1))
                    for i in range(2):
                        ins = mm(OA[S * i:S * (i + 1), :], cv[:, b, 2 * g + i, :], big[:, g, i, :])
                    ins.then_inc(cav_done, 1)

                st(0)
                for g in range(NG):
                    if g + 1 < NG:
                        st(g + 1)
                    av(g)
                    scores_rows(nxt, *AT[f"g{g}"])
                    un_transpose(NG * s + g, g, cu_ready, cut_full,
                                 [(con_ready, NG * s + g)] if g else [(cmrow_ready, s + 1)])
                e.wait_ge(con_ready, NG * (s + 1))
                e.wait_ge(cexp_done, NG * (s + 1))
                for i in range(2):
                    transpose_half(xn_b, i, cot_full)
                rows_out(xt_b, w_c, A[:, 2:4, :], cpj_full, KC, cot_ready, 2 * s)
                scores_rows(nxt, *AT["norm3"])

            def mlp(s, nxt):
                for i in range(2):
                    e.wait_ge(ln_b, 4 * s + i + 3)
                    transpose_half(xn_b, i, xtc_full)
                    if i == 0:
                        scores_rows(nxt, *AT["halfm"])
                    e.wait_ge(xtc_ready, 2 * s + i + 1)
                    e.wait_ge(x2, 2 * (s + 1))
                    h = slice(i * N // 2, (i + 1) * N // 2)
                    for m in range(3):
                        for k in range(KC):
                            ins = mm(A[:, (m + 2) % 4, h], w_1[:, k, m * P:(m + 1) * P], xt_b[:, k, h],
                                     k == 0, k == KC - 1)
                        if i:
                            ins.then_inc(h_full, 1)
                for m in range(3, MC):
                    if m > 3:
                        e.wait_ge(h_ready, MC * s + m - 3)
                    for k in range(KC):
                        ins = mm(A[:, (m + 2) % 4, :], w_1[:, k, m * P:(m + 1) * P], xt_b[:, k, :], k == 0, k == KC - 1)
                    ins.then_inc(h_full, 1)
                    if m > 3:
                        scores_rows(nxt, *AT[f"h{m}"])
                e.wait_ge(h_ready, MC * (s + 1))
                for t in range(TN):
                    for k in range(MC):
                        ins = mm(A[:, t // 2, (t % 2) * D:(t % 2 + 1) * D], hid[:, k, t * P:(t + 1) * P], w_2[:, k, :],
                                 k == 0, k == MC - 1)
                    if t % 2:
                        ins.then_inc(mo_full, 1)
                    scores_rows(nxt, *AT[f"o{t}"])

            condition()
            modulation(0)
            norm_rows(0)
            for i in range(4):
                qk(0, i)
            context()
            values(0)
            cross_values(0, A[:, 0:2, :])
            cross_keys(0, A[:, 2:4, :])
            modulation(1)
            scores_rows(0, 0, TILES)
            for s in range(2 * B):
                nxt = s + 1 if s < 2 * B - 1 else None
                attend(s, nxt)
                post_self(s, nxt)
                cross(s, nxt)
                mlp(s, nxt)


_INS = ["x", "cond_1024", "ctx_1024", "mask_BxS2_bf0"] + [n for layer in LAYER for n in layer.values()]


def kernel(**inputs):
    import numpy as _np
    import concourse.bacc as _bacc
    from concourse import mybir as _mybir
    from concourse.bass_utils import run_bass_kernel_spmd as _run

    nc = _bacc.Bacc("TRN2", target_bir_lowering=False, num_devices=1)
    arrays, args = {}, {}
    for name in _INS:
        v = _np.ascontiguousarray(inputs[name])
        arrays[f"in_{name}_dram"] = v
        args[name] = nc.dram_tensor(f"in_{name}_dram", v.shape, _mybir.dt.from_np(v.dtype), kind="ExternalInput").ap()
    o = nc.dram_tensor("out_0_dram", (B, N, D), _mybir.dt.float32, kind="ExternalOutput").ap()
    build(nc, args, o)
    r = _run(nc, [arrays], core_ids=[0])
    return r.results[0]["out_0_dram"]
```

```python
from contextlib import ExitStack

import concourse.bass as bass
from concourse import mybir

ALU = mybir.AluOpType
ACT = mybir.ActivationFunctionType
AX = mybir.AxisListType
F32 = mybir.dt.float32
BF16 = mybir.dt.bfloat16
U8 = mybir.dt.uint8

P = 128
B, N, D = 4, 512, 256
H, HD = 16, 16
S = 64
DF = 4 * D
TN = N // P
KC = D // P
MC = DF // P
G = 4
NG = H // G
HC = H // KC
EPS = 1e-6
SCALE = float(HD) ** -0.5
MASKED = -1e30
Q_TERMS = (0, 0, 1, 1, 0, 2)
K_TERMS = (0, 1, 0, 1, 2, 0)
ROWS = HD * len(Q_TERMS)
QK_ORDER = (0, 2, 1, 3)
TILES = H * TN
MROW_LAG = 4
TILES_OF = dict(unit13=1, unit14=2, unit15=2, av=1, ot=0, proj=2, pa=3, va=0, norm2=1, halfq=0, cqa=3, cqb=2, q0=2, q1=2, stack=4, half=2, cross2=2, cmrow=1, crows=2, g0=2, g1=3, g2=1, g3=0, cot=0, ca=1, norm3=1, vb=1, halfm=1, ha=3, hb=3, h3=2, h4=1, h5=1, h6=1, h7=1, o0=3, o1=2, o2=3, o3=2)
AT, _m = {}, 0
for _step, _n in TILES_OF.items():
    AT[_step], _m = (_m, _m + _n), _m + _n
assert _m == TILES
START = (26, 32)
ROW_TILE = [TILES // NG * (g + 1) + MROW_LAG for g in range(NG - 1)]
ROW_TILE = [AT["ca"][0] if AT["g0"][0] <= m < AT["ca"][0] else m for m in ROW_TILE]
QK_AT = (4, 6, 8, 10)

LAYER = [
    dict(mod_w="L0_xcond_ada_w", mod_b="L0_xcond_ada_b", qkv_w="L0_xcond_qkv_w", qkv_b="L0_xcond_qkv_b",
         p_w="L0_xcond_sa_proj_w", p_b="L0_xcond_sa_proj_b", q_w="L0_xcond_q_w", q_b="L0_xcond_q_b",
         kv_w="L0_xcond_kv_w", kv_b="L0_xcond_kv_b", c_w="L0_xcond_ca_proj_w", c_b="L0_xcond_ca_proj_b",
         w1="L0_xcond_fc1_w", b1="L0_xcond_fc1_b", w2="L0_xcond_fc2_w", b2="L0_xcond_fc2_b"),
    dict(mod_w="L1_xcond_W_mod", mod_b="L1_xcond_b_mod", qkv_w="L1_xcond_W_qkv", qkv_b="L1_xcond_b_qkv",
         p_w="L1_xcond_W_proj", p_b="L1_xcond_b_proj", q_w="L1_xcond_W_qc", q_b="L1_xcond_b_qc",
         kv_w="L1_xcond_W_kvc", kv_b="L1_xcond_b_kvc", c_w="L1_xcond_W_cproj", c_b="L1_xcond_b_cproj",
         w1="L1_xcond_W_mlp1", b1="L1_xcond_b_mlp1", w2="L1_xcond_W_mlp2", b2="L1_xcond_b_mlp2"),
]
GELU = [ACT.Gelu, ACT.Gelu_apprx_tanh]
GATE_A, GATE_M = 2, 5
SHIFT_A, SCALE_A, SHIFT_M, SCALE_M = range(4)


def build(nc, a, out):
    ctx = ExitStack()
    with ctx:
        def sb(name, shape, dt=F32):
            t = ctx.enter_context(nc.sbuf_tensor(name, shape, dt))
            return t[tuple(slice(None) for _ in shape)]

        def sem(name):
            return ctx.enter_context(nc.semaphore(name))

        w_qk = sb("w_qk", [P, KC, 2 * D])
        w_v = sb("w_v", [P, KC, D])
        w_p = sb("w_p", [P, KC, D])
        w_q = sb("w_q", [P, KC, D])
        w_c = sb("w_c", [P, KC, D])
        w_1 = sb("w_1", [P, KC, DF])
        w_2 = sb("w_2", [P, MC, D])
        rows = sb("rows", [P, 5, D])
        b_v, b_p, b_c, b_2, b_cv = (rows[:, i, :] for i in range(5))
        colr = sb("colr", [12 + MC, P])
        colp = sb("colp", [8, P])
        colpp = sb("colpp", [8, P])
        NCOL = 12 + MC + 8
        columns = sb("columns", [P, 2, NCOL])
        modb = columns[:, :, 0:12]
        col1 = columns[:, :, 12:12 + MC]
        cols = columns[:, :, 12 + MC:]
        colq = sb("colq", [P, 2, 4])
        modc = sb("modc", [P, 2, 8, B])
        gate = sb("gate", [P, 2, D])
        grow = sb("grow", [B, 2, 2, D])
        gb_m = sb("gb_m", [B, 2, D])
        gbt = sb("gbt", [P, D])
        x = sb("x", [P, B, TN, D])
        xn_a = sb("xn_a", [P, TN, D])
        xt_a = sb("xt_a", [P, KC, N])
        xn_b = sb("xn_b", [P, TN, D])
        xt_b = sb("xt_b", [P, KC, N])
        qst = sb("qst", [ROWS + 3, H, N], BF16)
        kst = sb("kst", [ROWS + 3, H, N], BF16)
        cqst = sb("cqst", [ROWS + 4, H, N], BF16)
        ckst = sb("ckst", [ROWS + 4, H, B * S], BF16)
        vaug = sb("vaug", [P, TN, H, 2 * HD])
        cv = sb("cv", [P, B, H // 2, 4 * HD])
        big = sb("big", [P, 4, 2, N])
        hid = big[:, :, :, :].rearrange("p a b n -> p (a b) n")
        qf = sb("qf", [P, 2, N])
        part = sb("part", [P, 3, 4, N], BF16)
        cpart = sb("cpart", [P, 3, 2, N], BF16)
        u = sb("u", [P, 2, N])
        tmp = sb("tmp", [P, 2, D])
        nmax = sb("nmax", [P, NG, TN, G])
        nres = sb("nres", [P, TN, G])
        mp = sb("mp", [P, NG, TN, 3, G], BF16)
        mrow = sb("mrow", [3 * G, 2, N], BF16)
        cnmax = sb("cnmax", [P, TN, H])
        cnres = sb("cnres", [P, TN, H])
        cmp_ = sb("cmp", [P, TN, 3, H], BF16)
        cmrow = sb("cmrow", [3 * H, N], BF16)
        stat = sb("stat", [P, TN, 6])
        mv = sb("mv", [P, TN, 2])
        rstd = sb("rstd", [P, TN])
        half = sb("half", [P, TN])
        warm = sb("warm", [1, 1])
        rsum = sb("rsum", [P, TN, G])
        ident = sb("ident", [P, P])
        identb = sb("identb", [P, P], BF16)
        cond = sb("cond", [B, D])
        cs = gbt[0:B, :]
        csT = sb("csT", [P, KC, B])
        stage = sb("stage", [P, KC, 2 * D])
        cxT = sb("cxT", [P, 2, KC, B * S])
        cmv = sb("cmv", [P, 2, 2])
        crstd = sb("crstd", [P, 2])
        mask8 = sb("mask8", [ROWS + 1, B * S], U8)
        w_mod = big[:, 0:3, :, :].rearrange("p a b n -> p (a b n)").rearrange("p (k n) -> p k n", k=KC)
        modr = xn_b.rearrange("p t d -> p (t d)")[0:B, :]
        w_kv = xt_b
        w_ck = tmp
        w_pg = tmp
        raw_q = (big[:, 3, 0, :].rearrange("p (k n) -> p k n", k=KC), stage[:, 0, :].rearrange("p (k n) -> p k n", k=KC))
        ckf = (big[:, 3, 1, :].rearrange("p (k n) -> p k n", k=KC), stage[:, 1, :].rearrange("p (k n) -> p k n", k=KC))
        cx = u[:, 0, :].rearrange("p (k n) -> p k n", k=2)
        cxn = u[:, 1, :].rearrange("p (k n) -> p k n", k=2)

        A = ctx.enter_context(nc.psum_tensor("A", [P, 4, 512], F32))
        R = ctx.enter_context(nc.psum_tensor("R", [P, 2, 512], F32))
        OA = ctx.enter_context(nc.psum_tensor("OA", [P, 512], F32))
        MI = ctx.enter_context(nc.psum_tensor("MI", [P, 512], F32))

        idents = sem("idents")
        fill_v = sem("fill_v")
        ones_ready = sem("ones_ready")
        mask_ready = sem("mask_ready")
        fill_k = sem("fill_k")
        c_pool = sem("c_pool")
        c_dve = sem("c_dve")
        ld_x0 = sem("ld_x0")
        ld_x = sem("ld_x")
        ld_cond = sem("ld_cond")
        ld_ctx = sem("ld_ctx")
        ld_cols = sem("ld_cols")
        ld_mod = sem("ld_mod")
        ld_qk = sem("ld_qk")
        ld_v = sem("ld_v")
        ld_bp = sem("ld_bp")
        ld_kv = sem("ld_kv")
        ld_w = sem("ld_w")
        silu = sem("silu")
        csT_full = sem("csT_full")
        csT_ready = sem("csT_ready")
        colp_ready = sem("colp_ready")
        cols_full = sem("cols_full")
        cols_ready = sem("cols_ready")
        mr_full = sem("mr_full")
        mr_ready = sem("mr_ready")
        mc_full = sem("mc_full")
        mc_ready = sem("mc_ready")
        cxv = sem("cxv")
        cxr = sem("cxr")
        cxn_ready = sem("cxn_ready")
        cxt_full = sem("cxt_full")
        cxt_ready = sem("cxt_ready")
        wqk_ready = sem("wqk_ready")
        wq_ready = sem("wq_ready")
        wpg_ready = sem("wpg_ready")
        kv_full = sem("kv_full")
        kv_ready = sem("kv_ready")
        ck_full = sem("ck_full")
        ck_ready = sem("ck_ready")
        ckparts = sem("ckparts")
        ckstack = sem("ckstack")
        gate_full = sem("gate_full")
        gate_ready = sem("gate_ready")
        lnv_a = sem("lnv_a")
        lnr_a = sem("lnr_a")
        ln_a = sem("ln_a")
        lnv_b = sem("lnv_b")
        lnr_b = sem("lnr_b")
        ln_b = sem("ln_b")
        xta_full = sem("xta_full")
        xta_ready = sem("xta_ready")
        qk_full = sem("qk_full")
        qk_evac = sem("qk_evac")
        parts = sem("parts")
        stack0 = sem("stack0")
        stack1 = sem("stack1")
        v_full = sem("v_full")
        v_ready = sem("v_ready")
        s_full = sem("s_full")
        s_max = sem("s_max")
        nmparts = sem("nmparts")
        mrow_full = sem("mrow_full")
        mrow_ready = sem("mrow_ready")
        mrd0 = sem("mrd0")
        mrd1 = sem("mrd1")
        mrd2 = sem("mrd2")
        mrd3 = sem("mrd3")
        st_full = sem("st_full")
        exp_done = sem("exp_done")
        av_done = sem("av_done")
        u_ready = sem("u_ready")
        ut_full = sem("ut_full")
        on_ready = sem("on_ready")
        ot_full = sem("ot_full")
        ot_ready = sem("ot_ready")
        pj_full = sem("pj_full")
        x1 = sem("x1")
        xg1 = sem("xg1")
        xtb_full = sem("xtb_full")
        xtb_ready = sem("xtb_ready")
        cq_full = sem("cq_full")
        cq_evac = sem("cq_evac")
        cparts = sem("cparts")
        cstack0 = sem("cstack0")
        cstack1 = sem("cstack1")
        cs_full = sem("cs_full")
        cs_max = sem("cs_max")
        cnmparts = sem("cnmparts")
        cmrow_full = sem("cmrow_full")
        cmrow_ready = sem("cmrow_ready")
        cmrd = sem("cmrd")
        cst_full = sem("cst_full")
        cexp_done = sem("cexp_done")
        cav_done = sem("cav_done")
        cu_ready = sem("cu_ready")
        cut_full = sem("cut_full")
        con_ready = sem("con_ready")
        cot_full = sem("cot_full")
        cot_ready = sem("cot_ready")
        cpj_full = sem("cpj_full")
        x2 = sem("x2")
        xg2 = sem("xg2")
        xtc_full = sem("xtc_full")
        xtc_ready = sem("xtc_ready")
        h_full = sem("h_full")
        h_ready = sem("h_ready")
        mo_full = sem("mo_full")
        x3 = sem("x3")
        xg3 = sem("xg3")
        st_out = sem("st_out")
        mrd = [mrd0, mrd1, mrd2, mrd3]
        stack = [stack0, stack1]
        cstack = [cstack0, cstack1]


        block = ctx.enter_context(nc.Block())
        NLD_COLS, NLD_MOD, NLD_V, NLD_KV, NLD_W = 16 * 5, 16 * 3, 16 * 2, 16 * 3, 16 * 6


        @block.sync
        def _(e):
            def ld(dst, src, done):
                e.dma_start(dst, src).then_inc(done, 16)

            def weight(name):
                return a[name].rearrange("(k p) n -> p k n", p=P)

            def load_modulation(L):
                n = LAYER[L]
                if L:
                    e.wait_ge(cols_full, L)
                ld(colr[0:12, :], a[n["mod_b"]].rearrange("(j p) -> j p", p=P), ld_cols)
                ld(colr[12:, :], a[n["b1"]].rearrange("(j p) -> j p", p=P), ld_cols)
                ld(colp[0:4, :], a[n["qkv_b"]][0:2 * D].rearrange("(j p) -> j p", p=P), ld_cols)
                ld(colp[4:6, :], a[n["q_b"]].rearrange("(j p) -> j p", p=P), ld_cols)
                ld(colp[6:8, :], a[n["kv_b"]][0:D].rearrange("(j p) -> j p", p=P), ld_cols)
                if L:
                    e.wait_ge(mr_full, L)
                    e.wait_ge(mr_ready, L)
                ld(w_mod, weight(n["mod_w"]), ld_mod)
                for i, m in enumerate((GATE_A, GATE_M)):
                    ld(gb_m[:, i, :], a[n["mod_b"]][m * D:(m + 1) * D].partition_broadcast(B), ld_mod)

            def load_qk(L):
                if L:
                    e.wait_ge(wqk_ready, L)
                ld(stage, weight(LAYER[L]["qkv_w"])[:, :, 0:2 * D], ld_qk)

            def load_v(L):
                n = LAYER[L]
                if L:
                    e.wait_ge(v_ready, 2 * B * L)
                ld(w_v, weight(n["qkv_w"])[:, :, 2 * D:3 * D], ld_v)
                ld(b_v, a[n["qkv_b"]][2 * D:3 * D].partition_broadcast(P), ld_v)

            def load_bp(L):
                if L:
                    e.wait_ge(xg1, B * L)
                ld(b_p, a[LAYER[L]["p_b"]].partition_broadcast(P), ld_bp)

            def load_cross(L):
                n = LAYER[L]
                if L:
                    e.wait_ge(x3, 2 * B * L)
                    e.wait_ge(wqk_ready, L + 1)
                ld(w_kv, weight(n["kv_w"]), ld_kv)
                ld(raw_q[L], weight(n["q_w"]), ld_kv)
                ld(b_cv, a[n["kv_b"]][D:2 * D].partition_broadcast(P), ld_kv)

            def load_rest(L):
                n = LAYER[L]
                ld(w_p, weight(n["p_w"]), ld_w)
                ld(w_c, weight(n["c_w"]), ld_w)
                ld(w_1, weight(n["w1"]), ld_w)
                ld(w_2, weight(n["w2"]), ld_w)
                for row, t in ((b_c, "c_b"), (b_2, "b2")):
                    ld(row, a[n[t]].partition_broadcast(P), ld_w)

            def stack_cross_keys(L):
                if L:
                    e.wait_ge(cst_full, NG * B * L)
                for c in range(KC):
                    for t, k in by_part(K_TERMS):
                        e.wait_ge(ckparts, 3 * (KC * L + c) + k + 1)
                        ld(ckst[HD * t:HD * (t + 1), HC * c:HC * (c + 1), :], cpart[:, k, c, 0:B * S], ckstack)

            def by_part(terms):
                return sorted(enumerate(terms), key=lambda term: term[1])

            def stack_self(s):
                for i, j in enumerate(QK_ORDER):
                    c, dst, terms = j % 2, (qst, kst)[j // 2], (Q_TERMS, K_TERMS)[j // 2]
                    if s:
                        e.wait_ge(st_full, 32 * (s - 1) + 16 * (c + 1))
                    for t, k in by_part(terms):
                        e.wait_ge(parts, 3 * (4 * s + i) + k + 1)
                        e.dma_start(dst[HD * t:HD * (t + 1), HC * c:HC * (c + 1), :],
                                    part[:, k, j, :]).then_inc(stack[c], 16)

            def max_rows(s, g):
                e.wait_ge(mrow_ready, NG * s + g + 1)
                e.dma_start(qst[ROWS:ROWS + 3, G * g:G * (g + 1), :], mrow[:, g % 2, :]).then_inc(mrd[g], 16)

            def stack_cross(s):
                e.wait_ge(cst_full, NG * s)
                for c in range(KC):
                    e.wait_ge(cq_evac, KC * s + c + 1)
                    for t, k in by_part(Q_TERMS):
                        if k:
                            e.wait_ge(cparts, 2 * (KC * s + c) + k)
                        e.dma_start(cqst[HD * t:HD * (t + 1), HC * c:HC * (c + 1), :],
                                    cpart[:, k, c, :]).then_inc(cstack[c], 16)

            def cross_max_rows(s):
                e.wait_ge(cmrow_ready, s + 1)
                e.dma_start(cqst[ROWS + 1:ROWS + 4, :, :], cmrow[:, :]).then_inc(cmrd, 16)

            def store(s):
                e.wait_ge(x3, 2 * (s + 1))
                e.dma_start(out[s - B].rearrange("(t p) d -> p t d", p=P), x[:, s - B, :, :]).then_inc(st_out, 16)

            ld(cond[:, :], a["cond_1024"], ld_cond)
            load_modulation(0)
            ld(x[:, 0, :, :], a["x"][0].rearrange("(t p) d -> p t d", p=P), ld_x0)
            load_qk(0)
            ld(cx, a["ctx_1024"].rearrange("(i b) s d -> (b s) i d", i=2), ld_ctx)
            ld(mask8[ROWS:ROWS + 1, :], a["mask_BxS2_bf0"].rearrange("(o b) s -> o (b s)", o=1), ld_ctx)
            load_v(0)
            load_bp(0)
            e.wait_ge(ones_ready, 1)
            ld(kst[ROWS:ROWS + 3, :, :], cmrow[0:3, :].unsqueeze(1).broadcast_to([3, H, N]), fill_k)
            ld(cqst[ROWS:ROWS + 1, :, :], cmrow[0:1, :].unsqueeze(1).broadcast_to([1, H, N]), fill_k)
            ld(ckst[ROWS + 1:ROWS + 4, :, :], cmrow[0:3, 0:B * S].unsqueeze(1).broadcast_to([3, H, B * S]), fill_k)
            e.wait_ge(mask_ready, 1)
            ld(ckst[ROWS:ROWS + 1, 1:H, :], ckst[ROWS:ROWS + 1, 0:1, :].broadcast_to([1, H - 1, B * S]), fill_k)
            load_cross(0)
            stack_self(0)
            ld(x[:, 1:B, :, :], a["x"][1:B].rearrange("b (t p) d -> p b t d", p=P), ld_x)
            load_modulation(1)
            load_qk(1)
            load_rest(0)
            stack_cross_keys(0)
            for g in range(NG):
                max_rows(0, g)
            for s in range(2 * B):
                more = s < 2 * B - 1
                if s == B:
                    load_cross(1)
                    load_rest(1)
                if more:
                    stack_self(s + 1)
                if s == B - 1:
                    load_v(1)
                    load_bp(1)
                if s == B:
                    stack_cross_keys(1)
                stack_cross(s)
                for g in range(NG):
                    if g == 1:
                        cross_max_rows(s)
                    if more:
                        max_rows(s + 1, g)
                if s >= B:
                    store(s)
            e.wait_ge(st_out, 16 * B)

        @block.gpsimd
        def _(e):
            n = [0]

            def link(ins):
                n[0] += 1
                ins.then_inc(c_pool, 1)
                e.wait_ge(c_pool, n[0])

            def constants():
                e.memset(ident[:, :], 0.0).then_inc(c_pool, 1)
                link(e.memset(identb[:, :], 0.0))
                n[0] += 1
                e.wait_ge(c_pool, 2)
                for m in (ident, identb):
                    ins = e.affine_select(out=m[:, :], in_=m[:, :], compare_op=ALU.not_equal, fill=1.0, base=0,
                                          pattern=[[-1, P]], channel_multiplier=1)
                ins.then_inc(idents, 1)
                link(e.memset(half[:, :], -0.5))

            def fill():
                link(e.memset(vaug[:, :, :, HD:2 * HD], 1.0))
                link(e.memset(cv[:, :, :, :], 0.0))
                link(e.memset(cv[0:S, :, :, HD:2 * HD], 1.0))
                e.memset(cv[S:P, :, :, 3 * HD:4 * HD], 1.0).then_inc(fill_v, 1)
                e.wait_ge(fill_v, 1)

            def power_halves(k):
                for i in range(2):
                    ts = slice(2 * i, 2 * i + 2)
                    power(mv[:, ts, 1], rstd[:, ts], lnv_b, lnr_b, k + i + 1)

            def power(v, r, vs, rs, target):
                e.wait_ge(vs, target)
                link(e.tensor_scalar(r, v, EPS, 1.0, ALU.add, ALU.mult))
                e.tensor_tensor(r, r, half[:, 0:r.shape[1]], ALU.pow).then_inc(rs, 1)

            def split(f, p0, p1, p2, done, k):
                e.tensor_scalar(p0, f, 1.0, 0.0, ALU.mult, ALU.add).then_inc(done, 1)
                e.wait_ge(done, 3 * k + 1)
                link(e.tensor_tensor(f, f, p0, ALU.subtract))
                e.tensor_scalar(p1, f, 1.0, 0.0, ALU.mult, ALU.add).then_inc(done, 1)
                e.wait_ge(done, 3 * k + 2)
                e.tensor_tensor(p2, f, p1, ALU.subtract).then_inc(done, 1)

            def key_parts(L):
                if L:
                    e.wait_ge(cstack0, 96 * B * L)
                    e.wait_ge(cstack1, 96 * B * L)
                for c in range(KC):
                    e.wait_ge(ck_ready, KC * L + c + 1)
                    split(ckf[L][:, c, :], cpart[:, 0, c, 0:B * S], cpart[:, 1, c, 0:B * S], cpart[:, 2, c, 0:B * S], ckparts,
                          KC * L + c)

            def self_parts(s):
                for i, j in enumerate(QK_ORDER):
                    e.wait_ge(qk_evac, 4 * s + i + 1)
                    if i == 0 and s:
                        e.wait_ge(stack0, 192 * s)
                        e.wait_ge(stack1, 192 * s)
                    split(qf[:, i % 2, :], part[:, 0, j, :], part[:, 1, j, :], part[:, 2, j, :], parts, 4 * s + i)

            def max_parts(s, g):
                e.wait_ge(s_max, 64 * s + 16 * (g + 1))
                if g == 0:
                    e.wait_ge(mrow_full, NG * s)
                f = nmax[:, g, :, :]
                link(e.tensor_scalar(mp[:, g, :, 0, :], f, 1.0, 0.0, ALU.mult, ALU.add))
                link(e.tensor_tensor(nres[:, :, :], f, mp[:, g, :, 0, :], ALU.subtract))
                link(e.tensor_scalar(mp[:, g, :, 1, :], nres[:, :, :], 1.0, 0.0, ALU.mult, ALU.add))
                link(e.tensor_tensor(mp[:, g, :, 2, :], nres[:, :, :], mp[:, g, :, 1, :], ALU.subtract))
                e.tensor_scalar(nres[:, :, :], f, 1.0, 0.0, ALU.mult, ALU.add).then_inc(nmparts, 1)

            def add_bias(s, b_row, gate_row, ready, target, done):
                e.wait_ge(ready, target)
                b = s % B
                if gate_row is not None:
                    link(e.tensor_tensor(gbt[:, :], gate_row, b_row, ALU.mult))
                    b_row = gbt[:, :]
                e.tensor_tensor(x[:, b, :, :], x[:, b, :, :], b_row.unsqueeze(1).broadcast_to([P, TN, D]),
                                ALU.add).then_inc(done, 1)

            def parts_until(s, m0, m1, more):
                for g in range(NG):
                    if more and m0 < TILES // NG * (g + 1) <= m1:
                        max_parts(s, g)

            def gated_weights(s):
                e.wait_ge(ld_w, NLD_W * (s // B + 1))
                e.wait_ge(x3, 2 * s)
                e.wait_ge(ck_full, KC * (s // B + 1))
                e.tensor_tensor(w_pg[:, :, :], w_p[:, :, :], gate[:, 0, :].unsqueeze(1).broadcast_to([P, KC, D]),
                                ALU.mult).then_inc(wpg_ready, 1)

            constants()
            power(mv[:, :, 1], rstd[:, :], lnv_a, lnr_a, 1)
            power(cmv[:, :, 1], crstd[:, :], cxv, cxr, 1)
            fill()
            self_parts(0)
            key_parts(0)
            parts_until(0, 0, START[0], True)
            power(mv[:, :, 1], rstd[:, :], lnv_a, lnr_a, 2)
            parts_until(0, START[0], TILES, True)
            for s in range(2 * B):
                more = s < 2 * B - 1
                L = s // B
                e.wait_ge(ld_bp, 16 * (L + 1))
                e.wait_ge(gate_ready, s + 1)
                add_bias(s, b_p, gate[:, 0, :], ln_a, s + 1, xg1)
                if s % B:
                    gated_weights(s)
                if more:
                    self_parts(s + 1)
                if s == B:
                    key_parts(1)
                if s % B == 0:
                    gated_weights(s)
                parts_until(s + 1, 0, AT["proj"][1], more)
                power_halves(4 * s)
                e.wait_ge(ld_w, NLD_W * (L + 1))
                add_bias(s, b_c, None, ln_b, 4 * s + 2, xg2)
                parts_until(s + 1, AT["proj"][1], AT["norm3"][0], more)
                power_halves(4 * s + 2)
                add_bias(s, b_2, gate[:, 1, :], ln_b, 4 * s + 4, xg3)
                parts_until(s + 1, AT["norm3"][0], AT["h5"][1], more)
                if s + 2 < 2 * B:
                    power(mv[:, :, 1], rstd[:, :], lnv_a, lnr_a, s + 3)
                parts_until(s + 1, AT["h5"][1], TILES, more)

        @block.vector
        def _(e):
            n = [0]

            def link(ins):
                n[0] += 1
                ins.then_inc(c_dve, 1)
                e.wait_ge(c_dve, n[0])

            def statistics(src, vs, ts=range(TN)):
                for t in ts:
                    ins = e.bn_stats(stat[:, t, :], src[:, t, :])
                link(ins)
                for t in ts:
                    ins = e.bn_aggr(mv[:, t, :], stat[:, t, :])
                ins.then_inc(vs, 1)

            def normalise(src, dst, vs, rs, done, k, ts=range(TN)):
                e.wait_ge(vs, k)
                e.wait_ge(rs, k)
                for t in ts:
                    ins = e.tensor_scalar(dst[:, t, :], src[:, t, :], mv[:, t, 0:1], rstd[:, t:t + 1],
                                          ALU.subtract, ALU.mult)
                ins.then_inc(done, 1)

            def permute(dst, src):
                return e.tensor_copy(dst.rearrange("p (j d h) -> p j d h", d=HD, h=HC),
                                     src.rearrange("p (j h d) -> p j d h", d=HD, h=HC))

            def mask_bias():
                e.wait_ge(ld_ctx, 32)
                e.tensor_scalar(ckst[ROWS:ROWS + 1, 0, :], mask8[ROWS:ROWS + 1, :],
                                MASKED, None, ALU.mult).then_inc(mask_ready, 1)

            def column_rows(L):
                e.wait_ge(ld_cols, NLD_COLS * (L + 1))
                permute(colpp[:, :], colp[:, :]).then_inc(colp_ready, 1)

            def modulation(L):
                e.wait_ge(cols_full, L + 1)
                e.tensor_copy(columns[:, L, :], MI[:, 256:256 + NCOL]).then_inc(c_dve, 1)
                n[0] += 1
                e.wait_ge(c_dve, n[0])
                e.tensor_scalar(colq[:, L, 0:2], cols[:, L, 0:2], SCALE, None, ALU.mult)
                e.tensor_scalar(colq[:, L, 2:4], cols[:, L, 4:6], SCALE, None, ALU.mult).then_inc(cols_ready, 1)
                e.wait_ge(ld_mod, NLD_MOD * (L + 1))
                e.wait_ge(mr_full, L + 1)
                e.tensor_copy(modr[:, 0:2 * D], A[0:B, 0, :])
                e.tensor_copy(modr[:, 2 * D:3 * D], A[0:B, 1, D:2 * D])
                e.tensor_copy(modr[:, 3 * D:4 * D], A[0:B, 2, 0:D])
                e.tensor_tensor(grow[:, L, 0, :], A[0:B, 1, 0:D], gb_m[:, 0, :], ALU.add)
                e.tensor_tensor(grow[:, L, 1, :], A[0:B, 2, D:2 * D], gb_m[:, 1, :], ALU.add).then_inc(mr_ready, 1)

            def modulation_columns(L):
                e.wait_ge(mc_full, L + 1)
                for i, m in enumerate((0, 6)):
                    ins = e.tensor_tensor(modc[:, L, 4 * i:4 * i + 4, :],
                                          MI[:, 16 * i:16 * i + 16].rearrange("p (j b) -> p j b", j=4),
                                          modb[:, L, m:m + 4].unsqueeze(2).broadcast_to([P, 4, B]), ALU.add)
                link(ins)
                for m in (SCALE_A, SCALE_M):
                    ins = e.tensor_scalar(modc[:, L, 2 * m:2 * m + 2, :], modc[:, L, 2 * m:2 * m + 2, :], 1.0, None, ALU.add)
                ins.then_inc(mc_ready, 1)

            def qk_weights(L):
                e.wait_ge(ld_qk, 16 * (L + 1))
                e.wait_ge(qk_full, 4 * B * L)
                for k in range(KC):
                    ins = permute(w_qk[:, k, :], stage[:, k, :])
                ins.then_inc(wqk_ready, 1)

            def cross_weights(L):
                e.wait_ge(ld_kv, NLD_KV * (L + 1))
                for k in range(KC):
                    permute(w_q[:, k, :], raw_q[L][:, k, :])
                    ins = permute(w_ck[:, k, :], w_kv[:, k, 0:D])
                ins.then_inc(wq_ready, 1)
                if L:
                    e.wait_ge(cst_full, NG * B * L)
                    e.memset(ckst[ROWS:ROWS + 1, :, :], 0.0).then_inc(mask_ready, 1)

            def context_norm():
                e.wait_ge(ld_ctx, 32)
                for t in range(2):
                    ins = e.bn_stats(stat[:, t, :], cx[:, t, :])
                link(ins)
                for t in range(2):
                    ins = e.bn_aggr(cmv[:, t, :], stat[:, t, :])
                ins.then_inc(cxv, 1)
                e.wait_ge(cxv, 1)
                e.wait_ge(cxr, 1)
                for t in range(2):
                    ins = e.tensor_scalar(cxn[:, t, :], cx[:, t, :], cmv[:, t, 0:1], crstd[:, t:t + 1],
                                          ALU.subtract, ALU.mult)
                ins.then_inc(cxn_ready, 1)

            def context_columns():
                for L in range(2):
                    e.wait_ge(cxt_full, L + 1)
                    e.tensor_copy(cxT[:, L, :, :], OA[:, :].rearrange("p (k n) -> p k n", k=KC)).then_inc(cxt_ready, 1)

            def cross_values(L, banks):
                if L:
                    e.wait_ge(cav_done, NG * B * L)
                else:
                    e.wait_ge(fill_v, 1)
                for b in range(B):
                    e.wait_ge(kv_full, 2 * L + b // 2 + 1)
                    src = banks[:, b // 2, (b % 2) * D:(b % 2 + 1) * D].rearrange("p (i o d) -> p i o d", o=2, d=HD)
                    br = b_cv.rearrange("p (i o d) -> p i o d", o=2, d=HD)
                    e.tensor_tensor(cv[0:S, b, :, 0:HD], src[0:S, :, 0, :], br[0:S, :, 0, :], ALU.add)
                    ins = e.tensor_tensor(cv[S:P, b, :, 2 * HD:3 * HD], src[S:P, :, 1, :], br[S:P, :, 1, :], ALU.add)
                ins.then_inc(kv_ready, 1)

            def gates(s):
                e.wait_ge(gate_full, s + 1)
                e.tensor_copy(gate[:, :, :], R[:, 1, :].rearrange("p (g n) -> p g n", g=2)).then_inc(gate_ready, 1)

            def norm1(s, nxt=None):
                b = s % B
                if s == 0:
                    e.wait_ge(ld_x0, 16)
                elif s < B:
                    e.wait_ge(ld_x, 16)
                else:
                    e.wait_ge(x3, 2 * (s - B + 1))
                e.wait_ge(xta_full, KC * s)
                statistics(x[:, b, :, :], lnv_a)
                maxes(nxt, *AT["h6"])
                normalise(x[:, b, :, :], xn_a, lnv_a, lnr_a, ln_a, s + 1)

            def modulate1(s):
                b, L = s % B, s // B
                e.wait_ge(v_full, 2 * s)
                e.wait_ge(mc_ready, L + 1)
                for c in range(KC):
                    e.wait_ge(xta_full, KC * s + c + 1)
                    e.tensor_scalar(xt_a[:, c, :], R[:, c, :], modc[:, L, 2 * SCALE_A + c, b:b + 1],
                                    modc[:, L, 2 * SHIFT_A + c, b:b + 1], ALU.mult, ALU.add).then_inc(xta_ready, 1)

            def values(s, i):
                if i:
                    e.wait_ge(av_done, 16 * s)
                    e.wait_ge(ld_v, NLD_V * (s // B + 1))
                e.wait_ge(v_full, 2 * s + 2 - i)
                e.tensor_tensor(vaug[:, 2 * i:2 * i + 2, :, 0:HD],
                                (OA, MI)[i][:, :].rearrange("p (t h d) -> p t h d", t=2, h=H),
                                b_v.rearrange("p (h d) -> p h d", h=H).unsqueeze(1).broadcast_to([P, 2, H, HD]),
                                ALU.add).then_inc(v_ready, 1)

            def maxes(s, m0, m1):
                if s is None:
                    return
                if m0 == 0:
                    e.wait_ge(nmparts, NG * s)
                for m in range(m0, m1):
                    h, t = m // TN, m % TN
                    e.wait_ge(s_full, TILES * s + m + 1)
                    e.tensor_reduce(nmax[:, h // G, t, h % G:h % G + 1], R[:, m % 2, :], AX.X, ALU.max,
                                    negate=True).then_inc(s_max, 1)

            def unnormalised(s, g):
                e.wait_ge(av_done, 16 * s + 4 * (g + 1))
                if g >= 2:
                    e.wait_ge(ut_full, NG * s + g - 1)
                elif s:
                    e.wait_ge(cut_full, NG * s)
                e.tensor_copy(u[:, g % 2, :], OA[:, :]).then_inc(u_ready, 1)

            def out_norm(k, g, ut, on):
                e.wait_ge(ut, k + 1)
                m = MI[:, :].rearrange("p (t j d) -> p t j d", t=TN, j=G)
                link(e.reciprocal(rsum[:, :, :], m[:, :, :, HD]))
                dst = xn_b[:, :, HD * G * g:HD * G * (g + 1)].rearrange("p t (j d) -> p t j d", j=G)
                e.tensor_tensor(dst, m[:, :, :, 0:HD], rsum[:, :, :].unsqueeze(3).broadcast_to([P, TN, G, HD]),
                                ALU.mult).then_inc(on, 1)

            def residual(s, full, xg, xs, gate_row, banks, halves=(0, 1)):
                b = s % B
                e.wait_ge(xg, s + 1)
                for i in halves:
                    e.wait_ge(full, 2 * s + i + 1)
                    y = banks[i].rearrange("p (t n) -> p t n", t=2)
                    if gate_row is not None:
                        e.wait_ge(xs, 2 * s + i)
                        link(e.tensor_tensor(tmp[:, :, :], y, gate_row.unsqueeze(1).broadcast_to([P, 2, D]), ALU.mult))
                        y = tmp[:, :, :]
                    e.tensor_tensor(x[:, b, 2 * i:2 * i + 2, :], y, x[:, b, 2 * i:2 * i + 2, :], ALU.add).then_inc(xs, 1)

            def cross_parts(s, nxt):
                for c in range(KC):
                    maxes(nxt, *AT[f"q{c}"])
                    e.wait_ge(cq_evac, KC * s + c + 1)
                    link(e.tensor_tensor(qf[:, c, :], qf[:, c, :], cpart[:, 0, c, :], ALU.subtract))
                    e.tensor_copy(cpart[:, 1, c, :], qf[:, c, :]).then_inc(cparts, 1)
                    e.wait_ge(cparts, 2 * (KC * s + c) + 1)
                    e.tensor_tensor(cpart[:, 2, c, :], qf[:, c, :], cpart[:, 1, c, :], ALU.subtract).then_inc(cparts, 1)

            def cross_max(s, t0):
                e.wait_ge(cmrow_full, s)
                for t in (t0, t0 + 1):
                    e.wait_ge(cs_full, TN * s + t + 1)
                    i = 2 * (t % 2)
                    e.tensor_reduce(cnmax[:, t, :], A[:, i:i + 2, :].rearrange("p i (h n) -> p (i h) n", n=S),
                                    AX.X, ALU.max, negate=True).then_inc(cs_max, 1)

            def cross_max_parts(s):
                e.wait_ge(cs_max, TN * (s + 1))
                f = cnmax[:, :, :]
                link(e.tensor_copy(cmp_[:, :, 0, :], f))
                link(e.tensor_tensor(cnres[:, :, :], f, cmp_[:, :, 0, :], ALU.subtract))
                link(e.tensor_copy(cmp_[:, :, 1, :], cnres[:, :, :]))
                e.tensor_tensor(cmp_[:, :, 2, :], cnres[:, :, :], cmp_[:, :, 1, :], ALU.subtract).then_inc(cnmparts, 1)

            e.memset(cmrow[0:4, :], 1.0).then_inc(ones_ready, 1)
            column_rows(0)
            e.wait_ge(csT_full, 1)
            e.tensor_copy(csT[:, :, :], MI[:, 0:KC * B].rearrange("p (k b) -> p k b", k=KC)).then_inc(csT_ready, 1)
            norm1(0)
            modulation(0)
            modulation_columns(0)
            qk_weights(0)
            modulate1(0)
            mask_bias()
            context_norm()
            context_columns()
            values(0, 1)
            values(0, 0)
            cross_weights(0)
            cross_values(0, A[:, 0:2, :])
            maxes(0, 0, START[0])
            column_rows(1)
            norm1(1)
            modulation(1)
            maxes(0, START[0], START[1])
            modulation_columns(1)
            maxes(0, START[1], TILES)
            for s in range(2 * B):
                b = s % B
                nxt = s + 1 if s < 2 * B - 1 else None
                gates(s)
                if s == B - 1:
                    qk_weights(1)
                if nxt is not None:
                    modulate1(nxt)
                e.wait_ge(xtc_full, KC * s)
                for g in range(NG):
                    unnormalised(s, g)
                    if s == B and g == 1:
                        cross_weights(1)
                    if s == B and g == 2:
                        cross_values(1, R)
                    if g == NG - 2:
                        maxes(nxt, *AT["unit13"])
                    if g == NG - 1:
                        maxes(nxt, *AT["av"])
                    out_norm(NG * s + g, g, ut_full, on_ready)
                    if g == NG - 2:
                        maxes(nxt, AT["unit14"][0], AT["unit15"][1])
                maxes(nxt, AT["ot"][0], AT["proj"][1])
                maxes(nxt, *AT["pa"])
                residual(s, pj_full, xg1, x1, None, (A[:, 2, :], A[:, 3, :]), (0,))
                e.wait_ge(x1, 2 * s + 1)
                statistics(x[:, b, :, :], lnv_b, (0, 1))
                maxes(nxt, *AT["va"])
                residual(s, pj_full, xg1, x1, None, (A[:, 2, :], A[:, 3, :]), (1,))
                e.wait_ge(ot_full, 2 * (s + 1))
                normalise(x[:, b, :, :], xn_b, lnv_b, lnr_b, ln_b, 4 * s + 1, (0, 1))
                e.wait_ge(x1, 2 * (s + 1))
                statistics(x[:, b, :, :], lnv_b, (2, 3))
                maxes(nxt, *AT["norm2"])
                normalise(x[:, b, :, :], xn_b, lnv_b, lnr_b, ln_b, 4 * s + 2, (2, 3))
                if nxt is not None:
                    values(nxt, 1)
                maxes(nxt, AT["halfq"][0], AT["cqb"][1])
                cross_parts(s, nxt)
                maxes(nxt, AT["stack"][0], AT["half"][1])
                cross_max(s, 0)
                maxes(nxt, *AT["cross2"])
                cross_max(s, 2)
                cross_max_parts(s)
                maxes(nxt, AT["cmrow"][0], AT["crows"][1])
                e.wait_ge(xtb_full, 2 * (s + 1))
                for g in range(NG):
                    maxes(nxt, *AT[f"g{g}"])
                    out_norm(NG * s + g, g, cut_full, con_ready)
                maxes(nxt, AT["cot"][0], AT["ca"][1])
                residual(s, cpj_full, xg2, x2, None, (A[:, 2, :], A[:, 3, :]), (0,))
                e.wait_ge(x2, 2 * s + 1)
                statistics(x[:, b, :, :], lnv_b, (0, 1))
                residual(s, cpj_full, xg2, x2, None, (A[:, 2, :], A[:, 3, :]), (1,))
                e.wait_ge(cot_full, 2 * (s + 1))
                normalise(x[:, b, :, :], xn_b, lnv_b, lnr_b, ln_b, 4 * s + 3, (0, 1))
                e.wait_ge(x2, 2 * (s + 1))
                statistics(x[:, b, :, :], lnv_b, (2, 3))
                maxes(nxt, AT["norm3"][0], AT["vb"][1])
                normalise(x[:, b, :, :], xn_b, lnv_b, lnr_b, ln_b, 4 * s + 4, (2, 3))
                if nxt is not None:
                    values(nxt, 0)
                maxes(nxt, AT["halfm"][0], AT["h5"][1])
                if s + 2 < 2 * B:
                    norm1(s + 2, nxt)
                else:
                    maxes(nxt, *AT["h6"])
                maxes(nxt, AT["h7"][0], AT["o1"][1])
                residual(s, mo_full, xg3, x3, gate[:, 1, :], (A[:, 0, :], MI[:, :]), (0,))
                maxes(nxt, AT["o2"][0], AT["o3"][1])
                residual(s, mo_full, xg3, x3, gate[:, 1, :], (A[:, 0, :], MI[:, :]), (1,))

        @block.scalar
        def _(e):
            def cross_keys(L, banks):
                e.wait_ge(cols_ready, L + 1)
                for c in range(KC):
                    e.wait_ge(ck_full, KC * L + c + 1)
                    e.activation(ckf[L][:, c, :], banks[:, c, 0:B * S], ACT.Identity,
                                 bias=cols[:, L, 6 + c:7 + c]).then_inc(ck_ready, 1)

            def qk(s, i):
                j, L = QK_ORDER[i], s // B
                if i == 0:
                    e.wait_ge(cols_ready, L + 1)
                    if s > 1:
                        e.wait_ge(cparts, 2 * KC * (s - 1))
                e.wait_ge(qk_full, 4 * s + i + 1)
                if i >= 2:
                    e.wait_ge(parts, 3 * (4 * s + i - 1))
                if j < 2:
                    ins = e.activation(qf[:, i % 2, :], R[:, i % 2, :], ACT.Identity, bias=colq[:, L, j:j + 1], scale=SCALE)
                else:
                    ins = e.activation(qf[:, i % 2, :], R[:, i % 2, :], ACT.Identity, bias=cols[:, L, j:j + 1])
                ins.then_inc(qk_evac, 1)

            def row_in(s, step):
                for g in range(NG - 1):
                    m0, m1 = AT[step]
                    if s is not None and m0 <= ROW_TILE[g] < m1:
                        row(s, g)

            def row(s, g):
                k = NG * s + g
                e.wait_ge(mrow_full, k + 1)
                if k >= 2:
                    e.wait_ge(mrd[(k - 2) % NG], 16 * ((k - 2) // NG + 1))
                e.copy(mrow[:, g % 2, :], R[0:3 * G, 0, :] if g == NG - 1 else OA[0:3 * G, :]).then_inc(mrow_ready, 1)

            def exps(s, n):
                if n == 0:
                    e.wait_ge(mo_full, 2 * s)
                    if s == 0:
                        e.wait_ge(mr_full, 2)
                        e.wait_ge(ckparts, 3 * KC)
                        e.wait_ge(wq_ready, 1)
                for m in (2 * n, 2 * n + 1):
                    e.wait_ge(st_full, 32 * s + m + 1)
                    if m >= 4:
                        e.wait_ge(av_done, 16 * s + (m - 4) // 2 + 1)
                    e.activation(big[:, m % 4, :, :], A[:, 2 - 2 * (m % 2):4 - 2 * (m % 2), :], ACT.Exp).then_inc(exp_done, 1)

            def copies(full, k, ready, free, fk):
                e.wait_ge(free, fk)
                for i in range(2):
                    h = slice(i * N // 2, (i + 1) * N // 2)
                    e.wait_ge(full, k + i + 1)
                    e.copy(xt_b[:, :, h], A[:, i, :].rearrange("p (c n) -> p c n", c=KC)).then_inc(ready, 1)

            def modulated(s, nxt):
                e.wait_ge(cpj_full, 2 * (s + 1))
                for i in range(2):
                    h = slice(i * N // 2, (i + 1) * N // 2)
                    e.wait_ge(xtc_full, 2 * s + i + 1)
                    for c in range(KC):
                        ins = e.activation(xt_b[:, c, h], A[:, i, c * N // 2:(c + 1) * N // 2], ACT.Identity,
                                           bias=modc[:, s // B, 2 * SHIFT_M + c, s % B:s % B + 1],
                                           scale=modc[:, s // B, 2 * SCALE_M + c, s % B:s % B + 1])
                    ins.then_inc(xtc_ready, 1)
                    for step in (("halfm", "ha"), ("hb",))[i]:
                        row_in(nxt, step)

            def cross_q(s, nxt):
                e.wait_ge(parts, 12 * (s + 1 if nxt is None else nxt + 1))
                e.wait_ge(cstack0, 96 * s)
                e.wait_ge(cstack1, 96 * s)
                e.wait_ge(ckstack, 192 * (s // B + 1))
                for c in range(KC):
                    e.wait_ge(cq_full, KC * s + c + 1)
                    for dst in (cpart[:, 0, c, :], qf[:, c, :]):
                        ins = e.activation(dst, A[:, 2 + c, :], ACT.Identity, bias=colq[:, s // B, 2 + c:3 + c],
                                           scale=SCALE)
                    ins.then_inc(cq_evac, 1)

            def cross(s, nxt):
                e.wait_ge(cmrow_full, s + 1)
                e.wait_ge(cmrd, 16 * s)
                e.copy(cmrow[:, :], MI[0:3 * H, :]).then_inc(cmrow_ready, 1)
                row_in(nxt, "crows")
                e.wait_ge(av_done, 16 * (s + 1))
                e.wait_ge(ut_full, NG * (s + 1))
                for g in range(NG + 1):
                    if g < NG:
                        e.wait_ge(cst_full, NG * s + g + 1)
                        i = 2 * (g % 2)
                        e.activation(big[:, g, :, :], A[:, i:i + 2, :], ACT.Exp).then_inc(cexp_done, 1)
                    if g:
                        e.wait_ge(cav_done, NG * s + g)
                        if g > 2:
                            e.wait_ge(cut_full, NG * s + g - 2)
                        e.copy(u[:, (g - 1) % 2, :], OA[:, :]).then_inc(cu_ready, 1)
                        row_in(nxt, f"g{g - 1}")

            def load_table(function):
                e.activation(warm[:, :], half[0:1, 0:1], function)

            def gelu(s, nxt):
                e.wait_ge(cav_done, NG * (s + 1))
                for m in range(MC):
                    e.wait_ge(h_full, MC * s + m + 1)
                    e.activation(hid[:, m, :], A[:, (m + 2) % 4, :], GELU[s // B], bias=col1[:, s // B, m:m + 1]).then_inc(h_ready, 1)
                    if m >= 3:
                        row_in(nxt, f"h{m}")

            e.wait_ge(ld_cond, 16)
            e.activation(cs[:, :], cond[:, :], ACT.Silu).then_inc(silu, 1)
            for i in range(4):
                qk(0, i)
            cross_keys(0, A[:, 2:4, :])
            for g in range(NG - 1):
                row(0, g)
            for s in range(2 * B):
                nxt = s + 1 if s < 2 * B - 1 else None
                for n in range(16):
                    exps(s, n)
                    if s == B and n == 13:
                        cross_keys(1, R)
                    if n == 1:
                        row(s, NG - 1)
                    if nxt is not None and n in QK_AT:
                        qk(nxt, QK_AT.index(n))
                copies(ot_full, 2 * s, ot_ready, h_full, MC * s)
                copies(xtb_full, 2 * s, xtb_ready, pj_full, 2 * (s + 1))
                cross_q(s, nxt)
                for step in ("q0", "q1", "stack"):
                    row_in(nxt, step)
                row_in(nxt, "half")
                row_in(nxt, "cross2")
                row_in(nxt, "cmrow")
                cross(s, nxt)
                copies(cot_full, 2 * s, cot_ready, cq_full, KC * (s + 1))
                for step in ("ca", "norm3", "vb"):
                    row_in(nxt, step)
                load_table(GELU[s // B])
                modulated(s, nxt)
                gelu(s, nxt)
                if s < 2 * B - 1:
                    load_table(ACT.Exp)
                for t in range(TN):
                    row_in(nxt, f"o{t}")

        @block.tensor
        def _(e):
            def mm(o, l, r, start=True, stop=True):
                return e.matmul(o, l, r, start=start, stop=stop, skip_group_check=True)

            def condition():
                e.wait_ge(silu, 1)
                e.wait_ge(idents, 1)
                for k in range(KC):
                    ins = e.transpose(MI[:, k * B:(k + 1) * B], cs[:, k * P:(k + 1) * P], ident[0:B, 0:B])
                ins.then_inc(csT_full, 1)

            def modulation(L):
                if L:
                    e.wait_ge(mc_ready, L)
                    e.wait_ge(v_ready, 2)
                    e.wait_ge(kv_ready, 1)
                    e.wait_ge(ck_ready, KC)
                else:
                    e.wait_ge(csT_ready, 1)
                e.wait_ge(ld_cols, NLD_COLS * (L + 1))
                e.wait_ge(colp_ready, L + 1)
                e.transpose(MI[:, 256:256 + 12 + MC], colr[:, :], ident[0:12 + MC, 0:12 + MC])
                e.transpose(MI[:, 268 + MC:276 + MC], colpp[:, :], ident[0:8, 0:8]).then_inc(cols_full, 1)
                e.wait_ge(ld_mod, NLD_MOD * (L + 1))
                for j in range(3):
                    for k in range(KC):
                        ins = mm(A[0:B, j, :], csT[:, k, :], w_mod[:, k, 2 * j * D:2 * (j + 1) * D], k == 0, k == KC - 1)
                ins.then_inc(mr_full, 1)

            def modulation_columns(L):
                e.wait_ge(mr_ready, L + 1)
                e.wait_ge(cols_ready, L + 1)
                for j in range(8):
                    ins = e.transpose(MI[:, j * B:(j + 1) * B], modr[:, j * P:(j + 1) * P], ident[0:B, 0:B])
                ins.then_inc(mc_full, 1)

            def context():
                for L, src in enumerate((cx, cxn)):
                    if L:
                        e.wait_ge(cxn_ready, 1)
                        e.wait_ge(cxt_ready, 1)
                    else:
                        e.wait_ge(ld_ctx, 32)
                    for k in range(KC):
                        for i in range(2):
                            o = k * B * S + i * P
                            ins = e.transpose(OA[:, o:o + P], src[:, i, k * P:(k + 1) * P], ident[:, :])
                    ins.then_inc(cxt_full, 1)

            def cross_values(L, banks):
                e.wait_ge(cxt_ready, 2)
                e.wait_ge(ld_kv, NLD_KV * (L + 1))
                for b in range(B):
                    for o in (0, S):
                        for k in range(KC):
                            ins = mm(banks[o:o + S, b // 2, (b % 2) * D:(b % 2 + 1) * D],
                                     cxT[:, L, k, b * S:(b + 1) * S], w_kv[:, k, D:2 * D], k == 0, k == KC - 1)
                    if b % 2:
                        ins.then_inc(kv_full, 1)

            def cross_keys(L, banks):
                e.wait_ge(wq_ready, L + 1)
                if L:
                    e.wait_ge(kv_ready, L + 1)
                for c in range(KC):
                    for k in range(KC):
                        ins = mm(banks[:, c, 0:B * S], w_ck[:, k, c * P:(c + 1) * P], cxT[:, L, k, :],
                                 k == 0, k == KC - 1)
                    ins.then_inc(ck_full, 1)

            def gates(s):
                e.wait_ge(mr_ready, s // B + 1)
                e.wait_ge(s_max, TILES * (s + 1))
                e.wait_ge(x3, 2 * s)
                b, L = s % B, s // B
                mm(R[:, 1, :], ident[0:B, b:b + 1].broadcast_to([B, P]),
                   grow[:, L, :, :].rearrange("p g n -> p (g n)")).then_inc(gate_full, 1)

            def transposes(src, dst, full):
                for c in range(KC):
                    for t in range(TN):
                        ins = e.transpose(dst[:, c, t * P:(t + 1) * P], src[:, t, c * P:(c + 1) * P], ident[:, :])
                    ins.then_inc(full, 1)

            def transpose_half(src, i, full):
                for c in range(KC):
                    for t in (2 * i, 2 * i + 1):
                        o = c * N // 2 + (t % 2) * P
                        ins = e.transpose(A[:, i, o:o + P], src[:, t, c * P:(c + 1) * P], ident[:, :])
                ins.then_inc(full, 1)

            def rows_out(src, w, dst, full, kc, ready, target, s, step):
                for i in range(2):
                    e.wait_ge(ready, target + i + 1)
                    for t in (2 * i, 2 * i + 1):
                        for k in range(kc):
                            ins = mm(dst[:, i, (t % 2) * D:(t % 2 + 1) * D], src[:, k, t * P:(t + 1) * P], w[:, k, :],
                                     k == 0, k == kc - 1)
                            if t % 2 and k == kc - 1:
                                ins.then_inc(full, 1)
                            if i == 0:
                                among(s, step, kc * t + k, 2 * kc)

            def norm_rows(s):
                e.wait_ge(ln_a, s + 1)
                e.wait_ge(s_max, TILES * s)
                e.wait_ge(mrow_ready, NG * s)
                e.wait_ge(gate_ready, s)
                transposes(xn_a, R, xta_full)

            def qk(s, i):
                e.wait_ge(xta_ready, KC * (s + 1))
                e.wait_ge(wqk_ready, s // B + 1)
                if i >= 2:
                    e.wait_ge(qk_evac, 4 * s + i - 1)
                for k in range(KC):
                    ins = mm(R[:, i % 2, :], w_qk[:, k, QK_ORDER[i] * P:(QK_ORDER[i] + 1) * P], xt_a[:, k, :],
                             k == 0, k == KC - 1)
                ins.then_inc(qk_full, 1)

            def values(s, i):
                e.wait_ge(xta_ready, KC * (s + 1))
                e.wait_ge(ld_v, NLD_V * (s // B + 1))
                if i:
                    bank = MI
                    e.wait_ge(on_ready, NG * s)
                    e.wait_ge(mc_ready, 1 if s == 0 else 2)
                else:
                    bank = OA
                    e.wait_ge(cxt_ready, 2)
                    if s:
                        e.wait_ge(cu_ready, NG * s)
                        e.wait_ge(mrow_ready, NG * s + sum(m < AT["vb"][0] for m in ROW_TILE))
                for t in (2 * i, 2 * i + 1):
                    for k in range(KC):
                        ins = mm(bank[:, (t % 2) * D:(t % 2 + 1) * D], xt_a[:, k, t * P:(t + 1) * P], w_v[:, k, :],
                                 k == 0, k == KC - 1)
                        if s:
                            among(s, "va" if i else "vb", 2 * (t % 2) + k, 4)
                ins.then_inc(v_full, 1)

            def scores_rows(s, m0, m1):
                if s is None:
                    return
                if m0 == 0:
                    e.wait_ge(qk_evac, 4 * (s + 1))
                    if s == B + 1:
                        e.wait_ge(ck_ready, 2 * KC)
                for m in range(m0, m1):
                    h, t = m // TN, m % TN
                    if m % (TILES // KC) == 0:
                        e.wait_ge(stack[h // HC], 192 * (s + 1))
                    if m >= 2:
                        e.wait_ge(s_max, TILES * s + m - 1)
                    if m in ROW_TILE:
                        max_row(s, ROW_TILE.index(m))
                    mm(R[:, m % 2, :], qst[0:ROWS, h, t * P:(t + 1) * P], kst[0:ROWS, h, :]).then_inc(s_full, 1)

            def among(s, step, done, total):
                if s is not None:
                    m, n = AT[step][0], TILES_OF[step]
                    scores_rows(s, m + n * done // total, m + n * (done + 1) // total)

            def max_row(s, g):
                if g == NG - 1:
                    bank = R[:, 0, :]
                    e.wait_ge(s_max, TILES * (s + 1))
                else:
                    bank = OA
                    e.wait_ge(v_ready, 2 * (s + 1) if s == 0 or ROW_TILE[g] >= AT["vb"][0] else 2 * s)
                    if g:
                        e.wait_ge(mrow_ready, NG * s + g)
                    if s and ROW_TILE[g] >= AT["g0"][0]:
                        e.wait_ge(cu_ready, NG * s)
                e.wait_ge(nmparts, NG * s + g + 1)
                for t in range(TN):
                    ins = mm(bank[0:3 * G, t * P:(t + 1) * P], mp[:, g, t, :, :].rearrange("p a b -> p (a b)"), identb[:, :])
                ins.then_inc(mrow_full, 1)

            def un_transpose(k, g, ur, ut, free):
                e.wait_ge(ur, k + 1)
                for f, v in free:
                    e.wait_ge(f, v)
                for t in range(TN):
                    ins = e.transpose(MI[:, t * P:(t + 1) * P], u[:, g % 2, t * P:(t + 1) * P], ident[:, :])
                ins.then_inc(ut, 1)

            def attend(s, nxt):
                if s == 0:
                    e.wait_ge(fill_k, 16 * 4)
                def st(g, kc):
                    for i in range(2):
                        m = 32 * s + 2 * (4 * g + kc) + i
                        if m % 32 >= 2:
                            e.wait_ge(exp_done, m - 1)
                        elif m % 32 == 1 and s:
                            e.wait_ge(x3, 2 * s - 1)
                        for j in (2 * i, 2 * i + 1):
                            h = G * g + j
                            ins = mm(A[:, (j + 2) % 4, :], kst[0:ROWS + 3, h, kc * P:(kc + 1) * P], qst[0:ROWS + 3, h, :])
                        ins.then_inc(st_full, 1)

                def av(g, kc):
                    e.wait_ge(exp_done, 32 * s + 2 * (4 * g + kc) + 2)
                    if kc == 0:
                        if g:
                            e.wait_ge(u_ready, NG * s + g)
                        else:
                            e.wait_ge(cu_ready, NG * s)
                            e.wait_ge(mrow_ready, NG * s + NG - 1)
                    for j in range(G):
                        ins = mm(OA[32 * j:32 * j + 32, :], vaug[:, kc, G * g + j, :], big[:, 2 * (kc % 2) + j // 2, j % 2, :],
                                 kc == 0, kc == TN - 1)
                    ins.then_inc(av_done, 1)

                last = None
                for g in range(NG):
                    for kc in range(TN):
                        if kc == 0:
                            e.wait_ge(mrd[g], 16 * (s + 1))
                        st(g, kc)
                        n = TN * g + kc
                        if n == 1:
                            max_row(s, NG - 1)
                            gates(s)
                        if s == B and n == 12:
                            cross_values(1, R)
                        if s == B and n == 13:
                            cross_keys(1, R)
                        if nxt is not None and n == QK_AT[0] - 2:
                            norm_rows(nxt)
                        if nxt is not None and n in QK_AT:
                            qk(nxt, QK_AT.index(n))
                        if last:
                            av(*last)
                        if kc == 2 and g:
                            un_transpose(NG * s + g - 1, g - 1, u_ready, ut_full,
                                         [(on_ready, NG * s + g - 1)] if g > 1 else [(x3, 2 * s), (mc_ready, 2)])
                        if n >= 13:
                            scores_rows(nxt, *AT[f"unit{n}"])
                        last = (g, kc)
                av(*last)
                scores_rows(nxt, *AT["av"])
                un_transpose(NG * s + NG - 1, NG - 1, u_ready, ut_full, [(on_ready, NG * s + NG - 1)])

            def post_self(s, nxt):
                scores_rows(nxt, *AT["ot"])
                e.wait_ge(on_ready, NG * (s + 1))
                e.wait_ge(exp_done, 32 * (s + 1))
                for i in range(2):
                    transpose_half(xn_b, i, ot_full)
                scores_rows(nxt, *AT["proj"])
                e.wait_ge(wpg_ready, s + 1)
                rows_out(xt_b, w_pg, A[:, 2:4, :], pj_full, KC, ot_ready, 2 * s, nxt, "pa")
                if nxt is not None:
                    values(nxt, 1)

            def cross(s, nxt):
                b = s % B
                scores_rows(nxt, *AT["norm2"])
                e.wait_ge(ln_b, 4 * s + 1)
                transpose_half(xn_b, 0, xtb_full)
                scores_rows(nxt, *AT["halfq"])
                for i in range(2):
                    e.wait_ge(xtb_ready, 2 * s + i + 1)
                    e.wait_ge(x1, 2 * (s + 1))
                    h = slice(i * N // 2, (i + 1) * N // 2)
                    for c in range(KC):
                        if i == 0 and c == 1:
                            e.wait_ge(ln_b, 4 * s + 2)
                            transpose_half(xn_b, 1, xtb_full)
                        for k in range(KC):
                            ins = mm(A[:, 2 + c, h], w_q[:, k, c * P:(c + 1) * P], xt_b[:, k, h], k == 0, k == KC - 1)
                            if i and k == KC - 1:
                                ins.then_inc(cq_full, 1)
                            among(nxt, "cqb" if i else "cqa", KC * c + k, 2 * KC)
                scores_rows(nxt, AT["q0"][0], AT["stack"][1])
                e.wait_ge(cq_evac, KC * (s + 1))
                e.wait_ge(ckstack, 192 * (s // B + 1))
                e.wait_ge(mask_ready, 1 + s // B)

                def rows(t, c):
                    for h in range(HC * c, HC * (c + 1)):
                        ins = mm(A[:, 2 * (t % 2) + c, (h % HC) * S:(h % HC + 1) * S],
                                 cqst[0:ROWS + 1, h, t * P:(t + 1) * P], ckst[0:ROWS + 1, h, b * S:(b + 1) * S])
                    return ins

                for c in range(KC):
                    e.wait_ge(cstack[c], 96 * (s + 1))
                    for t in range(2):
                        ins = rows(t, c)
                        if c:
                            ins.then_inc(cs_full, 1)
                    if c == 0:
                        scores_rows(nxt, *AT["half"])
                scores_rows(nxt, *AT["cross2"])
                for t in range(2, TN):
                    e.wait_ge(cs_max, TN * s + t - 1)
                    for c in range(KC):
                        ins = rows(t, c)
                    ins.then_inc(cs_full, 1)
                scores_rows(nxt, *AT["cmrow"])
                e.wait_ge(cnmparts, s + 1)
                if nxt is not None:
                    e.wait_ge(v_ready, 2 * nxt + 1)
                e.wait_ge(on_ready, NG * (s + 1))
                for t in range(TN):
                    ins = mm(MI[0:3 * H, t * P:(t + 1) * P], cmp_[:, t, :, :].rearrange("p a b -> p (a b)"), identb[:, :])
                ins.then_inc(cmrow_full, 1)
                scores_rows(nxt, *AT["crows"])
                e.wait_ge(cmrd, 16 * (s + 1))
                e.wait_ge(cs_max, TN * (s + 1))

                def st(g):
                    if g >= 2:
                        e.wait_ge(cexp_done, NG * s + g - 1)
                    for j in range(G):
                        o = S * (j % 2)
                        ins = mm(A[o:o + S, 2 * (g % 2) + j // 2, :], ckst[:, G * g + j, b * S:(b + 1) * S], cqst[:, G * g + j, :])
                    ins.then_inc(cst_full, 1)

                def av(g):
                    e.wait_ge(cexp_done, NG * s + g + 1)
                    if g:
                        e.wait_ge(cu_ready, NG * s + g)
                    else:
                        e.wait_ge(u_ready, NG * (s + 1))
                        if nxt is not None:
                            e.wait_ge(mrow_ready, NG * nxt + sum(m < AT["g0"][0] for m in ROW_TILE))
                    for i in range(2):
                        ins = mm(OA[S * i:S * (i + 1), :], cv[:, b, 2 * g + i, :], big[:, g, i, :])
                    ins.then_inc(cav_done, 1)

                st(0)
                for g in range(NG):
                    if g + 1 < NG:
                        st(g + 1)
                    av(g)
                    scores_rows(nxt, *AT[f"g{g}"])
                    un_transpose(NG * s + g, g, cu_ready, cut_full,
                                 [(con_ready, NG * s + g)] if g else [(cmrow_ready, s + 1)])
                scores_rows(nxt, *AT["cot"])
                e.wait_ge(con_ready, NG * (s + 1))
                e.wait_ge(cexp_done, NG * (s + 1))
                for i in range(2):
                    transpose_half(xn_b, i, cot_full)
                rows_out(xt_b, w_c, A[:, 2:4, :], cpj_full, KC, cot_ready, 2 * s, nxt, "ca")
                scores_rows(nxt, *AT["norm3"])
                if nxt is not None:
                    values(nxt, 0)

            def mlp(s, nxt):
                e.wait_ge(ln_b, 4 * s + 3)
                transpose_half(xn_b, 0, xtc_full)
                scores_rows(nxt, *AT["halfm"])
                for i in range(2):
                    e.wait_ge(xtc_ready, 2 * s + i + 1)
                    e.wait_ge(x2, 2 * (s + 1))
                    h = slice(i * N // 2, (i + 1) * N // 2)
                    for m in range(3):
                        if i == 0 and m == 2:
                            e.wait_ge(ln_b, 4 * s + 4)
                            transpose_half(xn_b, 1, xtc_full)
                        for k in range(KC):
                            ins = mm(A[:, (m + 2) % 4, h], w_1[:, k, m * P:(m + 1) * P], xt_b[:, k, h],
                                     k == 0, k == KC - 1)
                            if i and k == KC - 1:
                                ins.then_inc(h_full, 1)
                            among(nxt, "hb" if i else "ha", KC * m + k, 3 * KC)
                for m in range(3, MC):
                    if m > 3:
                        e.wait_ge(h_ready, MC * s + m - 3)
                    for k in range(KC):
                        ins = mm(A[:, (m + 2) % 4, :], w_1[:, k, m * P:(m + 1) * P], xt_b[:, k, :], k == 0, k == KC - 1)
                        if k == KC - 1:
                            ins.then_inc(h_full, 1)
                        among(nxt, f"h{m}", k, KC)
                e.wait_ge(con_ready, NG * (s + 1))
                if nxt is not None:
                    e.wait_ge(v_ready, 2 * nxt + 1)
                for t in range(TN):
                    bank = A[:, 0, :] if t < 2 else MI
                    for k in range(MC):
                        if t == 0:
                            if k == 0:
                                e.wait_ge(h_ready, MC * s + MC - 1)
                            elif k == MC - 1:
                                e.wait_ge(h_ready, MC * s + k + 1)
                        ins = mm(bank[:, (t % 2) * D:(t % 2 + 1) * D], hid[:, k, t * P:(t + 1) * P], w_2[:, k, :],
                                 k == 0, k == MC - 1)
                        if t % 2 and k == MC - 1:
                            ins.then_inc(mo_full, 1)
                        among(nxt, f"o{t}", k, MC)

            condition()
            modulation(0)
            modulation_columns(0)
            norm_rows(0)
            for i in range(4):
                qk(0, i)
            context()
            values(0, 1)
            values(0, 0)
            cross_values(0, A[:, 0:2, :])
            cross_keys(0, A[:, 2:4, :])
            scores_rows(0, 0, START[0])
            modulation(1)
            scores_rows(0, START[0], START[1])
            modulation_columns(1)
            scores_rows(0, START[1], TILES)
            for s in range(2 * B):
                nxt = s + 1 if s < 2 * B - 1 else None
                attend(s, nxt)
                post_self(s, nxt)
                cross(s, nxt)
                mlp(s, nxt)


_INS = ["x", "cond_1024", "ctx_1024", "mask_BxS2_bf0"] + [n for layer in LAYER for n in layer.values()]


def kernel(**inputs):
    import numpy as _np
    import concourse.bacc as _bacc
    from concourse import mybir as _mybir
    from concourse.bass_utils import run_bass_kernel_spmd as _run

    nc = _bacc.Bacc("TRN2", target_bir_lowering=False, num_devices=1)
    arrays, args = {}, {}
    for name in _INS:
        v = _np.ascontiguousarray(inputs[name])
        arrays[f"in_{name}_dram"] = v
        args[name] = nc.dram_tensor(f"in_{name}_dram", v.shape, _mybir.dt.from_np(v.dtype), kind="ExternalInput").ap()
    o = nc.dram_tensor("out_0_dram", (B, N, D), _mybir.dt.float32, kind="ExternalOutput").ap()
    build(nc, args, o)
    r = _run(nc, [arrays], core_ids=[0])
    return r.results[0]["out_0_dram"]
```
